# Optimizing a Trainium2 kernel written in Bass

```python
import numpy as np
import jax
import jax.numpy as jnp

def _softmax(x, axis=-1):
    return jax.nn.softmax(x, axis=axis)
def _gelu(x):
    return jax.nn.gelu(x, approximate=True)
def _silu(x):
    return jax.nn.silu(x)
def _sigmoid(x):
    return jax.nn.sigmoid(x)
def _layernorm(x, axis=-1, eps=1e-5):
    m = jnp.mean(x, axis=axis, keepdims=True)
    v = jnp.var(x, axis=axis, keepdims=True)
    return (x - m) / jnp.sqrt(v + eps)
def _scatter_add(tgt, idx, src, axis=0):
    return tgt.at[idx].add(src)
def _segment_sum(src, seg, n):
    return jax.ops.segment_sum(src, seg, n)

kernel_name = 'mk_conv_seq_d4_conv_nhwc128_387dfa'

def setup_inputs(seed: int = 0):
    np.random.seed(seed)
    _w = jnp.asarray
    def _rec_inputs():
        import jax
        import jax.numpy as jnp
        _gk = jax.random.key(seed)
        x = -0.0005207 + 1.001 * jax.random.normal(jax.random.fold_in(_gk, 1), (4, 64, 64, 128), jnp.float32)
        return x
    x = _rec_inputs()
    def _L0_conv_setup():
        import jax, jax.numpy as jnp
        import numpy as np
        B, H, W, C, K = (4, 64, 64, 128, 8)
        CK = C // K
        key = jax.random.key(seed)
        k1, k2, k3, k4, k5 = jax.random.split(key, 5)
        x = jax.random.normal(k1, (B, H, W, C), dtype=jnp.float32)
        kernel_f = jax.random.normal(k2, (1, 1, C, CK), dtype=jnp.float32) * (1.0 / np.sqrt(C))
        kernel_g = jax.random.normal(k3, (1, 1, C, CK), dtype=jnp.float32) * (1.0 / np.sqrt(C))
        kernel_h = jax.random.normal(k4, (1, 1, C, C), dtype=jnp.float32) * (1.0 / np.sqrt(C))
        gamma = jax.random.uniform(k5, (1,), dtype=jnp.float32)
        return {'x': x, 'kernel_f': kernel_f, 'kernel_g': kernel_g, 'kernel_h': kernel_h, 'gamma': gamma}
    _L0_conv_all = _L0_conv_setup()
    _L0_conv_in = {k: v for k, v in _L0_conv_all.items() if k in ('kernel_f', 'kernel_g', 'kernel_h', 'gamma', )}
    del _L0_conv_all

    def _L1_conv_setup():
        import jax, jax.numpy as jnp
        import numpy as np
        R = 2
        key = jax.random.key(seed)
        k1, k2 = jax.random.split(key)
        x = jax.random.normal(k1, (4, 32, 128, 128), dtype=jnp.float32)
        gamma = jax.random.normal(k2, (1,), dtype=jnp.float32)
        return {'x': x, 'gamma': gamma}
    _L1_conv_all = _L1_conv_setup()
    _L1_conv_in = {k: v for k, v in _L1_conv_all.items() if k in ('gamma', )}
    del _L1_conv_all

    def _L2_conv_setup():
        import jax, jax.numpy as jnp
        import numpy as np
        DIM = 128
        HEADS = 4
        K = 7
        MLP_RATIO = 4
        EPS = 1e-05

        def _ln(x, g, b):
            m = jnp.mean(x, axis=-1, keepdims=True)
            v = jnp.mean(jnp.square(x - m), axis=-1, keepdims=True)
            return (x - m) * jax.lax.rsqrt(v + EPS) * g + b

        def _neigh_idx(L, k):
            i = jnp.arange(L)
            start = jnp.clip(i - k // 2, 0, L - k)
            idx = start[:, None] + jnp.arange(k)[None, :]
            rel = idx - i[:, None] + (k - 1)
            return (idx, rel)

        def _neighborhood_attention(x, qkv_w, qkv_b, rpb, proj_w, proj_b):
            B, H, W, C = x.shape
            nh, hd = (HEADS, C // HEADS)
            scale = hd ** (-0.5)
            qkv = (x @ qkv_w + qkv_b).reshape(B, H, W, 3, nh, hd)
            qkv = qkv.transpose(3, 0, 4, 1, 2, 5)
            q, k_, v = (qkv[0] * scale, qkv[1], qkv[2])
            ih, rh = _neigh_idx(H, K)
            iw, rw = _neigh_idx(W, K)
            kg = k_[:, :, ih][:, :, :, :, iw]
            vg = v[:, :, ih][:, :, :, :, iw]
            attn = jnp.einsum('bnywc,bnykxjc->bnyxkj', q, kg)
            bias = rpb[:, rh][:, :, :, rw]
            attn = attn + bias.transpose(0, 1, 3, 2, 4)[None]
            a = jax.nn.softmax(attn.reshape(B, nh, H, W, K * K), axis=-1)
            a = a.reshape(B, nh, H, W, K, K)
            out = jnp.einsum('bnyxkj,bnykxjc->bnyxc', a, vg)
            out = out.transpose(0, 2, 3, 1, 4).reshape(B, H, W, C)
            return out @ proj_w + proj_b
        key = jax.random.key(seed)
        ks = jax.random.split(key, 8)
        B, H, W, C = (4, 64, 64, DIM)
        hid = C * MLP_RATIO
        s = lambda k, shape: jax.random.normal(k, shape, jnp.float32) * 0.02
        return {'x': jax.random.normal(ks[0], (B, H, W, C), jnp.float32), 'ln1_g': jnp.ones((C,), jnp.float32), 'ln1_b': jnp.zeros((C,), jnp.float32), 'qkv_w': s(ks[1], (C, 3 * C)), 'qkv_b': jnp.zeros((3 * C,), jnp.float32), 'rpb': s(ks[2], (HEADS, 2 * K - 1, 2 * K - 1)), 'proj_w': s(ks[3], (C, C)), 'proj_b': jnp.zeros((C,), jnp.float32), 'ln2_g': jnp.ones((C,), jnp.float32), 'ln2_b': jnp.zeros((C,), jnp.float32), 'fc1_w': s(ks[4], (C, hid)), 'fc1_b': jnp.zeros((hid,), jnp.float32), 'fc2_w': s(ks[5], (hid, C)), 'fc2_b': jnp.zeros((C,), jnp.float32)}
    _L2_conv_all = _L2_conv_setup()
    _L2_conv_in = {k: v for k, v in _L2_conv_all.items() if k in ('ln1_g', 'ln1_b', 'qkv_w', 'qkv_b', 'rpb', 'proj_w', 'proj_b', 'ln2_g', 'ln2_b', 'fc1_w', 'fc1_b', 'fc2_w', 'fc2_b', )}
    del _L2_conv_all

    def _L3_conv_setup():
        import jax, jax.numpy as jnp
        import numpy as np
        NUM_HEAD = 8

        def conv_same(x, w, b):
            return jax.lax.conv_general_dilated(x, w, window_strides=(1, 1), padding='SAME', dimension_numbers=('NHWC', 'HWIO', 'NHWC')) + b

        def _gated_resnet(x, W1, b1, W2, b2, Wq, bq, Wk, bk, Wv, bv, W3, b3):
            B, H, W, C = x.shape
            c1 = conv_same(jax.nn.elu(x), W1, b1)
            c2 = conv_same(c1, W2, b2)
            a, b = jnp.split(c2, 2, axis=-1)
            c3 = a * jax.nn.sigmoid(b)
            N = H * W
            f = c3.reshape(B, N, C)
            q = f @ Wq + bq
            k = f @ Wk + bk
            v = f @ Wv + bv
            scale = jnp.float32(np.sqrt(C // 8))
            dot = jnp.einsum('bnd,bmd->bnm', q, k) / scale
            mask = jnp.tril(jnp.ones((N, N), jnp.float32), -1)
            dot = dot - (1.0 - mask) * 10000000000.0
            dot = dot - jnp.max(dot, axis=-1, keepdims=True)
            e = jnp.exp(dot) * mask
            probs = e / (jnp.sum(e, axis=-1, keepdims=True) + 1e-10)
            atten = jnp.einsum('bnm,bmd->bnd', probs, v)
            multihead = jnp.tile(atten, (1, 1, NUM_HEAD)).reshape(B, H, W, -1)
            mh = multihead @ W3 + b3
            c3 = c3 + mh.reshape(B, H, W, C)
            return x + c3
        key = jax.random.key(seed)
        ks = jax.random.split(key, 8)
        B, H, W, C = (4, 64, 64, 128)
        DQK, DV = (4, 16)
        s = 0.02
        return {'x': jax.random.normal(ks[0], (B, H, W, C), dtype=jnp.float32), 'W1': jax.random.normal(ks[1], (3, 3, C, C), dtype=jnp.float32) * s, 'b1': jnp.zeros((C,), jnp.float32), 'W2': jax.random.normal(ks[2], (3, 3, C, 2 * C), dtype=jnp.float32) * s, 'b2': jnp.zeros((2 * C,), jnp.float32), 'Wq': jax.random.normal(ks[3], (C, DQK), dtype=jnp.float32) * s, 'bq': jnp.zeros((DQK,), jnp.float32), 'Wk': jax.random.normal(ks[4], (C, DQK), dtype=jnp.float32) * s, 'bk': jnp.zeros((DQK,), jnp.float32), 'Wv': jax.random.normal(ks[5], (C, DV), dtype=jnp.float32) * s, 'bv': jnp.zeros((DV,), jnp.float32), 'W3': jax.random.normal(ks[6], (NUM_HEAD * DV, C), dtype=jnp.float32) * s, 'b3': jnp.zeros((C,), jnp.float32)}
    _L3_conv_all = _L3_conv_setup()
    _L3_conv_in = {k: v for k, v in _L3_conv_all.items() if k in ('W1', 'b1', 'W2', 'b2', 'Wq', 'bq', 'Wk', 'bk', 'Wv', 'bv', 'W3', 'b3', )}
    del _L3_conv_all

    return {
        "x": x,
        "L0_conv_kernel_f": _L0_conv_in["kernel_f"],
        "L0_conv_kernel_g": _L0_conv_in["kernel_g"],
        "L0_conv_kernel_h": _L0_conv_in["kernel_h"],
        "L0_conv_gamma": _L0_conv_in["gamma"],
        "L1_conv_gamma": _L1_conv_in["gamma"],
        "L2_conv_ln1_g": _L2_conv_in["ln1_g"],
        "L2_conv_ln1_b": _L2_conv_in["ln1_b"],
        "L2_conv_qkv_w": _L2_conv_in["qkv_w"],
        "L2_conv_qkv_b": _L2_conv_in["qkv_b"],
        "L2_conv_rpb": _L2_conv_in["rpb"],
        "L2_conv_proj_w": _L2_conv_in["proj_w"],
        "L2_conv_proj_b": _L2_conv_in["proj_b"],
        "L2_conv_ln2_g": _L2_conv_in["ln2_g"],
        "L2_conv_ln2_b": _L2_conv_in["ln2_b"],
        "L2_conv_fc1_w": _L2_conv_in["fc1_w"],
        "L2_conv_fc1_b": _L2_conv_in["fc1_b"],
        "L2_conv_fc2_w": _L2_conv_in["fc2_w"],
        "L2_conv_fc2_b": _L2_conv_in["fc2_b"],
        "L3_conv_W1": _L3_conv_in["W1"],
        "L3_conv_b1": _L3_conv_in["b1"],
        "L3_conv_W2": _L3_conv_in["W2"],
        "L3_conv_b2": _L3_conv_in["b2"],
        "L3_conv_Wq": _L3_conv_in["Wq"],
        "L3_conv_bq": _L3_conv_in["bq"],
        "L3_conv_Wk": _L3_conv_in["Wk"],
        "L3_conv_bk": _L3_conv_in["bk"],
        "L3_conv_Wv": _L3_conv_in["Wv"],
        "L3_conv_bv": _L3_conv_in["bv"],
        "L3_conv_W3": _L3_conv_in["W3"],
        "L3_conv_b3": _L3_conv_in["b3"],
    }

def reference(x, L0_conv_kernel_f, L0_conv_kernel_g, L0_conv_kernel_h, L0_conv_gamma, L1_conv_gamma, L2_conv_ln1_g, L2_conv_ln1_b, L2_conv_qkv_w, L2_conv_qkv_b, L2_conv_rpb, L2_conv_proj_w, L2_conv_proj_b, L2_conv_ln2_g, L2_conv_ln2_b, L2_conv_fc1_w, L2_conv_fc1_b, L2_conv_fc2_w, L2_conv_fc2_b, L3_conv_W1, L3_conv_b1, L3_conv_W2, L3_conv_b2, L3_conv_Wq, L3_conv_bq, L3_conv_Wk, L3_conv_bk, L3_conv_Wv, L3_conv_bv, L3_conv_W3, L3_conv_b3):
    import jax
    import jax.numpy as jnp
    def _L0_conv_ref(x, kernel_f, kernel_g, kernel_h, gamma):
        import jax, jax.numpy as jnp
        import numpy as np
        B, H, W, C, K = (4, 64, 64, 128, 8)
        CK = C // K
        b, h, w, c = x.shape
        n = h * w
        xf = x.reshape(b, n, c)
        f = jnp.einsum('bnc,cd->bnd', xf, kernel_f[0, 0])
        g = jnp.einsum('bnc,cd->bnd', xf, kernel_g[0, 0])
        hh = jnp.einsum('bnc,cd->bnd', xf, kernel_h[0, 0])
        s = jnp.einsum('bnd,bmd->bnm', g, f)
        beta = jax.nn.softmax(s, axis=1)
        v = jnp.einsum('bnm,bmc->bnc', beta, hh)
        v = v.reshape(b, h, w, c)
        return gamma * v + x

    def _L1_conv_ref(x, gamma):
        import jax, jax.numpy as jnp
        import numpy as np
        R = 2
        B, C, H, W = x.shape
        h, w = (H // R, W // R)
        xs = x.reshape(B, C, h, R, w, R).transpose(0, 1, 3, 5, 2, 4).reshape(B, C * R * R, h, w)
        hw = h * w
        q = xs.reshape(B, C * R * R, hw)
        energy = jnp.einsum('bci,bcj->bij', q, q)
        d = jnp.sqrt(jnp.diagonal(energy, axis1=1, axis2=2))
        energy = energy / (d[:, :, None] * d[:, None, :])
        attn = jax.nn.softmax(energy, axis=-1)
        out = jnp.einsum('bcj,bij->bci', q, attn).reshape(B, C * R * R, h, w)
        out = gamma * out + xs
        out = out.reshape(B, C, R, R, h, w).transpose(0, 1, 4, 2, 5, 3).reshape(B, C, H, W)
        return out

    def _L2_conv_ref(x, ln1_g, ln1_b, qkv_w, qkv_b, rpb, proj_w, proj_b, ln2_g, ln2_b, fc1_w, fc1_b, fc2_w, fc2_b):
        import jax, jax.numpy as jnp
        import numpy as np
        DIM = 128
        HEADS = 4
        K = 7
        MLP_RATIO = 4
        EPS = 1e-05

        def _ln(x, g, b):
            m = jnp.mean(x, axis=-1, keepdims=True)
            v = jnp.mean(jnp.square(x - m), axis=-1, keepdims=True)
            return (x - m) * jax.lax.rsqrt(v + EPS) * g + b

        def _neigh_idx(L, k):
            i = jnp.arange(L)
            start = jnp.clip(i - k // 2, 0, L - k)
            idx = start[:, None] + jnp.arange(k)[None, :]
            rel = idx - i[:, None] + (k - 1)
            return (idx, rel)

        def _neighborhood_attention(x, qkv_w, qkv_b, rpb, proj_w, proj_b):
            B, H, W, C = x.shape
            nh, hd = (HEADS, C // HEADS)
            scale = hd ** (-0.5)
            qkv = (x @ qkv_w + qkv_b).reshape(B, H, W, 3, nh, hd)
            qkv = qkv.transpose(3, 0, 4, 1, 2, 5)
            q, k_, v = (qkv[0] * scale, qkv[1], qkv[2])
            ih, rh = _neigh_idx(H, K)
            iw, rw = _neigh_idx(W, K)
            kg = k_[:, :, ih][:, :, :, :, iw]
            vg = v[:, :, ih][:, :, :, :, iw]
            attn = jnp.einsum('bnywc,bnykxjc->bnyxkj', q, kg)
            bias = rpb[:, rh][:, :, :, rw]
            attn = attn + bias.transpose(0, 1, 3, 2, 4)[None]
            a = jax.nn.softmax(attn.reshape(B, nh, H, W, K * K), axis=-1)
            a = a.reshape(B, nh, H, W, K, K)
            out = jnp.einsum('bnyxkj,bnykxjc->bnyxc', a, vg)
            out = out.transpose(0, 2, 3, 1, 4).reshape(B, H, W, C)
            return out @ proj_w + proj_b
        h = x + _neighborhood_attention(_ln(x, ln1_g, ln1_b), qkv_w, qkv_b, rpb, proj_w, proj_b)
        y = _ln(h, ln2_g, ln2_b)
        y = jax.nn.gelu(y @ fc1_w + fc1_b, approximate=False) @ fc2_w + fc2_b
        return h + y

    def _L3_conv_ref(x, W1, b1, W2, b2, Wq, bq, Wk, bk, Wv, bv, W3, b3):
        import jax, jax.numpy as jnp
        import numpy as np
        NUM_HEAD = 8

        def conv_same(x, w, b):
            return jax.lax.conv_general_dilated(x, w, window_strides=(1, 1), padding='SAME', dimension_numbers=('NHWC', 'HWIO', 'NHWC')) + b

        def _gated_resnet(x, W1, b1, W2, b2, Wq, bq, Wk, bk, Wv, bv, W3, b3):
            B, H, W, C = x.shape
            c1 = conv_same(jax.nn.elu(x), W1, b1)
            c2 = conv_same(c1, W2, b2)
            a, b = jnp.split(c2, 2, axis=-1)
            c3 = a * jax.nn.sigmoid(b)
            N = H * W
            f = c3.reshape(B, N, C)
            q = f @ Wq + bq
            k = f @ Wk + bk
            v = f @ Wv + bv
            scale = jnp.float32(np.sqrt(C // 8))
            dot = jnp.einsum('bnd,bmd->bnm', q, k) / scale
            mask = jnp.tril(jnp.ones((N, N), jnp.float32), -1)
            dot = dot - (1.0 - mask) * 10000000000.0
            dot = dot - jnp.max(dot, axis=-1, keepdims=True)
            e = jnp.exp(dot) * mask
            probs = e / (jnp.sum(e, axis=-1, keepdims=True) + 1e-10)
            atten = jnp.einsum('bnm,bmd->bnd', probs, v)
            multihead = jnp.tile(atten, (1, 1, NUM_HEAD)).reshape(B, H, W, -1)
            mh = multihead @ W3 + b3
            c3 = c3 + mh.reshape(B, H, W, C)
            return x + c3
        return _gated_resnet(x, W1, b1, W2, b2, Wq, bq, Wk, bk, Wv, bv, W3, b3)

    def _gn(v, G=32, eps=1e-5):
        B_, H_, W_, C_ = v.shape
        g = v.reshape(B_, H_, W_, G, C_ // G)
        m = jnp.mean(g, axis=(1, 2, 4), keepdims=True)
        s = jnp.var(g, axis=(1, 2, 4), keepdims=True)
        return ((g - m) / jnp.sqrt(s + eps)).reshape(v.shape)

    def _ln_c(v, eps=1e-6):
        m = jnp.mean(v, axis=-1, keepdims=True)
        s = jnp.var(v, axis=-1, keepdims=True)
        return (v - m) / jnp.sqrt(s + eps)

    def _ln_t(v, eps=1e-5):
        m = jnp.mean(v, axis=-1, keepdims=True)
        s = jnp.var(v, axis=-1, keepdims=True)
        return (v - m) / jnp.sqrt(s + eps)

    def _to_tokens(v):
        B_, H_, W_, C_ = v.shape
        return v.reshape(B_, H_ * W_, C_)
    def _from_tokens(t, like):
        return t.reshape(like.shape)

    x = _L0_conv_ref(x, L0_conv_kernel_f, L0_conv_kernel_g, L0_conv_kernel_h, L0_conv_gamma)
    x = _L1_conv_ref(x, L1_conv_gamma)
    x = _L2_conv_ref(x, L2_conv_ln1_g, L2_conv_ln1_b, L2_conv_qkv_w, L2_conv_qkv_b, L2_conv_rpb, L2_conv_proj_w, L2_conv_proj_b, L2_conv_ln2_g, L2_conv_ln2_b, L2_conv_fc1_w, L2_conv_fc1_b, L2_conv_fc2_w, L2_conv_fc2_b)
    x = _L3_conv_ref(x, L3_conv_W1, L3_conv_b1, L3_conv_W2, L3_conv_b2, L3_conv_Wq, L3_conv_bq, L3_conv_Wk, L3_conv_bk, L3_conv_Wv, L3_conv_bv, L3_conv_W3, L3_conv_b3)
    return x


_drawn_inputs = setup_inputs


def setup_inputs(seed=0):
    import zlib

    import numpy as np

    out = dict(_drawn_inputs(seed))
    spreads = {'L2_conv_ln1_g': (1.0, 0.6),
     'L2_conv_ln1_b': (0.0, 0.8),
     'L2_conv_qkv_b': (0.0, 0.1),
     'L2_conv_proj_b': (0.0, 0.1),
     'L2_conv_ln2_g': (1.0, 0.6),
     'L2_conv_ln2_b': (0.0, 0.8),
     'L2_conv_fc1_b': (0.0, 0.343),
     'L2_conv_fc2_b': (0.0, 0.1),
     'L3_conv_b1': (0.0, 0.1),
     'L3_conv_b2': (0.0, 0.1),
     'L3_conv_bq': (0.0, 2.0),
     'L3_conv_bk': (0.0, 2.0),
     'L3_conv_bv': (0.0, 0.286),
     'L3_conv_b3': (0.0, 0.1)}
    factors = {'L2_conv_qkv_w': 2.92,
     'L2_conv_rpb': 64.0,
     'L3_conv_Wq': 64.0,
     'L3_conv_Wk': 64.0,
     'L3_conv_Wv': 8.0}
    for name, (base, spread) in spreads.items():
        noise = np.random.default_rng([zlib.crc32(name.encode()), seed]).standard_normal(out[name].shape)
        drawn = base * np.exp(spread * noise) if base else spread * noise
        out[name] = jnp.asarray(drawn.astype(out[name].dtype))
    for name, factor in factors.items():
        out[name] = (out[name] * factor).astype(out[name].dtype)
    return out
```

```python
from contextlib import ExitStack

import numpy as np
import concourse.bass as bass
from concourse import mybir

F32 = mybir.dt.float32
F32R = mybir.dt.float32r
BF16 = mybir.dt.bfloat16
ACT = mybir.ActivationFunctionType
ALU = mybir.AluOpType
AX = mybir.AxisListType

P = 128
B = 4
HW = 64
C = 128
N = HW * HW
TILES = N // P
CHUNK = 512
CHUNKS = N // CHUNK


class Memory:

    def __init__(self, nc, ctx, stage):
        self.nc, self.ctx, self.stage = nc, ctx, stage

    def sb(self, name, shape, dt=F32):
        return self.ctx.enter_context(self.nc.sbuf_tensor(f"{self.stage}_{name}", shape, dt))

    def ps(self, name, shape, dt=F32):
        return self.ctx.enter_context(self.nc.psum_tensor(f"{self.stage}_{name}", shape, dt))

    def sem(self, name):
        return self.ctx.enter_context(self.nc.semaphore(f"{self.stage}_{name}"))


def split_product(pe, out, left, right, start, stop):
    pe.matmul(out, left[1], right[0], start=start, stop=False)
    pe.matmul(out, left[0], right[1], start=False, stop=False)
    return pe.matmul(out, left[0], right[0], start=False, stop=stop)


LEFT_PARTS = [0, 0, 1, 1, 0, 2, 1, 2]
RIGHT_PARTS = [0, 1, 0, 1, 2, 0, 2, 1]
PART_ROW = [0, 64, 96]


def column_softmax_attention(nc, x, y, w_fg, w_h, gamma, ident_in):
    D = 16
    RING = 6
    GROUP = 2
    LEAD = 2
    QUARTER = 1024
    QUARTERS = N // QUARTER
    PAIRS = TILES // GROUP
    with ExitStack() as ctx:
        mem = Memory(nc, ctx, "l0")
        x_tok = mem.sb("x_tok", [P, TILES, C])
        x_ch = mem.sb("x_ch", [P, N])
        h_tok = mem.sb("h_tok", [P, TILES, C])
        out_tok = mem.sb("out_tok", [P, TILES, C])
        fg = out_tok[:, :, :].rearrange("p t c -> p (t c)")
        value = x_ch
        f_stack = mem.sb("f_stack", [P, N], BF16)
        g_stack = mem.sb("g_stack", [P, N], BF16)
        exps = mem.sb("exps", [P, RING, N])
        fg_rest = exps[:, RING - 1, :]
        parts = exps[:, RING - 2, 0:N // 2].bitcast(BF16)
        h_scaled = mem.sb("h_scaled", [P, RING, C])
        quarter_max = mem.sb("quarter_max", [P, RING, QUARTERS])
        neg_max = mem.sb("neg_max", [P, RING])
        total = mem.sb("total", [P, RING])
        inverse = mem.sb("inverse", [P, RING])
        fg_w = mem.sb("fg_w", [P, P])
        h_w = mem.sb("h_w", [P, C])
        gamma_col = mem.sb("gamma_col", [P, 1])
        ident = mem.sb("ident", [P, P])
        score_ps = [mem.ps(f"score{i}", [P, QUARTER]) for i in range(2)]
        value_ps = [mem.ps(f"value{i}", [P, CHUNK]) for i in range(2)]
        work_ps = [mem.ps(f"work{i}", [P, CHUNK]) for i in range(2)]

        const_in = mem.sem("const_in")
        x_in = mem.sem("x_in")
        x_stored = mem.sem("x_stored")
        turned = mem.sem("turned")
        x_copied = mem.sem("x_copied")
        fg_made = mem.sem("fg_made")
        fg_copied = mem.sem("fg_copied")
        split_step = mem.sem("split_step")
        stacked = mem.sem("stacked")
        h_made = mem.sem("h_made")
        h_copied = mem.sem("h_copied")
        scored = mem.sem("scored")
        score_copied = mem.sem("score_copied")
        max_ready = mem.sem("max_ready")
        neg_ready = mem.sem("neg_ready")
        exp_ready = mem.sem("exp_ready")
        inverse_ready = mem.sem("inverse_ready")
        h_scaled_ready = mem.sem("h_scaled_ready")
        value_made = mem.sem("value_made")
        value_added = mem.sem("value_added")
        back = mem.sem("back")
        out_ready = mem.sem("out_ready")
        block = ctx.enter_context(nc.Block())

        x_v = x.rearrange("b (t p) c -> b p t c", p=P)
        y_v = y.rearrange("b (t p) c -> b p t c", p=P)

        @block.sync
        def _(sp):
            sp.dma_start(fg_w[:, :], w_fg).then_inc(const_in, 16)
            sp.dma_start(h_w[:, :], w_h).then_inc(const_in, 16)
            sp.dma_start(gamma_col[:, :], gamma).then_inc(const_in, 16)
            sp.dma_start(ident[:, :], ident_in).then_inc(const_in, 16)
            with sp.Fori(0, B) as b:
                for a in range(0, TILES, 8):
                    sp.dma_start(x_tok[:, a:a + 8, :], x_v[bass.ds(b, 1), :, a:a + 8].rearrange("b p t c -> p (b t) c")).then_inc(x_in, 16)
                sp.wait_ge(split_step, b * 5 + 5)
                for r in range(8):
                    left, right = PART_ROW[LEFT_PARTS[r]], PART_ROW[RIGHT_PARTS[r]]
                    sp.dma_start(f_stack[D * r:D * r + D, :], parts[left:left + D, :]).then_inc(stacked, 16)
                    sp.dma_start(g_stack[D * r:D * r + D, :], parts[right + D:right + 2 * D, :]).then_inc(stacked, 16)
                sp.wait_ge(out_ready, b * CHUNKS + CHUNKS)
                for a in range(0, TILES, 8):
                    sp.dma_start(y_v[bass.ds(b, 1), :, a:a + 8].rearrange("b p t c -> p (b t) c"), out_tok[:, a:a + 8, :]).then_inc(x_stored, 16)
            sp.wait_ge(x_stored, 64 * B + 16)

        @block.tensor
        def _(pe):
            pe.wait_ge(const_in, 64)

            def scores(b, t):
                for q in range(QUARTERS):
                    i = t * QUARTERS + q
                    pe.wait_ge(score_copied, b * (TILES * QUARTERS) + i + 1)
                    for half in range(QUARTER // CHUNK):
                        a = q * QUARTER + half * CHUNK
                        mm = pe.matmul(score_ps[i % 2][:, half * CHUNK:(half + 1) * CHUNK],
                                       f_stack[:, t * P:(t + 1) * P], g_stack[:, a:a + CHUNK], start=True, stop=True)
                    mm.then_inc(scored, 1)
                    yield

            def values(b, pair):
                pe.wait_ge(exp_ready, b * TILES + GROUP * (pair + 1))
                pe.wait_ge(h_scaled_ready, b * TILES + GROUP * (pair + 1))
                for c in range(CHUNKS):
                    i = pair * CHUNKS + c
                    pe.wait_ge(value_added, b * (PAIRS * CHUNKS) + i + 1)
                    for k in range(GROUP):
                        slot = (GROUP * pair + k) % RING
                        mm = pe.matmul(value_ps[i % 2][:, :], h_scaled[:, slot, :],
                                       exps[:, slot, c * CHUNK:(c + 1) * CHUNK], start=(k == 0), stop=(k == GROUP - 1))
                    mm.then_inc(value_made, 1)
                    yield

            with pe.Fori(0, B) as b:
                pe.wait_ge(x_in, b * 64 + 64)
                for g in range(CHUNKS):
                    pe.wait_ge(x_copied, b * (4 * CHUNKS) + g + 1)
                    for k in range(4):
                        mm = pe.transpose(work_ps[g % 2][:, k * P:(k + 1) * P], x_tok[:, 4 * g + k, :], ident[:, :])
                    mm.then_inc(turned, 1)
                for c in range(CHUNKS):
                    pe.wait_ge(x_copied, b * (4 * CHUNKS) + CHUNKS + c + 1)
                    pe.wait_ge(x_copied, b * (4 * CHUNKS) + c + 3)
                    pe.matmul(work_ps[c % 2][:, :], fg_w[:, :], x_ch[:, c * CHUNK:(c + 1) * CHUNK],
                              start=True, stop=True).then_inc(turned, 1)
                for g in range(CHUNKS):
                    pe.wait_ge(x_copied, b * (4 * CHUNKS) + 2 * CHUNKS + g + 1)
                    for k in range(4):
                        t = 4 * g + k
                        mm = pe.matmul(work_ps[g % 2][:, k * P:(k + 1) * P], x_ch[:, t * P:(t + 1) * P], h_w[:, :],
                                       start=True, stop=True)
                    mm.then_inc(turned, 1)
                pe.wait_ge(stacked, b * 256 + 272)
                for t in range(LEAD * GROUP):
                    for _ in scores(b, t):
                        pass
                for pair in range(PAIRS):
                    ahead = [s for t in range(GROUP * (pair + LEAD), min(GROUP * (pair + LEAD + 1), TILES)) for s in (t,)]
                    steps = iter(())
                    if ahead:
                        def both():
                            for t in ahead:
                                yield from scores(b, t)
                        steps = both()
                    for _ in values(b, pair):
                        next(steps, None)
                    for _ in steps:
                        pass
                for g in range(CHUNKS):
                    if g == 0:
                        pe.wait_ge(value_added, b * (PAIRS * CHUNKS) + PAIRS * CHUNKS + 2)
                    pe.wait_ge(x_copied, b * (4 * CHUNKS) + 3 * CHUNKS + g + 1)
                    for k in range(4):
                        t = 4 * g + k
                        mm = pe.transpose(work_ps[g % 2][:, k * P:(k + 1) * P], value[:, t * P:(t + 1) * P], ident[:, :])
                    mm.then_inc(turned, 1)

        @block.scalar
        def _(act):
            act.sem_inc(x_copied, 2)
            act.sem_inc(x_stored, 16)
            with act.Fori(0, B) as b:
                for g in range(CHUNKS):
                    act.wait_ge(turned, b * (4 * CHUNKS) + g + 1)
                    act.activation(x_ch[:, g * CHUNK:(g + 1) * CHUNK], work_ps[g % 2][:, :], ACT.Copy).then_inc(x_copied, 1)
                act.wait_ge(x_stored, b * 64 + 16)
                for c in range(CHUNKS):
                    act.wait_ge(turned, b * (4 * CHUNKS) + CHUNKS + c + 1)
                    act.activation(fg[:, c * CHUNK:(c + 1) * CHUNK], work_ps[c % 2][:, :], ACT.Copy).then_inc(x_copied, 1)
                for g in range(CHUNKS):
                    act.wait_ge(turned, b * (4 * CHUNKS) + 2 * CHUNKS + g + 1)
                    act.activation(h_tok[:, 4 * g:4 * g + 4, :].rearrange("p t c -> p (t c)"), work_ps[g % 2][:, :],
                                   ACT.Copy).then_inc(x_copied, 1)
                for t in range(TILES):
                    slot = t % RING
                    act.wait_ge(neg_ready, b * TILES + t + 1)
                    act.activation(exps[:, slot, :], exps[:, slot, :], ACT.Exp, bias=neg_max[:, slot:slot + 1],
                                   accum_out=total[:, slot:slot + 1]).then_inc(exp_ready, 1)

        @block.vector
        def _(dve):
            dve.sem_inc(stacked, 16)
            dve.sem_inc(score_copied, 2)
            dve.sem_inc(value_added, 2)
            dve.wait_ge(const_in, 64)

            def take_quarter(b, t, q):
                i, slot = t * QUARTERS + q, t % RING
                dve.wait_ge(scored, b * (TILES * QUARTERS) + i + 1)
                dve.tensor_scalar(exps[:, slot, q * QUARTER:(q + 1) * QUARTER], score_ps[i % 2][:, :], 1.0, None,
                                  ALU.mult, ALU.max, accum_out=quarter_max[:, slot, q:q + 1]).then_inc(score_copied, 1)
                if q == QUARTERS - 1:
                    dve.wait_ge(score_copied, b * (TILES * QUARTERS) + i + 3)
                    dve.tensor_reduce(neg_max[:, slot:slot + 1], quarter_max[:, slot, :], AX.X, ALU.max,
                                      negate=True).then_inc(neg_ready, 1)

            def scale_h(b, t):
                slot = t % RING
                dve.wait_ge(exp_ready, b * TILES + t + 1)
                dve.reciprocal(inverse[:, slot:slot + 1], total[:, slot:slot + 1]).then_inc(inverse_ready, 1)
                dve.wait_ge(inverse_ready, b * TILES + t + 1)
                dve.tensor_scalar(h_scaled[:, slot, :], h_tok[:, t, :], inverse[:, slot:slot + 1], None,
                                  ALU.mult).then_inc(h_scaled_ready, 1)

            def add_chunk(b, pair, c):
                i = pair * CHUNKS + c
                out = value[:, c * CHUNK:(c + 1) * CHUNK]
                dve.wait_ge(value_made, b * (PAIRS * CHUNKS) + i + 1)
                if pair == 0:
                    dve.tensor_copy(out, value_ps[i % 2][:, :]).then_inc(value_added, 1)
                else:
                    dve.wait_ge(value_added, b * (PAIRS * CHUNKS) + i - CHUNKS + 3)
                    dve.tensor_tensor(out, out, value_ps[i % 2][:, :], ALU.add).then_inc(value_added, 1)

            with dve.Fori(0, B) as b:
                dve.wait_ge(x_copied, b * (4 * CHUNKS) + 2 * CHUNKS + 2)
                dve.wait_ge(stacked, b * 256 + 16)
                dve.tensor_copy(parts[:, :], fg[:, :]).then_inc(split_step, 1)
                dve.wait_ge(split_step, b * 5 + 1)
                dve.tensor_tensor(fg_rest[64:128, :], fg[64:128, :], parts[64:128, :], ALU.subtract).then_inc(split_step, 1)
                dve.wait_ge(split_step, b * 5 + 2)
                dve.tensor_copy(parts[64:128, :], fg_rest[64:128, :]).then_inc(split_step, 1)
                dve.wait_ge(split_step, b * 5 + 3)
                dve.tensor_tensor(fg_rest[96:128, :], fg_rest[96:128, :], parts[96:128, :], ALU.subtract).then_inc(split_step, 1)
                dve.wait_ge(split_step, b * 5 + 4)
                dve.tensor_copy(parts[96:128, :], fg_rest[96:128, :]).then_inc(split_step, 1)
                dve.wait_ge(split_step, b * 5 + 5)
                dve.wait_ge(x_copied, b * (4 * CHUNKS) + 3 * CHUNKS + 2)
                for t in range(LEAD * GROUP):
                    for q in range(QUARTERS):
                        take_quarter(b, t, q)
                for pair in range(PAIRS):
                    for k in range(GROUP):
                        scale_h(b, GROUP * pair + k)
                    for c in range(CHUNKS):
                        t = GROUP * (pair + LEAD) + c // QUARTERS
                        if t < TILES:
                            take_quarter(b, t, c % QUARTERS)
                        add_chunk(b, pair, c)
                for g in range(CHUNKS):
                    dve.wait_ge(turned, b * (4 * CHUNKS) + 3 * CHUNKS + g + 1)
                    dve.scalar_tensor_tensor(out_tok[:, 4 * g:4 * g + 4, :].rearrange("p t c -> p (t c)"),
                                             work_ps[g % 2][:, :], gamma_col[:, 0:1],
                                             x_tok[:, 4 * g:4 * g + 4, :].rearrange("p t c -> p (t c)"),
                                             ALU.mult, ALU.add).then_inc(x_copied, 1)
                    dve.wait_ge(x_copied, b * (4 * CHUNKS) + 3 * CHUNKS + g + 3)
                    dve.sem_inc(out_ready, 1)


def cosine_attention(nc, x, y, gamma, ident_in):
    TOK = 2048
    JT = TOK // P
    IQ = TOK // CHUNK
    PER = CHUNK // P
    H = 32
    KT = 2
    RING = 6
    LEAD = 4
    STEPS = IQ * JT
    BANKS = 4
    UNROLL = 2
    with ExitStack() as ctx:
        mem = Memory(nc, ctx, "l1")
        q_img = mem.sb("q_img", [P, UNROLL, H, C])
        hat = mem.sb("hat", [P, KT, CHUNK])
        hat_high = mem.sb("hat_high", [P, KT, TOK], F32R)
        hat_low = mem.sb("hat_low", [P, KT, TOK], F32R)
        q_tok = mem.sb("q_tok", [P, JT, KT * P])
        tok_high = mem.sb("tok_high", [P, JT, KT * P], F32R)
        tok_low = mem.sb("tok_low", [P, JT, KT * P], F32R)
        exps = mem.sb("exps", [P, RING, CHUNK])
        exps_high = mem.sb("exps_high", [P, RING, CHUNK], F32R)
        exps_low = mem.sb("exps_low", [P, RING, CHUNK], F32R)
        out_img = mem.sb("out_img", [P, H, C])
        square = mem.sb("square", [P, 2, KT * P])
        diag = mem.sb("diag", [P, JT, P])
        length = mem.sb("length", [P, JT])
        sums = mem.sb("sums", [P, JT, IQ])
        total = mem.sb("total", [P, JT])
        inverse = mem.sb("inverse", [P, JT])
        ones = mem.sb("ones", [P, P])
        ident = mem.sb("ident", [P, P])
        gamma_col = mem.sb("gamma_col", [P, 1])
        energy_ps = [mem.ps(f"energy{i}", [P, CHUNK]) for i in range(BANKS)]
        value_ps = [mem.ps(f"value{i}", [P, CHUNK]) for i in range(KT)]
        work_ps = [mem.ps(f"work{i}", [P, CHUNK]) for i in range(2)]

        const_in, ones_ready = mem.sem("const_in"), mem.sem("ones_ready")
        q_in = [mem.sem(f"q_in{u}") for u in range(UNROLL)]
        work_made = mem.sem("work_made")
        work_used = [mem.sem(f"work_used{i}") for i in range(2)]
        squared, length_ready, diag_step = mem.sem("squared"), mem.sem("length_ready"), mem.sem("diag_step")
        hat_step, tok_high_ready, tok_ready = mem.sem("hat_step"), mem.sem("tok_high_ready"), mem.sem("tok_ready")
        energy_made, exp_ready = mem.sem("energy_made"), mem.sem("exp_ready")
        exp_high_ready, exp_split = mem.sem("exp_high_ready"), mem.sem("exp_split")
        value_step, value_taken = mem.sem("value_step"), mem.sem("value_taken")
        scaled, out_ready, out_stored, out_free = mem.sem("scaled"), mem.sem("out_ready"), mem.sem("out_stored"), mem.sem("out_free")
        block = ctx.enter_context(nc.Block())

        x_v = x.rearrange("(g u) i (h r) c -> g u r i h c", r=2, u=UNROLL)
        y_v = y.rearrange("(g u) i (h r) c -> g u r i h c", r=2, u=UNROLL)
        q_cols = [q_img[:, u, :, :].rearrange("p h (w r) -> p r (h w)", r=2) for u in range(UNROLL)]
        out_cols = out_img[:, :, :].rearrange("p h (w r) -> p r (h w)", r=2)
        TURNS = JT // 2
        WORK = TURNS + 2 * IQ
        DIAG = 5

        def images(eng):
            with eng.Fori(0, B // UNROLL) as g:
                for u in range(UNROLL):
                    yield g * UNROLL + u, u, g

        @block.sync
        def _(sp):
            sp.dma_start(ident[:, :], ident_in).then_inc(const_in, 16)
            sp.dma_start(gamma_col[:, :], gamma).then_inc(const_in, 16)
            for b, u, g in images(sp):
                sp.wait_ge(out_ready, b * IQ + IQ)
                for r in range(2):
                    for a in range(0, H, 8):
                        sp.dma_start(q_img[64 * r:64 * r + 64, u, a:a + 8, :],
                                     x_v[bass.ds(g, 1), u, r, :, a:a + 8, :].rearrange("g i h c -> (g i) h c")).then_inc(q_in[u], 16)

        @block.gpsimd
        def _(pool):
            pool.sem_inc(out_ready, UNROLL * IQ)
            pool.memset(ones[:, :], 1.0).then_inc(ones_ready, 1)
            for b, u, g in images(pool):
                for k in range(IQ):
                    pool.wait_ge(out_ready, b * IQ + UNROLL * IQ + k + 1)
                    for r in range(2):
                        a = H // IQ * k
                        pool.dma_start(y_v[bass.ds(g, 1), u, r, :, a:a + 8, :].rearrange("g i h c -> (g i) h c"),
                                       out_img[64 * r:64 * r + 64, a:a + 8, :]).then_inc(out_stored, 16)
                pool.wait_ge(out_stored, b * 128 + 128)
                pool.sem_inc(out_free, 1)

        @block.tensor
        def _(pe):
            pe.wait_ge(const_in, 32)
            pe.wait_ge(ones_ready, 1)

            def energy(b, i):
                iq, jt = divmod(i, JT)
                if iq == 0 and jt % PER == 0:
                    pe.wait_ge(hat_step, b * (3 * IQ) + 3 * (jt // PER) + 3)
                pe.wait_ge(exp_ready, b * STEPS + i + 1)
                rows, cols = slice(jt * P, (jt + 1) * P), slice(iq * CHUNK, (iq + 1) * CHUNK)
                for k in range(KT):
                    mm = split_product(pe, energy_ps[i % BANKS][:, :], (hat_high[:, k, rows], hat_low[:, k, rows]),
                                       (hat_high[:, k, cols], hat_low[:, k, cols]), k == 0, k == KT - 1)
                mm.then_inc(energy_made, 1)

            def value(b, i):
                iq, jt = divmod(i, JT)
                if iq == 0 and jt % PER == 0:
                    pe.wait_ge(tok_ready, b * IQ + jt // PER + 1)
                pe.wait_ge(exp_split, b * STEPS + i + RING + 1)
                s = i % RING
                for k in range(KT):
                    if jt == 0:
                        pe.wait_ge(value_taken, b * (KT * IQ) + KT * iq + k + 1)
                    rows = slice(k * P, (k + 1) * P)
                    mm = split_product(pe, value_ps[k][:, :], (tok_high[:, jt, rows], tok_low[:, jt, rows]),
                                       (exps_high[:, s, :], exps_low[:, s, :]), jt == 0, jt == JT - 1)
                mm.then_inc(value_step, 1)

            def broadcast(b, w):
                c = w % IQ
                pe.wait_ge(work_used[w % 2], b * (WORK // 2) + w // 2 + 1)
                pe.matmul(work_ps[w % 2][:, :], ones[:, :], diag[:, PER * c:PER * c + PER, :].rearrange("p t c -> p (t c)"),
                          start=True, stop=True).then_inc(work_made, 1)

            for b, u, g in images(pe):
                pe.wait_ge(q_in[u], b * (128 // UNROLL) + (128 - u * (128 // UNROLL)))
                for w in range(TURNS):
                    pe.wait_ge(work_used[w % 2], b * (WORK // 2) + w // 2 + 1)
                    for m in range(4):
                        jt, k = 2 * w + m // 2, m % 2
                        mm = pe.transpose(work_ps[w % 2][:, m * P:(m + 1) * P], q_cols[u][:, k, jt * P:(jt + 1) * P], ident[:, :])
                    mm.then_inc(work_made, 1)
                pe.wait_ge(diag_step, b * DIAG + 2)
                for c in range(IQ):
                    broadcast(b, TURNS + c)
                for i in range(LEAD):
                    energy(b, i)
                for i in range(STEPS):
                    if i + LEAD < STEPS:
                        energy(b, i + LEAD)
                    value(b, i)
                pe.wait_ge(diag_step, b * DIAG + DIAG)
                for c in range(IQ):
                    broadcast(b, TURNS + IQ + c)

        @block.scalar
        def _(act):
            act.sem_inc(exp_ready, BANKS)
            act.sem_inc(exp_split, RING)
            for b, u, g in images(act):
                for w in range(TURNS):
                    act.wait_ge(work_made, b * WORK + w + 1)
                    if w > 0:
                        act.wait_ge(squared, b * JT + 2 * w)
                    for m in range(2):
                        jt = 2 * w + m
                        act.activation(square[:, m, :], work_ps[w % 2][:, m * KT * P:(m + 1) * KT * P], ACT.Square,
                                       accum_out=length[:, jt:jt + 1]).then_inc(squared, 1)
                    act.activation(q_tok[:, 2 * w:2 * w + 2, :].rearrange("p t c -> p (t c)"), work_ps[w % 2][:, :],
                                   ACT.Copy).then_inc(work_used[w % 2], 1)
                act.wait_ge(squared, b * JT + JT)
                act.activation(length[:, :], length[:, :], ACT.Sqrt).then_inc(length_ready, 1)
                for i in range(STEPS):
                    iq, jt = divmod(i, JT)
                    act.wait_ge(energy_made, b * STEPS + i + 1)
                    act.wait_ge(exp_split, b * STEPS + i + 1)
                    act.activation(exps[:, i % RING, :], energy_ps[i % BANKS][:, :], ACT.Exp,
                                   accum_out=sums[:, jt, iq:iq + 1]).then_inc(exp_ready, 1)

        @block.vector
        def _(dve):
            for bank in range(2):
                dve.sem_inc(work_used[bank], 1)
            dve.sem_inc(out_free, 1)
            dve.sem_inc(value_taken, 2)
            dve.sem_inc(value_step, RING)
            dve.wait_ge(const_in, 32)

            def diagonals(b, numbers, step):
                dve.reciprocal(inverse[:, :], numbers).then_inc(diag_step, 1)
                dve.wait_ge(diag_step, b * DIAG + step)
                dve.tensor_tensor(diag[:, :, :], ident[:, None, :].to_broadcast([P, JT, P]),
                                  inverse[:, :, None].to_broadcast([P, JT, P]), ALU.mult).then_inc(diag_step, 1)

            def unit_columns(b, u, c):
                w, cols = TURNS + c, slice(c * CHUNK, (c + 1) * CHUNK)
                first = b * (3 * IQ) + 3 * c
                dve.wait_ge(work_made, b * WORK + w + 1)
                dve.tensor_tensor(hat[:, :, :], q_cols[u][:, :, cols], work_ps[w % 2][:, None, :].to_broadcast([P, KT, CHUNK]),
                                  ALU.mult).then_inc(hat_step, 1)
                dve.wait_ge(hat_step, first + 1)
                dve.sem_inc(work_used[w % 2], 1)
                dve.tensor_copy(hat_high[:, :, cols], hat[:, :, :]).then_inc(hat_step, 1)
                dve.wait_ge(hat_step, first + 2)
                dve.tensor_tensor(hat_low[:, :, cols], hat[:, :, :], hat_high[:, :, cols].bitcast(F32), ALU.subtract).then_inc(hat_step, 1)

            def split_tokens(b, c):
                tiles = slice(PER * c, PER * c + PER)
                dve.tensor_copy(tok_high[:, tiles, :], q_tok[:, tiles, :]).then_inc(tok_high_ready, 1)
                dve.wait_ge(tok_high_ready, b * IQ + c + 1)
                dve.tensor_tensor(tok_low[:, tiles, :], q_tok[:, tiles, :], tok_high[:, tiles, :].bitcast(F32),
                                  ALU.subtract).then_inc(tok_ready, 1)

            def take(b, iq):
                cols = slice(iq * CHUNK, (iq + 1) * CHUNK)
                dve.wait_ge(value_step, b * STEPS + (iq + 1) * JT + RING)
                for k in range(KT):
                    dve.tensor_scalar(out_cols[:, k, cols], value_ps[k][:, :], gamma_col[:, 0:1], None, ALU.mult).then_inc(value_taken, 1)

            for b, u, g in images(dve):
                dve.wait_ge(length_ready, b + 1)
                diagonals(b, length[:, :], 1)
                unit_columns(b, u, 0)
                for bank in range(2):
                    dve.wait_ge(work_used[bank], b * (WORK // 2) + TURNS // 2 + 1)
                split_tokens(b, 0)
                for i in range(STEPS):
                    if i < JT and i % PER == 0 and i // PER + 1 < IQ:
                        unit_columns(b, u, i // PER + 1)
                        split_tokens(b, i // PER + 1)
                    s = i % RING
                    dve.wait_ge(exp_ready, b * STEPS + i + BANKS + 1)
                    dve.wait_ge(value_step, b * STEPS + i + 1)
                    dve.tensor_copy(exps_high[:, s, :], exps[:, s, :]).then_inc(exp_high_ready, 1)
                    dve.wait_ge(exp_high_ready, b * STEPS + i + 1)
                    dve.tensor_tensor(exps_low[:, s, :], exps[:, s, :], exps_high[:, s, :].bitcast(F32), ALU.subtract).then_inc(exp_split, 1)
                    if i == 2:
                        dve.wait_ge(out_free, b + 1)
                    if i > JT and i % JT == 2:
                        take(b, i // JT - 1)
                dve.tensor_reduce(total[:, :], sums[:, :, :], AX.X, ALU.add).then_inc(diag_step, 1)
                dve.wait_ge(diag_step, b * DIAG + 3)
                diagonals(b, total[:, :], 4)
                take(b, IQ - 1)
                dve.wait_ge(value_taken, b * (KT * IQ) + KT * IQ + 2)
                for c in range(IQ):
                    w = TURNS + IQ + c
                    cols = slice(c * CHUNK, (c + 1) * CHUNK)
                    dve.wait_ge(work_made, b * WORK + w + 1)
                    dve.tensor_tensor(out_cols[:, :, cols], out_cols[:, :, cols], work_ps[w % 2][:, None, :].to_broadcast([P, KT, CHUNK]),
                                      ALU.mult).then_inc(scaled, 1)
                    dve.wait_ge(scaled, b * IQ + c + 1)
                    dve.sem_inc(work_used[w % 2], 1)
                    dve.tensor_tensor(out_cols[:, :, cols], out_cols[:, :, cols], q_cols[u][:, :, cols], ALU.add).then_inc(out_ready, 1)


HEADS = 4
WIN = 7
QY, QX = 8, 16
RY, RX = QY + WIN - 1, QX + WIN - 1
BY, BX = HW // QY, HW // QX
KEYS = RY * RX
KEY_ROWS = [5, 5, 4]
MASKED = -1e30
EPS = 1e-5
SCALE = float(C // HEADS) ** -0.5


def region_start(k, side, region):
    return min(max(k * side - WIN // 2, 0), HW - region)


def neighbourhood_attention(nc, x, h_out, v_dram, w_qkv, w_proj, cols, rows, bias_in, ident_in):
    RING = 4
    with ExitStack() as ctx:
        mem = Memory(nc, ctx, "l2a")
        x_tok = mem.sb("x_tok", [P, TILES, C])
        res = mem.sb("res", [P, TILES, C])
        x_ch = mem.sb("x_ch", [P, N])
        x_sum = mem.sb("x_sum", [P, HW])
        q_sum = mem.sb("q_sum", [P, HW])
        k_ch = mem.sb("k_ch", [P, N])
        bias = mem.sb("bias", [P, HEADS, 9, KEYS])
        probs = mem.sb("probs", [P, RING, HEADS, KEYS])
        turned = mem.sb("turned", [P, 2, 3, HEADS, P])
        v_tile = mem.sb("v_tile", [P, 4, 3, C])
        v_stage = mem.sb("v_stage", [P, 2, 4, C])
        q_masked = mem.sb("q_masked", [P, 2, HEADS, P])
        o_band = mem.sb("o_band", [P, QY, HW])
        qkv_w = mem.sb("qkv_w", [P, 3 * C])
        proj_w = mem.sb("proj_w", [P, C])
        col = mem.sb("col", [P, 8])
        row = mem.sb("row", [P, 2, C])
        q_bias = mem.sb("q_bias", [P, 1])
        eps = mem.sb("eps", [P, 1])
        stats = mem.sb("stats", [P, TILES, 6])
        mean_var = mem.sb("mean_var", [P, TILES, 2])
        std = mem.sb("std", [P, TILES])
        maxima = mem.sb("maxima", [P, RING, HEADS])
        neg_max = mem.sb("neg_max", [P, RING, HEADS])
        sums = mem.sb("sums", [P, RING, HEADS])
        inverse = mem.sb("inverse", [P, RING, HEADS])
        ident = mem.sb("ident", [P, P])
        score_ps = [mem.ps(f"score{i}", [P, CHUNK]) for i in range(4)]
        turn_ps = [mem.ps(f"turn{i}", [P, CHUNK]) for i in range(3)]
        out_ps = mem.ps("out", [P, CHUNK])

        const_in, x_in, h_stored = mem.sem("const_in"), mem.sem("x_in"), mem.sem("h_stored")
        v_stored, v_in = [mem.sem(f"v_stored{i}") for i in range(2)], [mem.sem(f"v_in{i}") for i in range(4)]
        small_ready, res_ready, masked = mem.sem("small_ready"), mem.sem("res_ready"), mem.sem("masked")
        waited, pool_waited = mem.sem("waited"), mem.sem("pool_waited")
        norm_ready, sum_ready = mem.sem("norm_ready"), mem.sem("sum_ready")
        stat_ready, std_ready, x_normed = mem.sem("stat_ready"), mem.sem("std_ready"), mem.sem("x_normed")
        pre_made, pre_copied, v_copied = mem.sem("pre_made"), mem.sem("pre_copied"), mem.sem("v_copied")
        q_ready = mem.sem("q_ready")
        scored, score_used = mem.sem("scored"), mem.sem("score_used")
        neg_ready, exp_ready, inverse_ready = mem.sem("neg_ready"), mem.sem("exp_ready"), mem.sem("inverse_ready")
        probs_ready = mem.sem("probs_ready")
        turn_made = [mem.sem(f"turn_made{i}") for i in range(3)]
        turn_used = [mem.sem(f"turn_used{i}") for i in range(3)]
        tile_done, band_taken, h_ready = mem.sem("tile_done"), mem.sem("band_taken"), mem.sem("h_ready")
        block = ctx.enter_context(nc.Block())

        T = BY * BX
        PER0 = T + BY
        x_v = x.rearrange("b (t p) c -> b p t c", p=P)
        h_v = h_out.rearrange("b (t p) c -> b p t c", p=P)
        v_v = v_dram.rearrange("b (t p) c -> b p t c", p=P)
        v_img = v_dram.rearrange("b (y x) c -> b y x c", x=HW)
        k_img = k_ch[:, :].rearrange("p (y x) -> p y x", x=HW)

        made0 = [t + max(0, (t - 1) // BX) + 1 for t in range(T)]
        made0_band = [min(BX * (j + 1) + 1, T) + j + 1 for j in range(BY)]
        ACT_PRE = 17

        def place(i):
            j, k = divmod(i, BX)
            edge = lambda n, last: 0 if n == 0 else 2 if n == last else 1
            return j, k, region_start(j, QY, RY), region_start(k, QX, RX), 3 * edge(j, BY - 1) + edge(k, BX - 1)

        def store(sp, b, j):
            sp.wait_ge(h_ready, b * BY + j + 1)
            sp.dma_start(h_v[bass.ds(b, 1), :, 4 * j:4 * j + 4].rearrange("b p t c -> p (b t) c"), res[:, 4 * j:4 * j + 4, :]).then_inc(h_stored, 16)

        @block.sync
        def _(sp):
            for dst, src in ((qkv_w[:, :], w_qkv), (proj_w[:, :], w_proj), (col[:, :], cols), (row[:, :, :], rows),
                             (ident[:, :], ident_in), (bias[:, :, :, :], bias_in)):
                sp.dma_start(dst, src).then_inc(const_in, 16)
            with sp.Fori(0, B) as b:
                sp.wait_ge(pre_copied, b * ACT_PRE + 1)
                for a in range(0, TILES, 8):
                    sp.dma_start(x_tok[:, a:a + 8, :], x_v[bass.ds(b, 1), :, a:a + 8].rearrange("b p t c -> p (b t) c")).then_inc(x_in, 16)
                for g in range(8):
                    sp.wait_ge(v_copied, b * 8 + g + 1)
                    sp.dma_start(v_v[bass.ds(b, 1), :, 4 * g:4 * g + 4].rearrange("b p t c -> p (b t) c"),
                                 v_stage[:, g % 2, :, :]).then_inc(v_stored[g % 2], 16)
                for slot in range(2):
                    sp.wait_ge(v_stored[slot], b * 64 + 80)
                for i in range(T):
                    _, _, y0, x0, _ = place(i)
                    sp.wait_ge(tile_done, b * T + i + 1)
                    r0 = 0
                    for c, rows_c in enumerate(KEY_ROWS):
                        sp.dma_start(v_tile[0:rows_c * RX, i % 4, c, :],
                                     v_img[bass.ds(b, 1), y0 + r0:y0 + r0 + rows_c, x0:x0 + RX, :].rearrange("b r x c -> (b r) x c")).then_inc(v_in[i % 4], 16)
                        r0 += rows_c
                    if i % BX == BX - 1 and i >= 2 * BX:
                        store(sp, b, i // BX - 2)
                store(sp, b, BY - 2)
                store(sp, b, BY - 1)
            sp.wait_ge(h_stored, 16 * BY * B + 16)

        def weight(pool, b, i):
            s = i % RING
            pool.wait_ge(inverse_ready, b * T + i + 1)
            pool.tensor_tensor(probs[:, s, :, :], probs[:, s, :, :], inverse[:, s, :, None].to_broadcast([P, HEADS, KEYS]),
                               ALU.mult).then_inc(probs_ready, 1)

        @block.gpsimd
        def _(pool):
            pool.memset(eps[:, :], EPS).then_inc(small_ready, 1)
            pool.wait_ge(const_in, 96)
            pool.tensor_scalar(q_bias[:, :], col[:, 2:3], SCALE * HW, None, ALU.mult).then_inc(small_ready, 1)
            with pool.Fori(0, B) as b:
                pool.wait_ge(x_in, b * 64 + 64)
                pool.wait_ge(h_stored, b * (16 * BY) + 16)
                pool.tensor_tensor(res[:, :, :], x_tok[:, :, :], row[:, 1:2, :].to_broadcast([P, TILES, C]), ALU.add).then_inc(res_ready, 1)
                for i in range(T):
                    if i % BX == 0:
                        j = i // BX
                        pool.wait_ge(q_ready, b + 1)
                        pool.wait_ge(scored, b * (4 * T) + 16 * j + 8)
                        pool.sem_inc(pool_waited, 1)
                        for h in range(HEADS):
                            pool.tensor_scalar(q_masked[:, j % 2, h, :].rearrange("p (y x) -> p y x", x=QX),
                                               q_sum[:, QY * j:QY * j + QY, None].to_broadcast([P, QY, QX]), col[:, 4 + h:5 + h],
                                               None, ALU.mult).then_inc(masked, 1)
                    if i >= 1:
                        weight(pool, b, i - 1)
                weight(pool, b, T - 1)

        @block.tensor
        def _(pe):
            pe.wait_ge(const_in, 96)

            with pe.Fori(0, B) as b:
                pe.wait_ge(score_used, b * (4 * T) + 4)
                pe.wait_ge(x_normed, b * TILES + TILES)
                for g in range(8):
                    if g >= 4:
                        pe.wait_ge(pre_copied, b * ACT_PRE + g - 3 + 1)
                    for m in range(4):
                        mm = pe.transpose(score_ps[g % 4][:, m * P:(m + 1) * P], x_tok[:, 4 * g + m, :], ident[:, :])
                    mm.then_inc(pre_made, 1)
                for g in range(8):
                    w = 8 + g
                    pe.wait_ge(pre_copied, b * ACT_PRE + max(w - 3, g + 1) + 1)
                    pe.matmul(score_ps[w % 4][:, :], qkv_w[:, C:2 * C], x_ch[:, g * CHUNK:(g + 1) * CHUNK],
                              start=True, stop=True).then_inc(pre_made, 1)
                pe.wait_ge(sum_ready, b + 1)
                pe.wait_ge(pre_copied, b * ACT_PRE + 16 - 3 + 1)
                pe.matmul(score_ps[0][:, 0:HW], qkv_w[:, 0:C], x_sum[:, :], start=True, stop=True).then_inc(pre_made, 1)
                for g in range(8):
                    w = ACT_PRE + g
                    pe.wait_ge(pre_copied, b * ACT_PRE + min(w - 3, ACT_PRE) + 1)
                    if g >= 4:
                        pe.wait_ge(v_copied, b * 8 + g - 3)
                    for m in range(4):
                        t = 4 * g + m
                        mm = pe.matmul(score_ps[w % 4][:, m * P:(m + 1) * P], x_ch[:, t * P:(t + 1) * P], qkv_w[:, 2 * C:3 * C],
                                       start=True, stop=True)
                    mm.then_inc(pre_made, 1)
                pe.wait_ge(v_copied, b * 8 + 8)

                def scores(i):
                    j, _, y0, x0, _ = place(i)
                    pe.wait_ge(masked, b * (4 * BY) + 4 * j + 4)
                    for h in range(HEADS):
                        pe.wait_ge(score_used, b * (4 * T) + 4 * i + h + 1)
                        pe.matmul(score_ps[h][:, 0:KEYS], q_masked[:, j % 2, h, :], k_img[:, y0:y0 + RY, x0:x0 + RX],
                                  start=True, stop=True).then_inc(scored, 1)

                def turn(i):
                    j = i // BX
                    pe.wait_ge(probs_ready, b * T + i + 1)
                    k0 = 0
                    for c, rows_c in enumerate(KEY_ROWS):
                        n = rows_c * RX
                        use = b * PER0 + made0[i] - 1 if c == 0 else b * T + i
                        pe.wait_ge(turn_used[c], use + 1)
                        for h in range(HEADS):
                            mm = pe.transpose(turn_ps[c][0:n, h * P:(h + 1) * P], probs[:, i % RING, h, k0:k0 + n], ident[:, :])
                        mm.then_inc(turn_made[c], 1)
                        k0 += n

                def values(i):
                    j, k = divmod(i, BX)
                    pe.wait_ge(v_in[i % 4], (b * (T // 4) + i // 4 + 1) * (16 * 3))
                    if k == 0:
                        pe.wait_ge(band_taken, b * BY + j + 1)
                    for c, rows_c in enumerate(KEY_ROWS):
                        n = rows_c * RX
                        use = b * PER0 + made0[i] - 1 if c == 0 else b * T + i
                        pe.wait_ge(turn_used[c], use + 2)
                        for h in range(HEADS):
                            mm = pe.matmul(out_ps[32 * h:32 * h + 32, k * P:(k + 1) * P], v_tile[0:n, i % 4, c, 32 * h:32 * h + 32],
                                           turned[0:n, i % 2, c, h, :], start=(c == 0), stop=(c == 2))
                    mm.then_inc(tile_done, 1)

                def project(j):
                    pe.wait_ge(band_taken, b * BY + j + 2)
                    pe.wait_ge(turn_used[0], b * PER0 + made0_band[j])
                    flat = o_band[:, :, :].rearrange("p y x -> p (y x)")
                    for m in range(4):
                        mm = pe.matmul(turn_ps[0][:, m * P:(m + 1) * P], flat[:, m * P:(m + 1) * P], proj_w[:, :], start=True, stop=True)
                    mm.then_inc(turn_made[0], 1)

                for i in range(T + 4):
                    if i < T:
                        scores(i)
                    if i >= 4 and (i - 4) % BX == BX - 1:
                        project((i - 4) // BX)
                    if 2 <= i <= T + 1:
                        turn(i - 2)
                    if 3 <= i <= T + 2:
                        values(i - 3)

        @block.scalar
        def _(act):
            act.sem_inc(pre_copied, 1)
            act.sem_inc(turn_used[1], 1)
            act.sem_inc(turn_used[2], 1)
            act.wait_ge(small_ready, 2)
            act.wait_ge(const_in, 96)
            with act.Fori(0, B) as b:
                act.wait_ge(stat_ready, b * TILES + TILES)
                act.activation(std[:, :], mean_var[:, :, 1], ACT.Sqrt, bias=eps[:, 0:1]).then_inc(std_ready, 1)
                for g in range(8):
                    act.wait_ge(pre_made, b * 25 + g + 1)
                    act.activation(x_ch[:, g * CHUNK:(g + 1) * CHUNK], score_ps[g % 4][:, :], ACT.Identity,
                                   scale=col[:, 0:1], bias=col[:, 1:2]).then_inc(pre_copied, 1)
                for g in range(8):
                    act.wait_ge(pre_made, b * 25 + 8 + g + 1)
                    act.activation(k_ch[:, g * CHUNK:(g + 1) * CHUNK], score_ps[g % 4][:, :], ACT.Identity,
                                   bias=col[:, 3:4]).then_inc(pre_copied, 1)
                act.wait_ge(pre_made, b * 25 + 17)
                act.activation(q_sum[:, :], score_ps[0][:, 0:HW], ACT.Identity, scale=SCALE, bias=q_bias[:, 0:1]).then_inc(pre_copied, 1)
                act.wait_ge(pre_copied, b * ACT_PRE + ACT_PRE + 1)
                act.sem_inc(q_ready, 1)
                for i in range(T + 3):
                    if i >= 3:
                        t = i - 3
                        for c in (1, 2):
                            n = KEY_ROWS[c] * RX
                            act.wait_ge(turn_made[c], b * T + t + 1)
                            act.wait_ge(tile_done, b * T + t + 3)
                            act.activation(turned[0:n, t % 2, c, :, :].rearrange("p h q -> p (h q)"), turn_ps[c][0:n, :],
                                           ACT.Copy).then_inc(turn_used[c], 1)
                    if i < T:
                        act.wait_ge(neg_ready, b * T + i + 1)
                        s = i % RING
                        for h in range(HEADS):
                            act.activation(probs[:, s, h, :], probs[:, s, h, :], ACT.Exp, bias=neg_max[:, s, h:h + 1],
                                           accum_out=sums[:, s, h:h + 1]).then_inc(exp_ready, 1)

        @block.vector
        def _(dve):
            dve.sem_inc(score_used, 4)
            dve.sem_inc(scored, 24)
            dve.sem_inc(turn_used[0], 1)
            dve.sem_inc(tile_done, 4)
            dve.sem_inc(band_taken, 1)
            dve.sem_inc(h_stored, 16)
            for slot in range(2):
                dve.sem_inc(v_stored[slot], 16)
            dve.wait_ge(const_in, 96)
            with dve.Fori(0, B) as b:
                dve.wait_ge(x_in, b * 64 + 64)
                for t in range(TILES):
                    dve.bn_stats(stats[:, t, :], x_tok[:, t, :]).then_inc(norm_ready, 1)
                dve.wait_ge(norm_ready, b * (TILES + 1) + TILES)
                dve.sem_inc(waited, 1)
                for t in range(TILES):
                    dve.bn_aggr(mean_var[:, t, :], stats[:, t, :]).then_inc(stat_ready, 1)
                dve.wait_ge(std_ready, b + 1)
                dve.reciprocal(std[:, :], std[:, :]).then_inc(norm_ready, 1)
                dve.wait_ge(norm_ready, b * (TILES + 1) + TILES + 1)
                dve.wait_ge(res_ready, b + 1)
                for t in range(TILES):
                    dve.tensor_scalar(x_tok[:, t, :], x_tok[:, t, :], mean_var[:, t, 0:1], std[:, t:t + 1],
                                      ALU.subtract, ALU.mult).then_inc(x_normed, 1)
                dve.wait_ge(pre_copied, b * ACT_PRE + 8 + 1)
                dve.tensor_reduce(x_sum[:, :], x_ch[:, :].rearrange("p (y x) -> p y x", x=HW), AX.X, ALU.add).then_inc(sum_ready, 1)
                for g in range(8):
                    w = ACT_PRE + g
                    dve.wait_ge(pre_made, b * 25 + w + 1)
                    dve.wait_ge(v_stored[g % 2], b * 64 + 16 * (g // 2) + 16)
                    dve.tensor_tensor(v_stage[:, g % 2, :, :], score_ps[w % 4][:, :].rearrange("p (t c) -> p t c", c=C),
                                      row[:, 0:1, :].to_broadcast([P, 4, C]), ALU.add).then_inc(v_copied, 1)
                for i in range(T + 4):
                    if 3 <= i <= T + 2:
                        t = i - 3
                        n = KEY_ROWS[0] * RX
                        dve.wait_ge(turn_made[0], b * PER0 + made0[t])
                        dve.wait_ge(tile_done, b * T + t + 3)
                        dve.tensor_copy(turned[0:n, t % 2, 0, :, :].rearrange("p h q -> p (h q)"), turn_ps[0][0:n, :]).then_inc(turn_used[0], 1)
                    if i >= 4 and (i - 4) % BX == BX - 1:
                        j = (i - 4) // BX
                        dve.wait_ge(tile_done, b * T + BX * (j + 1) + 4)
                        for k in range(BX):
                            ins = dve.tensor_copy(o_band[:, :, k * QX:(k + 1) * QX],
                                                  out_ps[:, k * P:(k + 1) * P].rearrange("p (y x) -> p y x", x=QX))
                        ins.then_inc(band_taken, 1)
                    if i < T:
                        s = i % RING
                        cls = place(i)[4]
                        for h in range(HEADS):
                            dve.wait_ge(scored, b * (4 * T) + 4 * i + h + 25)
                            if h == 0 and i >= RING:
                                dve.wait_ge(turn_made[2], b * T + i - RING + 1)
                            dve.sem_inc(waited, 1)
                            dve.tensor_tensor_reduce(probs[:, s, h, :], score_ps[h][:, 0:KEYS], bias[:, h, cls, :], 1.0, -3e38,
                                                     ALU.add, ALU.max, maxima[:, s, h:h + 1]).then_inc(score_used, 1)
                        dve.wait_ge(score_used, b * (4 * T) + 4 * i + 8)
                        dve.tensor_scalar(neg_max[:, s, :], maxima[:, s, :], -1.0, None, ALU.mult).then_inc(neg_ready, 1)
                    if 1 <= i <= T:
                        s = (i - 1) % RING
                        dve.wait_ge(exp_ready, b * (4 * T) + 4 * (i - 1) + 4)
                        dve.reciprocal(inverse[:, s, :], sums[:, s, :]).then_inc(inverse_ready, 1)
                    if i >= 4 and (i - 4) % BX == BX - 1:
                        dve.wait_ge(turn_made[0], b * PER0 + made0_band[j])
                        r = res[:, 4 * j:4 * j + 4, :].rearrange("p t c -> p (t c)")
                        dve.tensor_tensor(r, r, turn_ps[0][:, :], ALU.add).then_inc(turn_used[0], 1)
                        dve.wait_ge(turn_used[0], b * PER0 + made0_band[j] + 1)
                        dve.sem_inc(h_ready, 1)


HID = 4 * C


def mlp(nc, h_in, y, w_fc1, w_fc2, cols, row_in, ident_in):
    F = HID // P
    with ExitStack() as ctx:
        mem = Memory(nc, ctx, "l2b")
        h_tok = mem.sb("h_tok", [P, TILES, C])
        n_tok = mem.sb("n_tok", [P, TILES, C])
        res = mem.sb("res", [P, TILES, C])
        n_ch = mem.sb("n_ch", [P, N])
        hidden = mem.sb("hidden", [P, 2, F, CHUNK])
        fc1_w = mem.sb("fc1_w", [P, HID])
        fc2_w = mem.sb("fc2_w", [P, F, C])
        col = mem.sb("col", [P, 6])
        row = mem.sb("row", [P, 1, C])
        eps = mem.sb("eps", [P, 1])
        stats = mem.sb("stats", [P, TILES, 6])
        mean_var = mem.sb("mean_var", [P, TILES, 2])
        std = mem.sb("std", [P, TILES])
        ident = mem.sb("ident", [P, P])
        turn_ps = [mem.ps(f"turn{i}", [P, CHUNK]) for i in range(2)]
        hid_ps = [mem.ps(f"hid{i}", [P, CHUNK]) for i in range(3)]
        out_ps = [mem.ps(f"out{i}", [P, CHUNK]) for i in range(2)]

        const_in, h_in_sem, y_stored = mem.sem("const_in"), mem.sem("h_in"), mem.sem("y_stored")
        eps_ready, res_ready, stats_ready = mem.sem("eps_ready"), mem.sem("res_ready"), mem.sem("stats_ready")
        aggr_ready, std_ready, inv_ready, normed = mem.sem("aggr_ready"), mem.sem("std_ready"), mem.sem("inv_ready"), mem.sem("normed")
        turned, n_ready = mem.sem("turned"), mem.sem("n_ready")
        hid_made, hid_ready, out_made, out_ready = mem.sem("hid_made"), mem.sem("hid_ready"), mem.sem("out_made"), mem.sem("out_ready")
        waited, sp_waited = mem.sem("waited"), mem.sem("sp_waited")
        block = ctx.enter_context(nc.Block())

        h_v = h_in.rearrange("b (t p) c -> b p t c", p=P)
        y_v = y.rearrange("b (t p) c -> b p t c", p=P)

        @block.sync
        def _(sp):
            for dst, src in ((fc1_w[:, :], w_fc1), (fc2_w[:, :, :], w_fc2.rearrange("(f p) c -> p f c", p=P)), (col[:, :], cols),
                             (row[:, :, :], row_in), (ident[:, :], ident_in)):
                sp.dma_start(dst, src).then_inc(const_in, 16)
            with sp.Fori(0, B) as b:
                sp.wait_ge(normed, b * TILES + 1)
                sp.sem_inc(sp_waited, 1)
                sp.wait_ge(res_ready, b + 1)
                for a in range(0, TILES, 8):
                    sp.dma_start(h_tok[:, a:a + 8, :], h_v[bass.ds(b, 1), :, a:a + 8].rearrange("b p t c -> p (b t) c")).then_inc(h_in_sem, 16)
                for g in range(CHUNKS):
                    sp.wait_ge(out_ready, b * CHUNKS + g + 3)
                    sp.dma_start(y_v[bass.ds(b, 1), :, 4 * g:4 * g + 4].rearrange("b p t c -> p (b t) c"), res[:, 4 * g:4 * g + 4, :]).then_inc(y_stored, 16)
            sp.wait_ge(y_stored, 16 * CHUNKS * B + 16)

        @block.gpsimd
        def _(pool):
            pool.memset(eps[:, :], EPS).then_inc(eps_ready, 1)
            pool.sem_inc(res_ready, 1)
            pool.sem_inc(y_stored, 16)
            pool.wait_ge(const_in, 80)
            with pool.Fori(0, B) as b:
                pool.wait_ge(h_in_sem, b * 64 + 64)
                pool.wait_ge(y_stored, b * (16 * CHUNKS) + 16)
                pool.tensor_tensor(res[:, :, :], h_tok[:, :, :], row[:, :, :].to_broadcast([P, TILES, C]), ALU.add).then_inc(res_ready, 1)

        @block.tensor
        def _(pe):
            pe.wait_ge(const_in, 80)
            with pe.Fori(0, B) as b:
                pe.wait_ge(normed, b * TILES + TILES + 1)

                def turn(g):
                    pe.wait_ge(n_ready, b * CHUNKS + g + 1)
                    for m in range(4):
                        mm = pe.transpose(turn_ps[g % 2][:, m * P:(m + 1) * P], n_tok[:, 4 * g + m, :], ident[:, :])
                    mm.then_inc(turned, 1)

                def up(g):
                    pe.wait_ge(n_ready, b * CHUNKS + g + 3)
                    for f in range(F):
                        i = g * F + f
                        pe.wait_ge(hid_ready, b * (CHUNKS * F) + i + 1)
                        pe.matmul(hid_ps[i % 3][:, :], fc1_w[:, f * P:(f + 1) * P], n_ch[:, g * CHUNK:(g + 1) * CHUNK],
                                  start=True, stop=True).then_inc(hid_made, 1)

                def down(g):
                    pe.wait_ge(hid_ready, b * (CHUNKS * F) + (g + 1) * F + 3)
                    pe.wait_ge(out_ready, b * CHUNKS + g + 1)
                    for m in range(4):
                        for f in range(F):
                            mm = pe.matmul(out_ps[g % 2][:, m * P:(m + 1) * P], hidden[:, g % 2, f, m * P:(m + 1) * P], fc2_w[:, f, :],
                                           start=(f == 0), stop=(f == F - 1))
                    mm.then_inc(out_made, 1)

                for g in range(CHUNKS):
                    turn(g)
                up(0)
                for g in range(CHUNKS):
                    if g + 1 < CHUNKS:
                        up(g + 1)
                    down(g)

        @block.scalar
        def _(act):
            act.sem_inc(n_ready, 2)
            act.sem_inc(hid_ready, 3)
            act.wait_ge(eps_ready, 1)
            act.wait_ge(const_in, 80)
            with act.Fori(0, B) as b:
                act.wait_ge(aggr_ready, b * TILES + TILES)
                act.activation(std[:, :], mean_var[:, :, 1], ACT.Sqrt, bias=eps[:, 0:1]).then_inc(std_ready, 1)
                for g in range(CHUNKS):
                    act.wait_ge(turned, b * CHUNKS + g + 1)
                    act.activation(n_ch[:, g * CHUNK:(g + 1) * CHUNK], turn_ps[g % 2][:, :], ACT.Identity,
                                   scale=col[:, 0:1], bias=col[:, 1:2]).then_inc(n_ready, 1)
                for i in range(CHUNKS * F):
                    g, f = divmod(i, F)
                    act.wait_ge(hid_made, b * (CHUNKS * F) + i + 1)
                    if f == 0 and g >= 2:
                        act.wait_ge(out_made, b * CHUNKS + g - 1)
                    act.activation(hidden[:, g % 2, f, :], hid_ps[i % 3][:, :], ACT.Gelu, bias=col[:, 2 + f:3 + f]).then_inc(hid_ready, 1)

        @block.vector
        def _(dve):
            dve.sem_inc(normed, 1)
            dve.sem_inc(out_ready, 2)
            with dve.Fori(0, B) as b:
                dve.wait_ge(h_in_sem, b * 64 + 64)
                for t in range(TILES):
                    dve.bn_stats(stats[:, t, :], h_tok[:, t, :]).then_inc(stats_ready, 1)
                dve.wait_ge(stats_ready, b * TILES + TILES)
                dve.sem_inc(waited, 1)
                for t in range(TILES):
                    dve.bn_aggr(mean_var[:, t, :], stats[:, t, :]).then_inc(aggr_ready, 1)
                dve.wait_ge(std_ready, b + 1)
                dve.reciprocal(std[:, :], std[:, :]).then_inc(inv_ready, 1)
                dve.wait_ge(inv_ready, b + 1)
                for t in range(TILES):
                    dve.tensor_scalar(n_tok[:, t, :], h_tok[:, t, :], mean_var[:, t, 0:1], std[:, t:t + 1],
                                      ALU.subtract, ALU.mult).then_inc(normed, 1)
                dve.wait_ge(res_ready, b + 2)
                for g in range(CHUNKS):
                    dve.wait_ge(out_made, b * CHUNKS + g + 1)
                    r = res[:, 4 * g:4 * g + 4, :].rearrange("p t c -> p (t c)")
                    dve.tensor_tensor(r, r, out_ps[g % 2][:, :], ALU.add).then_inc(out_ready, 1)


class Ring:

    def __init__(self, banks, owners, sems, seeds):
        self.banks, self.owners, self.sems, self.seeds = banks, owners, sems, seeds
        self.total = {e: owners.count(e) for e in sems}
        seen = {e: 0 for e in sems}
        self.index = []
        for e in owners:
            self.index.append(seen[e])
            seen[e] += 1

    def copied(self, b, u):
        e = self.owners[u]
        return self.sems[e], b * self.total[e] + self.index[u] + 1 + self.seeds[e]


def gated_conv_attention(nc, x, y, w_in, ident_in):
    PW = HW + 2
    ROWS = CHUNK // HW
    D, DV = 4, 16
    SCALE4 = 0.25
    MX = 9
    FLOOR = -1e10 / SCALE4
    with ExitStack() as ctx:
        mem = Memory(nc, ctx, "l3")
        x_tok = mem.sb("x_tok", [P, TILES, C])
        elu = mem.sb("elu", [P, PW, PW])
        conv1 = mem.sb("conv1", [P, PW, PW])
        c3 = mem.sb("c3", [P, N])
        qk = mem.sb("qk", [P, N])
        qk_rest = mem.sb("qk_rest", [P, N])
        parts = mem.sb("parts", [P, N], BF16)
        q_stack = mem.sb("q_stack", [P, N], BF16)
        k_stack = mem.sb("k_stack", [P, N], BF16)
        v_ext = mem.sb("v_ext", [P, TILES, DV + 1])
        exps = mem.sb("exps", [P, 3, CHUNK])
        low = mem.sb("low", [P, 3, CHUNK])
        gate = mem.sb("gate", [P, 2, CHUNK])
        sum_sb = mem.sb("sum_sb", [DV + 1, 2, CHUNK])
        inv_sum = mem.sb("inv_sum", [P, CHUNK])
        mixed = mem.sb("mixed", [P, 2, CHUNK])
        x_res = mem.sb("x_res", [P, 2, 4, C])
        maxima = mem.sb("maxima", [P, TILES, MX])
        neg_max = mem.sb("neg_max", [P, TILES])
        max_row = mem.sb("max_row", [TILES, P])
        max_rest = mem.sb("max_rest", [TILES, P])
        max_parts = mem.sb("max_parts", [TILES, 3, P], BF16)
        w1 = mem.sb("w1", [P, 9, C])
        w2 = mem.sb("w2", [P, 9, 2 * C])
        w_qk = mem.sb("w_qk", [P, P])
        w_v = mem.sb("w_v", [P, DV])
        w3 = mem.sb("w3", [P, C])
        w3_sum = mem.sb("w3_sum", [DV + 1, C])
        pick = mem.sb("pick", [P, DV + 1])
        ones_row = mem.sb("ones_row", [DV + 1, P])
        col = mem.sb("col", [P, 5])
        v_bias = mem.sb("v_bias", [P, 1, DV])
        ident = mem.sb("ident", [P, P])
        tri = mem.sb("tri", [P, 2, P])
        ident_bf = mem.sb("ident_bf", [P, P], BF16)
        tri_bf = mem.sb("tri_bf", [P, 2, P], BF16)
        work_ps = [mem.ps(f"work{i}", [P, CHUNK]) for i in range(3)]
        score_ps = [mem.ps(f"score{i}", [P, CHUNK]) for i in range(3)]
        sum_ps = [mem.ps(f"sum{i}", [P, CHUNK]) for i in range(2)]

        s = {n: mem.sem(n) for n in (
            "const_in x_in res_in0 res_in1 stacked max_stacked y_stored0 y_stored1 const_ready pads_ready work_made act_copied dve_copied low_ready "
            "low_exp low_less elu_ready qk_split v_made v_ready max_step max_cleared maxima_cleared "
            "score_made exp_ready summed sum_copied w3_made w3_ready out_step mixed_ready out_ready waited pool_waited").split()}
        block = ctx.enter_context(nc.Block())

        x_v = x.rearrange("b (t p) c -> b p t c", p=P)
        y_v = y.rearrange("b (t p) c -> b p t c", p=P)

        FIRST = [(t, c) for t in range(TILES) for c in range(t // 4 + 1)]
        SECOND = [(c, m) for c in range(CHUNKS) for m in range(4 * c + 4)]
        A0, B0, C0 = 0, CHUNKS, 2 * CHUNKS
        D0 = C0 + 2 * CHUNKS
        E0 = D0 + CHUNKS
        F0 = E0 + len(FIRST)
        H0 = F0 + 1
        owners = (["dve"] * CHUNKS + ["act"] * CHUNKS + ["act", "dve"] * CHUNKS + ["act"] * CHUNKS
                  + ["dve"] * len(FIRST) + ["dve"] + ["dve"] * (3 * CHUNKS))
        ring = Ring(3, owners, {"act": s["act_copied"], "dve": s["dve_copied"]}, {"act": 1, "dve": 1})
        USES = len(owners)

        def made(eng, b, u):
            eng.wait_ge(s["work_made"], b * USES + u + 1)

        def copied(eng, b, u):
            eng.wait_ge(*ring.copied(b, u))

        @block.sync
        def _(sp):
            for dst, src in ((w1[:, :, :], w_in["w1"].rearrange("t p c -> p t c")), (w2[:, :, :], w_in["w2"].rearrange("t p c -> p t c")),
                             (w_qk[:, :], w_in["w_qk"]), (w_v[:, :], w_in["w_v"]), (w3[:, :], w_in["w3"]), (pick[:, :], w_in["pick"]),
                             (ones_row[:, :], w_in["ones_row"]), (col[:, :], w_in["cols"]), (v_bias[:, :, :], w_in["v_bias"]),
                             (ident[:, :], ident_in), (tri[:, :, :], w_in["tri"])):
                sp.dma_start(dst, src).then_inc(s["const_in"], 16)
            with sp.Fori(0, B) as b:
                sp.wait_ge(s["work_made"], b * USES + 1)
                sp.sem_inc(s["waited"], 1)
                for a in range(0, TILES, 8):
                    sp.dma_start(x_tok[:, a:a + 8, :], x_v[bass.ds(b, 1), :, a:a + 8].rearrange("b p t c -> p (b t) c")).then_inc(s["x_in"], 16)
                sp.wait_ge(s["qk_split"], b * 5 + 5)
                for r in range(8):
                    left, right = PART_ROW[LEFT_PARTS[r]], PART_ROW[RIGHT_PARTS[r]]
                    sp.dma_start(q_stack[D * r:D * r + D, :], parts[left:left + D, :]).then_inc(s["stacked"], 16)
                    sp.dma_start(k_stack[D * r:D * r + D, :], parts[right + D:right + 2 * D, :]).then_inc(s["stacked"], 16)
                sp.wait_ge(s["max_step"], b * 7 + 7)
                for k in range(3):
                    sp.dma_start(q_stack[32 + k:33 + k, :], max_parts[:, k, :]).then_inc(s["max_stacked"], 16)
                for c in range(CHUNKS):
                    sp.wait_ge(s[f"y_stored{c % 2}"], b * 64 + 16 * (c // 2) + 16)
                    sp.dma_start(x_res[:, c % 2, :, :], x_v[bass.ds(b, 1), :, 4 * c:4 * c + 4].rearrange("b p t c -> p (b t) c")).then_inc(s[f"res_in{c % 2}"], 16)
                    sp.wait_ge(s["out_ready"], b * CHUNKS + c + 1)
                    sp.dma_start(y_v[bass.ds(b, 1), :, 4 * c:4 * c + 4].rearrange("b p t c -> p (b t) c"), x_res[:, c % 2, :, :]).then_inc(s[f"y_stored{c % 2}"], 16)
            for k in range(2):
                sp.wait_ge(s[f"y_stored{k}"], 64 * B + 16)

        @block.gpsimd
        def _(pool):
            pool.sem_inc(s["work_made"], 1)
            for k in range(2):
                pool.sem_inc(s[f"y_stored{k}"], 16)
            for t in (elu[:, :, :], conv1[:, :, :], q_stack[:, :], k_stack[:, :], v_ext[:, :, :]):
                pool.memset(t, 0.0).then_inc(s["pads_ready"], 1)
            pool.wait_ge(s["pads_ready"], 5)
            pool.memset(k_stack[32:64, :], 1.0).then_inc(s["pads_ready"], 1)
            pool.wait_ge(s["pads_ready"], 6)
            pool.memset(v_ext[:, :, DV:DV + 1], 1.0).then_inc(s["pads_ready"], 1)
            with pool.Fori(0, B) as b:
                for g in range(CHUNKS):
                    pool.wait_ge(s["low_exp"], b * CHUNKS + g + 1)
                    pool.sem_inc(s["pool_waited"], 1)
                    pool.tensor_scalar(low[:, g % 3, :], low[:, g % 3, :], -1.0, None, ALU.add).then_inc(s["low_less"], 1)
                pool.wait_ge(s["elu_ready"], b * CHUNKS + CHUNKS)
                pool.sem_inc(s["pool_waited"], 1)
                pool.memset(q_stack[32:64, :], 0.0).then_inc(s["max_cleared"], 1)

        @block.tensor
        def _(pe):
            pe.wait_ge(s["const_in"], 16 * 11)
            pe.wait_ge(s["pads_ready"], 7)
            pe.wait_ge(s["const_ready"], 2)
            pe.matmul(sum_ps[0][0:DV + 1, 0:C], pick[:, :], w3[:, :], start=True, stop=True).then_inc(s["w3_made"], 1)
            pe.wait_ge(s["w3_ready"], 1)
            with pe.Fori(0, B) as b:
                def bank(u):
                    if u >= 3:
                        copied(pe, b, u - 3)
                    return work_ps[u % 3]

                pe.wait_ge(s["dve_copied"], b * ring.total["dve"] + 1)
                pe.wait_ge(s["x_in"], b * 64 + 64)
                for g in range(CHUNKS):
                    ps = bank(A0 + g)
                    for m in range(4):
                        mm = pe.transpose(ps[:, m * P:(m + 1) * P], x_tok[:, 4 * g + m, :], ident[:, :])
                    mm.then_inc(s["work_made"], 1)

                def taps(ps, image, w, g):
                    for t in range(9):
                        dy, dx = divmod(t, 3)
                        mm = pe.matmul(ps[:, :], w[:, t, :], image[:, ROWS * g + dy:ROWS * g + dy + ROWS, dx:dx + HW],
                                       start=(t == 0), stop=(t == 8))
                    mm.then_inc(s["work_made"], 1)

                for g in range(CHUNKS):
                    ps = bank(B0 + g)
                    pe.wait_ge(s["elu_ready"], b * CHUNKS + min(g + 2, CHUNKS))
                    taps(ps, elu, w1, g)
                for g in range(CHUNKS):
                    for k in range(2):
                        ps = bank(C0 + 2 * g + k)
                        copied(pe, b, B0 + min(g + 1, CHUNKS - 1))
                        taps(ps, conv1, w2[:, :, C:2 * C] if k == 0 else w2[:, :, 0:C], g)
                for g in range(CHUNKS):
                    ps = bank(D0 + g)
                    copied(pe, b, C0 + 2 * g + 1)
                    pe.matmul(ps[:, :], w_qk[:, :], c3[:, g * CHUNK:(g + 1) * CHUNK], start=True, stop=True).then_inc(s["work_made"], 1)
                pe.wait_ge(s["sum_copied"], b * CHUNKS + 1)
                for t in range(TILES):
                    mm = pe.matmul(sum_ps[1][:, DV * t:DV * t + DV], c3[:, t * P:(t + 1) * P], w_v[:, :], start=True, stop=True)
                mm.then_inc(s["v_made"], 1)
                pe.wait_ge(s["stacked"], b * 256 + 256 + 16)
                pe.wait_ge(s["max_cleared"], b + 1)
                for i, (t, c) in enumerate(FIRST):
                    ps = bank(E0 + i)
                    wide = min(CHUNK, (t + 1) * P - c * CHUNK)
                    last = c == t // 4
                    mm = pe.matmul(ps[:, 0:wide], q_stack[:, t * P:(t + 1) * P], k_stack[:, c * CHUNK:c * CHUNK + wide],
                                   start=True, stop=not last)
                    if last:
                        mm = pe.matmul(ps[:, wide - P:wide], ident_bf[:, :], tri_bf[:, 0, :], start=False, stop=True)
                    mm.then_inc(s["work_made"], 1)
                ps = bank(F0)
                pe.wait_ge(s["max_step"], b * 7 + 1)
                pe.transpose(ps[0:TILES, 0:P], neg_max[:, :], ident[:, :]).then_inc(s["work_made"], 1)
                pe.wait_ge(s["max_stacked"], b * 48 + 48)
                pe.wait_ge(s["v_ready"], b + 1)

                def scores(i):
                    c, m = SECOND[i]
                    pe.wait_ge(s["exp_ready"], b * len(SECOND) + i + 1)
                    ps = score_ps[i % 3]
                    skip = max(0, m - 4 * c) * P
                    diagonal = m >= 4 * c
                    mm = pe.matmul(ps[:, skip:CHUNK], k_stack[:, m * P:(m + 1) * P], q_stack[:, c * CHUNK + skip:(c + 1) * CHUNK],
                                   start=True, stop=not diagonal)
                    if diagonal:
                        mm = pe.matmul(ps[:, skip:skip + P], ident_bf[:, :], tri_bf[:, 1, :], start=False, stop=True)
                    mm.then_inc(s["score_made"], 1)

                def values(i):
                    c, m = SECOND[i]
                    pe.wait_ge(s["exp_ready"], b * len(SECOND) + i + 4)
                    if m == 0:
                        pe.wait_ge(s["sum_copied"], b * CHUNKS + c + 1)
                    skip = max(0, m - 4 * c) * P
                    pe.matmul(sum_ps[c % 2][0:DV + 1, skip:CHUNK], v_ext[:, m, :], exps[:, i % 3, skip:CHUNK],
                              start=(m == 0), stop=(m == 4 * c + 3), skip_group_check=True).then_inc(s["summed"], 1)

                def mix(c):
                    pe.wait_ge(s["sum_copied"], b * CHUNKS + c + 3)
                    for k, w in ((0, ones_row), (1, w3_sum)):
                        ps = bank(H0 + 3 * c + k)
                        pe.matmul(ps[:, :], w[:, :], sum_sb[:, c % 2, :], start=True, stop=True).then_inc(s["work_made"], 1)

                def turn_back(c):
                    ps = bank(H0 + 3 * c + 2)
                    pe.wait_ge(s["mixed_ready"], b * CHUNKS + c + 1)
                    for m in range(4):
                        mm = pe.transpose(ps[:, m * P:(m + 1) * P], mixed[:, c % 2, m * P:(m + 1) * P], ident[:, :])
                    mm.then_inc(s["work_made"], 1)

                LEAD = 2
                for i in range(LEAD):
                    scores(i)
                for i, (c, m) in enumerate(SECOND):
                    if i + LEAD < len(SECOND):
                        scores(i + LEAD)
                    values(i)
                    if c > 0 and m == 2:
                        mix(c - 1)
                    if c > 0 and m == 6:
                        turn_back(c - 1)
                mix(CHUNKS - 1)
                turn_back(CHUNKS - 1)

        @block.scalar
        def _(act):
            act.sem_inc(s["act_copied"], 1)
            act.sem_inc(s["exp_ready"], 3)
            act.wait_ge(s["const_in"], 16 * 11)
            act.wait_ge(s["pads_ready"], 7)
            with act.Fori(0, B) as b:
                for g in range(CHUNKS):
                    act.wait_ge(s["low_ready"], b * CHUNKS + g + 1)
                    act.activation(low[:, g % 3, :], low[:, g % 3, :], ACT.Exp).then_inc(s["low_exp"], 1)
                for g in range(CHUNKS):
                    made(act, b, B0 + g + 1)
                    act.activation(conv1[:, 1 + ROWS * g:1 + ROWS * g + ROWS, 1:1 + HW],
                                   work_ps[(B0 + g) % 3][:, :].rearrange("p (y x) -> p y x", x=HW), ACT.Identity,
                                   bias=col[:, 0:1]).then_inc(s["act_copied"], 1)
                for g in range(CHUNKS):
                    u = C0 + 2 * g
                    made(act, b, u + 1)
                    if g >= 2:
                        copied(act, b, u - 3)
                    act.activation(gate[:, g % 2, :], work_ps[u % 3][:, :], ACT.Sigmoid, bias=col[:, 2:3]).then_inc(s["act_copied"], 1)
                for g in range(CHUNKS):
                    made(act, b, D0 + g + 1)
                    act.activation(qk[:, g * CHUNK:(g + 1) * CHUNK], work_ps[(D0 + g) % 3][:, :], ACT.Identity,
                                   bias=col[:, 4:5]).then_inc(s["act_copied"], 1)
                for i, (c, m) in enumerate(SECOND):
                    skip = max(0, m - 4 * c) * P
                    act.wait_ge(s["score_made"], b * len(SECOND) + i + 1)
                    act.wait_ge(s["summed"], b * len(SECOND) + i + 1)
                    act.activation(exps[:, i % 3, skip:CHUNK], score_ps[i % 3][:, skip:CHUNK], ACT.Exp, scale=SCALE4).then_inc(s["exp_ready"], 1)

        @block.vector
        def _(dve):
            dve.sem_inc(s["dve_copied"], 1)
            dve.sem_inc(s["summed"], 3)
            dve.sem_inc(s["sum_copied"], 2)
            dve.sem_inc(s["stacked"], 16)
            dve.wait_ge(s["const_in"], 16 * 11)
            dve.tensor_copy(ident_bf[:, :], ident[:, :]).then_inc(s["const_ready"], 1)
            dve.tensor_copy(tri_bf[:, :, :], tri[:, :, :]).then_inc(s["const_ready"], 1)
            dve.wait_ge(s["w3_made"], 1)
            dve.tensor_copy(w3_sum[:, :], sum_ps[0][0:DV + 1, 0:C]).then_inc(s["w3_ready"], 1)
            dve.wait_ge(s["pads_ready"], 7)
            with dve.Fori(0, B) as b:
                def low_part(g):
                    made(dve, b, A0 + g + 1)
                    dve.tensor_scalar(low[:, g % 3, :], work_ps[(A0 + g) % 3][:, :], 0.0, None, ALU.min).then_inc(s["low_ready"], 1)

                low_part(0)
                low_part(1)
                for g in range(CHUNKS):
                    if g + 2 < CHUNKS:
                        low_part(g + 2)
                    dve.wait_ge(s["low_less"], b * CHUNKS + g + 1)
                    dve.sem_inc(s["waited"], 1)
                    dve.scalar_tensor_tensor(elu[:, 1 + ROWS * g:1 + ROWS * g + ROWS, 1:1 + HW],
                                             work_ps[(A0 + g) % 3][:, :].rearrange("p (y x) -> p y x", x=HW), 0.0,
                                             low[:, g % 3, :].rearrange("p (y x) -> p y x", x=HW), ALU.max, ALU.add).then_inc(s["dve_copied"], 1)
                    dve.wait_ge(*ring.copied(b, A0 + g))
                    dve.sem_inc(s["elu_ready"], 1)
                for g in range(CHUNKS):
                    u = C0 + 2 * g + 1
                    made(dve, b, u + 1)
                    copied(dve, b, u - 1)
                    dve.scalar_tensor_tensor(c3[:, g * CHUNK:(g + 1) * CHUNK], work_ps[u % 3][:, :], col[:, 1:2], gate[:, g % 2, :],
                                             ALU.add, ALU.mult).then_inc(s["dve_copied"], 1)
                copied(dve, b, D0 + CHUNKS - 1)
                dve.wait_ge(s["stacked"], b * 256 + 16)
                dve.tensor_copy(parts[:, :], qk[:, :]).then_inc(s["qk_split"], 1)
                dve.wait_ge(s["qk_split"], b * 5 + 1)
                dve.tensor_tensor(qk_rest[64:128, :], qk[64:128, :], parts[64:128, :], ALU.subtract).then_inc(s["qk_split"], 1)
                dve.wait_ge(s["qk_split"], b * 5 + 2)
                dve.tensor_copy(parts[64:128, :], qk_rest[64:128, :]).then_inc(s["qk_split"], 1)
                dve.wait_ge(s["qk_split"], b * 5 + 3)
                dve.tensor_tensor(qk_rest[96:128, :], qk_rest[96:128, :], parts[96:128, :], ALU.subtract).then_inc(s["qk_split"], 1)
                dve.wait_ge(s["qk_split"], b * 5 + 4)
                dve.tensor_copy(parts[96:128, :], qk_rest[96:128, :]).then_inc(s["qk_split"], 1)
                dve.wait_ge(s["v_made"], b + 1)
                dve.tensor_tensor(v_ext[:, :, 0:DV], sum_ps[1][:, :].rearrange("p (t d) -> p t d", d=DV),
                                  v_bias[:, :, :].to_broadcast([P, TILES, DV]), ALU.add).then_inc(s["v_ready"], 1)
                dve.memset(maxima[:, :, :], FLOOR).then_inc(s["maxima_cleared"], 1)
                dve.wait_ge(s["maxima_cleared"], b + 1)
                for i, (t, c) in enumerate(FIRST):
                    wide = min(CHUNK, (t + 1) * P - c * CHUNK)
                    made(dve, b, E0 + i + 1)
                    dve.tensor_reduce(maxima[:, t, c:c + 1], work_ps[(E0 + i) % 3][:, 0:wide], AX.X, ALU.max).then_inc(s["dve_copied"], 1)
                copied(dve, b, F0 - 1)
                dve.tensor_reduce(neg_max[:, :], maxima[:, :, :], AX.X, ALU.max, negate=True).then_inc(s["max_step"], 1)
                made(dve, b, F0 + 1)
                dve.tensor_copy(max_row[:, :], work_ps[F0 % 3][0:TILES, 0:P]).then_inc(s["dve_copied"], 1)
                copied(dve, b, F0)
                rest = max_row
                for k in range(3):
                    dve.tensor_copy(max_parts[:, k, :], rest[:, :]).then_inc(s["max_step"], 1)
                    dve.wait_ge(s["max_step"], b * 7 + 2 + 2 * k)
                    out = max_rest
                    dve.tensor_tensor(out[:, :], rest[:, :], max_parts[:, k, :], ALU.subtract).then_inc(s["max_step"], 1)
                    dve.wait_ge(s["max_step"], b * 7 + 3 + 2 * k)
                    rest = max_rest
                for c in range(CHUNKS):
                    dve.wait_ge(s["summed"], b * len(SECOND) + 3 + 2 * (c + 1) * (c + 2))
                    dve.tensor_copy(sum_sb[:, c % 2, :], sum_ps[c % 2][0:DV + 1, :]).then_inc(s["sum_copied"], 1)
                    u = H0 + 3 * c
                    made(dve, b, u + 1)
                    dve.tensor_scalar(inv_sum[:, :], work_ps[u % 3][:, :], 1e-10, None, ALU.add).then_inc(s["dve_copied"], 1)
                    copied(dve, b, u)
                    dve.reciprocal(inv_sum[:, :], inv_sum[:, :]).then_inc(s["out_step"], 1)
                    made(dve, b, u + 2)
                    dve.wait_ge(s["out_step"], b * CHUNKS + c + 1)
                    dve.tensor_tensor(mixed[:, c % 2, :], work_ps[(u + 1) % 3][:, :], inv_sum[:, :], ALU.mult).then_inc(s["dve_copied"], 1)
                    copied(dve, b, u + 1)
                    dve.sem_inc(s["waited"], 1)
                    dve.scalar_tensor_tensor(mixed[:, c % 2, :], mixed[:, c % 2, :], col[:, 3:4], c3[:, c * CHUNK:(c + 1) * CHUNK],
                                             ALU.add, ALU.add).then_inc(s["mixed_ready"], 1)
                    made(dve, b, u + 3)
                    dve.wait_ge(s[f"res_in{c % 2}"], b * 64 + 16 * (c // 2) + 16)
                    out = x_res[:, c % 2, :, :].rearrange("p t c -> p (t c)")
                    dve.tensor_tensor(out, out, work_ps[(u + 2) % 3][:, :], ALU.add).then_inc(s["dve_copied"], 1)
                    copied(dve, b, u + 2)
                    dve.sem_inc(s["out_ready"], 1)


def program(nc, a, out):
    def scratch(name, shape):
        return nc.dram_tensor(name, shape, F32, kind="Internal").ap()

    y0, y1, h2, y2, v = (scratch(n, (B, N, C)) for n in ("l0_y", "l1_y", "l2_h", "l2_y", "l2_v"))
    flat = out.rearrange("b y x c -> b (y x) c")
    column_softmax_attention(nc, a["x"].rearrange("b y x c -> b (y x) c"), y0, a["l0_w_fg"], a["l0_w_h"], a["l0_gamma"], a["ident"])
    cosine_attention(nc, y0.rearrange("b (i j) c -> b i j c", j=HW), y1.rearrange("b (i j) c -> b i j c", j=HW), a["l1_gamma"], a["ident"])
    neighbourhood_attention(nc, y1, h2, v, a["l2a_w_qkv"], a["l2a_w_proj"], a["l2a_cols"], a["l2a_rows"], a["l2a_bias"], a["ident"])
    mlp(nc, h2, y2, a["l2b_w_fc1"], a["l2b_w_fc2"], a["l2b_cols"], a["l2b_row"], a["ident"])
    gated_conv_attention(nc, y2, flat, {n[3:]: a[n] for n in a if n.startswith("l3_")}, a["ident"])



def bias_layout(rpb):
    def axis(side, region):
        out = []
        last = HW // side - 1
        for k in (0, 1, last):
            q = k * side + np.arange(side)[:, None]
            key = region_start(k, side, region) + np.arange(region)[None, :]
            start = np.clip(q - WIN // 2, 0, HW - WIN)
            inside = (key >= start) & (key < start + WIN)
            out.append((np.where(inside, key - q + WIN - 1, 0), inside))
        return out
    ys, xs = axis(QY, RY), axis(QX, RX)
    out = np.full((QY * QX, 4, 9, RY * RX), MASKED, np.float32)
    for a, (ry, iny) in enumerate(ys):
        for c, (rx, inx) in enumerate(xs):
            inside = (iny[:, None, :, None] & inx[None, :, None, :]).reshape(QY * QX, RY * RX)
            iy = np.broadcast_to(ry[:, None, :, None], (QY, QX, RY, RX)).reshape(QY * QX, RY * RX)
            ix = np.broadcast_to(rx[None, :, None, :], (QY, QX, RY, RX)).reshape(QY * QX, RY * RX)
            for h in range(4):
                view = out[:, h, 3 * a + c, :]
                view[inside] = rpb[h][iy[inside], ix[inside]]
    return out

def l2a(I):
    k = lambda n: I['L2_conv_' + n]
    heads = np.zeros((128, 4), np.float32)
    for h in range(4): heads[32 * h:32 * h + 32, h] = 1
    cols = np.concatenate([k('ln1_g')[:, None], k('ln1_b')[:, None], k('qkv_b')[0:128, None], k('qkv_b')[128:256, None], heads], 1)
    rows = np.tile(np.stack([k('qkv_b')[256:384], k('proj_b')])[None], (128, 1, 1))
    return dict(w_qkv=k('qkv_w'), w_proj=k('proj_w'), cols=cols.astype(np.float32), rows=rows, bias=bias_layout(k('rpb')))

def l2b(I):
    k = lambda n: I['L2_conv_' + n]
    cols = np.concatenate([k('ln2_g')[:, None], k('ln2_b')[:, None], k('fc1_b').reshape(4, 128).T], 1)
    return dict(w_fc1=k('fc1_w'), w_fc2=k('fc2_w'), cols=np.ascontiguousarray(cols), row=np.tile(k('fc2_b')[None, None], (128, 1, 1)))

def l3(I):
    k = lambda n: I['L3_conv_' + n]
    C = 128
    group = np.concatenate([k('Wq'), k('Wk'), np.zeros((C, 24), np.float32)], 1)
    gbias = np.concatenate([k('bq'), k('bk'), np.zeros(24, np.float32)])
    pick = np.zeros((C, 17), np.float32)
    for d in range(16): pick[d::16, d] = 1
    ones_row = np.zeros((17, C), np.float32); ones_row[16] = 1
    a = np.arange(C)
    tri = np.zeros((C, 2, C), np.float32)
    tri[:, 0][a[None, :] >= a[:, None]] = -1e30
    tri[:, 1][a[:, None] >= a[None, :]] = -1e30
    cols = np.stack([k('b1'), k('b2')[0:C], k('b2')[C:2 * C], k('b3'), np.tile(gbias, 4)], 1)
    return dict(w1=k('W1').reshape(9, C, C), w2=k('W2').reshape(9, C, 2 * C), w_qk=np.tile(group, (1, 4)), w_v=k('Wv'), w3=k('W3'),
                pick=pick, ones_row=ones_row, cols=np.ascontiguousarray(cols), v_bias=np.tile(k('bv')[None, None], (C, 1, 1)), tri=tri)


def l0(I):
    k = lambda n: I["L0_conv_kernel_" + n][0, 0]
    return dict(w_fg=np.tile(np.concatenate([k("f"), k("g")], 1), (1, 4)), w_h=k("h"), gamma=np.tile(I["L0_conv_gamma"], (P, 1)))


def arrays_of(I):
    a = {"x": I["x"], "ident": np.eye(P, dtype=np.float32), "l1_gamma": np.tile(I["L1_conv_gamma"], (P, 1))}
    for stage, made in (("l0", l0(I)), ("l2a", l2a(I)), ("l2b", l2b(I)), ("l3", l3(I))):
        a.update({f"{stage}_{n}": v for n, v in made.items()})
    return {n: np.ascontiguousarray(v) for n, v in a.items()}


def kernel(**inputs):
    import concourse.bacc as _bacc
    from concourse.bass_utils import run_bass_kernel_spmd as _run

    nc = _bacc.Bacc("TRN2", target_bir_lowering=False, num_devices=1)
    arrays = arrays_of({n: np.asarray(v) for n, v in inputs.items()})
    aps = {n: nc.dram_tensor(f"in_{n}", v.shape, mybir.dt.from_np(v.dtype), kind="ExternalInput").ap() for n, v in arrays.items()}
    out = nc.dram_tensor("out_0", (B, HW, HW, C), F32, kind="ExternalOutput").ap()
    program(nc, aps, out)
    r = _run(nc, [{f"in_{n}": v for n, v in arrays.items()}], core_ids=[0])
    return r.results[0]["out_0"]
```

```python
from contextlib import ExitStack

import numpy as np
import concourse.bass as bass
from concourse import mybir

F32 = mybir.dt.float32
F32R = mybir.dt.float32r
BF16 = mybir.dt.bfloat16
ACT = mybir.ActivationFunctionType
ALU = mybir.AluOpType
AX = mybir.AxisListType

P = 128
B = 4
HW = 64
C = 128
N = HW * HW
TILES = N // P
CHUNK = 512
CHUNKS = N // CHUNK


class Memory:

    def __init__(self, nc, ctx, stage):
        self.nc, self.ctx, self.stage = nc, ctx, stage

    def sb(self, name, shape, dt=F32):
        return self.ctx.enter_context(self.nc.sbuf_tensor(f"{self.stage}_{name}", shape, dt))

    def ps(self, name, shape, dt=F32):
        return self.ctx.enter_context(self.nc.psum_tensor(f"{self.stage}_{name}", shape, dt))

    def sem(self, name):
        return self.ctx.enter_context(self.nc.semaphore(f"{self.stage}_{name}"))


def split_product(pe, out, left, right, start, stop):
    pe.matmul(out, left[1], right[0], start=start, stop=False)
    pe.matmul(out, left[0], right[1], start=False, stop=False)
    return pe.matmul(out, left[0], right[0], start=False, stop=stop)


LEFT_PARTS = [0, 0, 1, 1, 0, 2, 1, 2]
RIGHT_PARTS = [0, 1, 0, 1, 2, 0, 2, 1]
PART_ROW = [0, 64, 96]


def column_softmax_attention(nc, x, y, w_fg, w_h, gamma, ident_in):
    D = 16
    RING = 6
    GROUP = 2
    LEAD = 2
    QUARTER = 1024
    QUARTERS = N // QUARTER
    PAIRS = TILES // GROUP
    with ExitStack() as ctx:
        mem = Memory(nc, ctx, "l0")
        x_tok = mem.sb("x_tok", [P, TILES, C])
        x_ch = mem.sb("x_ch", [P, N])
        h_tok = mem.sb("h_tok", [P, TILES, C])
        out_tok = mem.sb("out_tok", [P, TILES, C])
        fg = out_tok[:, :, :].rearrange("p t c -> p (t c)")
        value = x_ch
        f_stack = mem.sb("f_stack", [P, N], BF16)
        g_stack = mem.sb("g_stack", [P, N], BF16)
        exps = mem.sb("exps", [P, RING, N])
        fg_rest = exps[:, RING - 1, :]
        parts = exps[:, RING - 2, 0:N // 2].bitcast(BF16)
        h_scaled = mem.sb("h_scaled", [P, RING, C])
        quarter_max = mem.sb("quarter_max", [P, RING, QUARTERS])
        neg_max = mem.sb("neg_max", [P, RING])
        total = mem.sb("total", [P, RING])
        inverse = mem.sb("inverse", [P, RING])
        fg_w = mem.sb("fg_w", [P, P])
        h_w = mem.sb("h_w", [P, C])
        gamma_col = mem.sb("gamma_col", [P, 1])
        ident = mem.sb("ident", [P, P])
        score_ps = [mem.ps(f"score{i}", [P, QUARTER]) for i in range(2)]
        value_ps = [mem.ps(f"value{i}", [P, CHUNK]) for i in range(2)]
        work_ps = [mem.ps(f"work{i}", [P, CHUNK]) for i in range(2)]

        const_in = mem.sem("const_in")
        x_in = mem.sem("x_in")
        x_stored = mem.sem("x_stored")
        turned = mem.sem("turned")
        x_copied = mem.sem("x_copied")
        fg_made = mem.sem("fg_made")
        fg_copied = mem.sem("fg_copied")
        split_step = mem.sem("split_step")
        stacked = mem.sem("stacked")
        h_made = mem.sem("h_made")
        h_copied = mem.sem("h_copied")
        scored = mem.sem("scored")
        score_copied = mem.sem("score_copied")
        max_ready = mem.sem("max_ready")
        neg_ready = mem.sem("neg_ready")
        exp_ready = mem.sem("exp_ready")
        inverse_ready = mem.sem("inverse_ready")
        h_scaled_ready = mem.sem("h_scaled_ready")
        value_made = mem.sem("value_made")
        value_added = mem.sem("value_added")
        back = mem.sem("back")
        out_ready = mem.sem("out_ready")
        block = ctx.enter_context(nc.Block())

        x_v = x.rearrange("b (t p) c -> b p t c", p=P)
        y_v = y.rearrange("b (t p) c -> b p t c", p=P)

        @block.sync
        def _(sp):
            sp.dma_start(fg_w[:, :], w_fg).then_inc(const_in, 16)
            sp.dma_start(h_w[:, :], w_h).then_inc(const_in, 16)
            sp.dma_start(gamma_col[:, :], gamma).then_inc(const_in, 16)
            sp.dma_start(ident[:, :], ident_in).then_inc(const_in, 16)
            with sp.Fori(0, B) as b:
                for a in range(0, TILES, 8):
                    sp.dma_start(x_tok[:, a:a + 8, :], x_v[bass.ds(b, 1), :, a:a + 8].rearrange("b p t c -> p (b t) c")).then_inc(x_in, 16)
                sp.wait_ge(split_step, b * 5 + 5)
                for r in range(8):
                    left, right = PART_ROW[LEFT_PARTS[r]], PART_ROW[RIGHT_PARTS[r]]
                    sp.dma_start(f_stack[D * r:D * r + D, :], parts[left:left + D, :]).then_inc(stacked, 16)
                    sp.dma_start(g_stack[D * r:D * r + D, :], parts[right + D:right + 2 * D, :]).then_inc(stacked, 16)
                sp.wait_ge(out_ready, b * CHUNKS + CHUNKS)
                for a in range(0, TILES, 8):
                    sp.dma_start(y_v[bass.ds(b, 1), :, a:a + 8].rearrange("b p t c -> p (b t) c"), out_tok[:, a:a + 8, :]).then_inc(x_stored, 16)
            sp.wait_ge(x_stored, 64 * B + 16)

        @block.tensor
        def _(pe):
            pe.wait_ge(const_in, 64)

            def scores(b, t):
                for q in range(QUARTERS):
                    i = t * QUARTERS + q
                    pe.wait_ge(score_copied, b * (TILES * QUARTERS) + i + 1)
                    for half in range(QUARTER // CHUNK):
                        a = q * QUARTER + half * CHUNK
                        mm = pe.matmul(score_ps[i % 2][:, half * CHUNK:(half + 1) * CHUNK],
                                       f_stack[:, t * P:(t + 1) * P], g_stack[:, a:a + CHUNK], start=True, stop=True)
                    mm.then_inc(scored, 1)
                    yield

            def values(b, pair):
                pe.wait_ge(exp_ready, b * TILES + GROUP * (pair + 1))
                pe.wait_ge(h_scaled_ready, b * TILES + GROUP * (pair + 1))
                for c in range(CHUNKS):
                    i = pair * CHUNKS + c
                    pe.wait_ge(value_added, b * (PAIRS * CHUNKS) + i + 1)
                    for k in range(GROUP):
                        slot = (GROUP * pair + k) % RING
                        mm = pe.matmul(value_ps[i % 2][:, :], h_scaled[:, slot, :],
                                       exps[:, slot, c * CHUNK:(c + 1) * CHUNK], start=(k == 0), stop=(k == GROUP - 1))
                    mm.then_inc(value_made, 1)
                    yield

            with pe.Fori(0, B) as b:
                pe.wait_ge(x_in, b * 64 + 64)
                for g in range(CHUNKS):
                    pe.wait_ge(x_copied, b * (4 * CHUNKS) + g + 1)
                    for k in range(4):
                        mm = pe.transpose(work_ps[g % 2][:, k * P:(k + 1) * P], x_tok[:, 4 * g + k, :], ident[:, :])
                    mm.then_inc(turned, 1)
                for c in range(CHUNKS):
                    pe.wait_ge(x_copied, b * (4 * CHUNKS) + CHUNKS + c + 1)
                    pe.wait_ge(x_copied, b * (4 * CHUNKS) + c + 3)
                    pe.matmul(work_ps[c % 2][:, :], fg_w[:, :], x_ch[:, c * CHUNK:(c + 1) * CHUNK],
                              start=True, stop=True).then_inc(turned, 1)
                for g in range(CHUNKS):
                    pe.wait_ge(x_copied, b * (4 * CHUNKS) + 2 * CHUNKS + g + 1)
                    for k in range(4):
                        t = 4 * g + k
                        mm = pe.matmul(work_ps[g % 2][:, k * P:(k + 1) * P], x_ch[:, t * P:(t + 1) * P], h_w[:, :],
                                       start=True, stop=True)
                    mm.then_inc(turned, 1)
                pe.wait_ge(stacked, b * 256 + 272)
                for t in range(LEAD * GROUP):
                    for _ in scores(b, t):
                        pass
                for pair in range(PAIRS):
                    ahead = [s for t in range(GROUP * (pair + LEAD), min(GROUP * (pair + LEAD + 1), TILES)) for s in (t,)]
                    steps = iter(())
                    if ahead:
                        def both():
                            for t in ahead:
                                yield from scores(b, t)
                        steps = both()
                    for _ in values(b, pair):
                        next(steps, None)
                    for _ in steps:
                        pass
                for g in range(CHUNKS):
                    if g == 0:
                        pe.wait_ge(value_added, b * (PAIRS * CHUNKS) + PAIRS * CHUNKS + 2)
                    pe.wait_ge(x_copied, b * (4 * CHUNKS) + 3 * CHUNKS + g + 1)
                    for k in range(4):
                        t = 4 * g + k
                        mm = pe.transpose(work_ps[g % 2][:, k * P:(k + 1) * P], value[:, t * P:(t + 1) * P], ident[:, :])
                    mm.then_inc(turned, 1)

        @block.scalar
        def _(act):
            act.sem_inc(x_copied, 2)
            act.sem_inc(x_stored, 16)
            with act.Fori(0, B) as b:
                for g in range(CHUNKS):
                    act.wait_ge(turned, b * (4 * CHUNKS) + g + 1)
                    act.activation(x_ch[:, g * CHUNK:(g + 1) * CHUNK], work_ps[g % 2][:, :], ACT.Copy).then_inc(x_copied, 1)
                act.wait_ge(x_stored, b * 64 + 16)
                for c in range(CHUNKS):
                    act.wait_ge(turned, b * (4 * CHUNKS) + CHUNKS + c + 1)
                    act.activation(fg[:, c * CHUNK:(c + 1) * CHUNK], work_ps[c % 2][:, :], ACT.Copy).then_inc(x_copied, 1)
                for g in range(CHUNKS):
                    act.wait_ge(turned, b * (4 * CHUNKS) + 2 * CHUNKS + g + 1)
                    act.activation(h_tok[:, 4 * g:4 * g + 4, :].rearrange("p t c -> p (t c)"), work_ps[g % 2][:, :],
                                   ACT.Copy).then_inc(x_copied, 1)
                for t in range(TILES):
                    slot = t % RING
                    act.wait_ge(neg_ready, b * TILES + t + 1)
                    act.activation(exps[:, slot, :], exps[:, slot, :], ACT.Exp, bias=neg_max[:, slot:slot + 1],
                                   accum_out=total[:, slot:slot + 1]).then_inc(exp_ready, 1)

        @block.vector
        def _(dve):
            dve.sem_inc(stacked, 16)
            dve.sem_inc(score_copied, 2)
            dve.sem_inc(value_added, 2)
            dve.wait_ge(const_in, 64)

            def take_quarter(b, t, q):
                i, slot = t * QUARTERS + q, t % RING
                dve.wait_ge(scored, b * (TILES * QUARTERS) + i + 1)
                dve.tensor_scalar(exps[:, slot, q * QUARTER:(q + 1) * QUARTER], score_ps[i % 2][:, :], 1.0, None,
                                  ALU.mult, ALU.max, accum_out=quarter_max[:, slot, q:q + 1]).then_inc(score_copied, 1)
                if q == QUARTERS - 1:
                    dve.wait_ge(score_copied, b * (TILES * QUARTERS) + i + 3)
                    dve.tensor_reduce(neg_max[:, slot:slot + 1], quarter_max[:, slot, :], AX.X, ALU.max,
                                      negate=True).then_inc(neg_ready, 1)

            def scale_h(b, t):
                slot = t % RING
                dve.wait_ge(exp_ready, b * TILES + t + 1)
                dve.reciprocal(inverse[:, slot:slot + 1], total[:, slot:slot + 1]).then_inc(inverse_ready, 1)
                dve.wait_ge(inverse_ready, b * TILES + t + 1)
                dve.tensor_scalar(h_scaled[:, slot, :], h_tok[:, t, :], inverse[:, slot:slot + 1], None,
                                  ALU.mult).then_inc(h_scaled_ready, 1)

            def add_chunk(b, pair, c):
                i = pair * CHUNKS + c
                out = value[:, c * CHUNK:(c + 1) * CHUNK]
                dve.wait_ge(value_made, b * (PAIRS * CHUNKS) + i + 1)
                if pair == 0:
                    dve.tensor_copy(out, value_ps[i % 2][:, :]).then_inc(value_added, 1)
                else:
                    dve.wait_ge(value_added, b * (PAIRS * CHUNKS) + i - CHUNKS + 3)
                    dve.tensor_tensor(out, out, value_ps[i % 2][:, :], ALU.add).then_inc(value_added, 1)

            with dve.Fori(0, B) as b:
                dve.wait_ge(x_copied, b * (4 * CHUNKS) + 2 * CHUNKS + 2)
                dve.wait_ge(stacked, b * 256 + 16)
                dve.tensor_copy(parts[:, :], fg[:, :]).then_inc(split_step, 1)
                dve.wait_ge(split_step, b * 5 + 1)
                dve.tensor_tensor(fg_rest[64:128, :], fg[64:128, :], parts[64:128, :], ALU.subtract).then_inc(split_step, 1)
                dve.wait_ge(split_step, b * 5 + 2)
                dve.tensor_copy(parts[64:128, :], fg_rest[64:128, :]).then_inc(split_step, 1)
                dve.wait_ge(split_step, b * 5 + 3)
                dve.tensor_tensor(fg_rest[96:128, :], fg_rest[96:128, :], parts[96:128, :], ALU.subtract).then_inc(split_step, 1)
                dve.wait_ge(split_step, b * 5 + 4)
                dve.tensor_copy(parts[96:128, :], fg_rest[96:128, :]).then_inc(split_step, 1)
                dve.wait_ge(split_step, b * 5 + 5)
                dve.wait_ge(x_copied, b * (4 * CHUNKS) + 3 * CHUNKS + 2)
                for t in range(LEAD * GROUP):
                    for q in range(QUARTERS):
                        take_quarter(b, t, q)
                for pair in range(PAIRS):
                    for k in range(GROUP):
                        scale_h(b, GROUP * pair + k)
                    for c in range(CHUNKS):
                        t = GROUP * (pair + LEAD) + c // QUARTERS
                        if t < TILES:
                            take_quarter(b, t, c % QUARTERS)
                        add_chunk(b, pair, c)
                for g in range(CHUNKS):
                    dve.wait_ge(turned, b * (4 * CHUNKS) + 3 * CHUNKS + g + 1)
                    dve.scalar_tensor_tensor(out_tok[:, 4 * g:4 * g + 4, :].rearrange("p t c -> p (t c)"),
                                             work_ps[g % 2][:, :], gamma_col[:, 0:1],
                                             x_tok[:, 4 * g:4 * g + 4, :].rearrange("p t c -> p (t c)"),
                                             ALU.mult, ALU.add).then_inc(x_copied, 1)
                    dve.wait_ge(x_copied, b * (4 * CHUNKS) + 3 * CHUNKS + g + 3)
                    dve.sem_inc(out_ready, 1)


def cosine_attention(nc, x, y, gamma, ident_in):
    TOK = 2048
    JT = TOK // P
    IQ = TOK // CHUNK
    PER = CHUNK // P
    H = 32
    KT = 2
    RING = 6
    LEAD = 4
    STEPS = IQ * JT
    BANKS = 4
    UNROLL = 2
    with ExitStack() as ctx:
        mem = Memory(nc, ctx, "l1")
        q_img = mem.sb("q_img", [P, UNROLL, H, C])
        hat = mem.sb("hat", [P, KT, CHUNK])
        hat_high = mem.sb("hat_high", [P, KT, TOK], F32R)
        hat_low = mem.sb("hat_low", [P, KT, TOK], F32R)
        q_tok = mem.sb("q_tok", [P, JT, KT * P])
        tok_high = mem.sb("tok_high", [P, JT, KT * P], F32R)
        tok_low = mem.sb("tok_low", [P, JT, KT * P], F32R)
        exps = mem.sb("exps", [P, RING, CHUNK])
        exps_high = mem.sb("exps_high", [P, RING, CHUNK], F32R)
        exps_low = mem.sb("exps_low", [P, RING, CHUNK], F32R)
        out_img = mem.sb("out_img", [P, H, C])
        square = mem.sb("square", [P, 2, KT * P])
        diag = mem.sb("diag", [P, JT, P])
        length = mem.sb("length", [P, JT])
        sums = mem.sb("sums", [P, JT, IQ])
        total = mem.sb("total", [P, JT])
        inverse = mem.sb("inverse", [P, JT])
        ones = mem.sb("ones", [P, P])
        ident = mem.sb("ident", [P, P])
        gamma_col = mem.sb("gamma_col", [P, 1])
        energy_ps = [mem.ps(f"energy{i}", [P, CHUNK]) for i in range(BANKS)]
        value_ps = [mem.ps(f"value{i}", [P, CHUNK]) for i in range(KT)]
        work_ps = [mem.ps(f"work{i}", [P, CHUNK]) for i in range(2)]

        const_in, ones_ready = mem.sem("const_in"), mem.sem("ones_ready")
        q_in = [mem.sem(f"q_in{u}") for u in range(UNROLL)]
        work_made = mem.sem("work_made")
        work_used = [mem.sem(f"work_used{i}") for i in range(2)]
        squared, length_ready, diag_step = mem.sem("squared"), mem.sem("length_ready"), mem.sem("diag_step")
        hat_step, tok_high_ready, tok_ready = mem.sem("hat_step"), mem.sem("tok_high_ready"), mem.sem("tok_ready")
        energy_made, exp_ready = mem.sem("energy_made"), mem.sem("exp_ready")
        exp_high_ready, exp_split = mem.sem("exp_high_ready"), mem.sem("exp_split")
        value_step, value_taken = mem.sem("value_step"), mem.sem("value_taken")
        scaled, out_ready, out_stored, out_free = mem.sem("scaled"), mem.sem("out_ready"), mem.sem("out_stored"), mem.sem("out_free")
        block = ctx.enter_context(nc.Block())

        x_v = x.rearrange("(g u) i (h r) c -> g u r i h c", r=2, u=UNROLL)
        y_v = y.rearrange("(g u) i (h r) c -> g u r i h c", r=2, u=UNROLL)
        q_cols = [q_img[:, u, :, :].rearrange("p h (w r) -> p r (h w)", r=2) for u in range(UNROLL)]
        out_cols = out_img[:, :, :].rearrange("p h (w r) -> p r (h w)", r=2)
        TURNS = JT // 2
        WORK = TURNS + 2 * IQ
        DIAG = 5

        def images(eng):
            with eng.Fori(0, B // UNROLL) as g:
                for u in range(UNROLL):
                    yield g * UNROLL + u, u, g

        @block.sync
        def _(sp):
            sp.dma_start(ident[:, :], ident_in).then_inc(const_in, 16)
            sp.dma_start(gamma_col[:, :], gamma).then_inc(const_in, 16)
            for b, u, g in images(sp):
                sp.wait_ge(out_ready, b * IQ + IQ)
                for r in range(2):
                    for a in range(0, H, 8):
                        sp.dma_start(q_img[64 * r:64 * r + 64, u, a:a + 8, :],
                                     x_v[bass.ds(g, 1), u, r, :, a:a + 8, :].rearrange("g i h c -> (g i) h c")).then_inc(q_in[u], 16)

        @block.gpsimd
        def _(pool):
            pool.sem_inc(out_ready, UNROLL * IQ)
            pool.memset(ones[:, :], 1.0).then_inc(ones_ready, 1)
            for b, u, g in images(pool):
                for k in range(IQ):
                    pool.wait_ge(out_ready, b * IQ + UNROLL * IQ + k + 1)
                    for r in range(2):
                        a = H // IQ * k
                        pool.dma_start(y_v[bass.ds(g, 1), u, r, :, a:a + 8, :].rearrange("g i h c -> (g i) h c"),
                                       out_img[64 * r:64 * r + 64, a:a + 8, :]).then_inc(out_stored, 16)
                pool.wait_ge(out_stored, b * 128 + 128)
                pool.sem_inc(out_free, 1)

        @block.tensor
        def _(pe):
            pe.wait_ge(const_in, 32)
            pe.wait_ge(ones_ready, 1)

            def energy(b, i):
                iq, jt = divmod(i, JT)
                if iq == 0 and jt % PER == 0:
                    pe.wait_ge(hat_step, b * (3 * IQ) + 3 * (jt // PER) + 3)
                pe.wait_ge(exp_ready, b * STEPS + i + 1)
                rows, cols = slice(jt * P, (jt + 1) * P), slice(iq * CHUNK, (iq + 1) * CHUNK)
                for k in range(KT):
                    mm = split_product(pe, energy_ps[i % BANKS][:, :], (hat_high[:, k, rows], hat_low[:, k, rows]),
                                       (hat_high[:, k, cols], hat_low[:, k, cols]), k == 0, k == KT - 1)
                mm.then_inc(energy_made, 1)

            def value(b, i):
                iq, jt = divmod(i, JT)
                if iq == 0 and jt % PER == 0:
                    pe.wait_ge(tok_ready, b * IQ + jt // PER + 1)
                pe.wait_ge(exp_split, b * STEPS + i + RING + 1)
                s = i % RING
                for k in range(KT):
                    if jt == 0:
                        pe.wait_ge(value_taken, b * (KT * IQ) + KT * iq + k + 1)
                    rows = slice(k * P, (k + 1) * P)
                    mm = split_product(pe, value_ps[k][:, :], (tok_high[:, jt, rows], tok_low[:, jt, rows]),
                                       (exps_high[:, s, :], exps_low[:, s, :]), jt == 0, jt == JT - 1)
                mm.then_inc(value_step, 1)

            def broadcast(b, w):
                c = w % IQ
                pe.wait_ge(work_used[w % 2], b * (WORK // 2) + w // 2 + 1)
                pe.matmul(work_ps[w % 2][:, :], ones[:, :], diag[:, PER * c:PER * c + PER, :].rearrange("p t c -> p (t c)"),
                          start=True, stop=True).then_inc(work_made, 1)

            for b, u, g in images(pe):
                pe.wait_ge(q_in[u], b * (128 // UNROLL) + (128 - u * (128 // UNROLL)))
                for w in range(TURNS):
                    pe.wait_ge(work_used[w % 2], b * (WORK // 2) + w // 2 + 1)
                    for m in range(4):
                        jt, k = 2 * w + m // 2, m % 2
                        mm = pe.transpose(work_ps[w % 2][:, m * P:(m + 1) * P], q_cols[u][:, k, jt * P:(jt + 1) * P], ident[:, :])
                    mm.then_inc(work_made, 1)
                pe.wait_ge(diag_step, b * DIAG + 2)
                for c in range(IQ):
                    broadcast(b, TURNS + c)
                for i in range(LEAD):
                    energy(b, i)
                for i in range(STEPS):
                    if i + LEAD < STEPS:
                        energy(b, i + LEAD)
                    value(b, i)
                pe.wait_ge(diag_step, b * DIAG + DIAG)
                for c in range(IQ):
                    broadcast(b, TURNS + IQ + c)

        @block.scalar
        def _(act):
            act.sem_inc(exp_ready, BANKS)
            act.sem_inc(exp_split, RING)
            for b, u, g in images(act):
                for w in range(TURNS):
                    act.wait_ge(work_made, b * WORK + w + 1)
                    if w > 0:
                        act.wait_ge(squared, b * JT + 2 * w)
                    for m in range(2):
                        jt = 2 * w + m
                        act.activation(square[:, m, :], work_ps[w % 2][:, m * KT * P:(m + 1) * KT * P], ACT.Square,
                                       accum_out=length[:, jt:jt + 1]).then_inc(squared, 1)
                    act.activation(q_tok[:, 2 * w:2 * w + 2, :].rearrange("p t c -> p (t c)"), work_ps[w % 2][:, :],
                                   ACT.Copy).then_inc(work_used[w % 2], 1)
                act.wait_ge(squared, b * JT + JT)
                act.activation(length[:, :], length[:, :], ACT.Sqrt).then_inc(length_ready, 1)
                for i in range(STEPS):
                    iq, jt = divmod(i, JT)
                    act.wait_ge(energy_made, b * STEPS + i + 1)
                    act.wait_ge(exp_split, b * STEPS + i + 1)
                    act.activation(exps[:, i % RING, :], energy_ps[i % BANKS][:, :], ACT.Exp,
                                   accum_out=sums[:, jt, iq:iq + 1]).then_inc(exp_ready, 1)

        @block.vector
        def _(dve):
            for bank in range(2):
                dve.sem_inc(work_used[bank], 1)
            dve.sem_inc(out_free, 1)
            dve.sem_inc(value_taken, 2)
            dve.sem_inc(value_step, RING)
            dve.wait_ge(const_in, 32)

            def diagonals(b, numbers, step):
                dve.reciprocal(inverse[:, :], numbers).then_inc(diag_step, 1)
                dve.wait_ge(diag_step, b * DIAG + step)
                dve.tensor_tensor(diag[:, :, :], ident[:, None, :].to_broadcast([P, JT, P]),
                                  inverse[:, :, None].to_broadcast([P, JT, P]), ALU.mult).then_inc(diag_step, 1)

            def unit_columns(b, u, c):
                w, cols = TURNS + c, slice(c * CHUNK, (c + 1) * CHUNK)
                first = b * (3 * IQ) + 3 * c
                dve.wait_ge(work_made, b * WORK + w + 1)
                dve.tensor_tensor(hat[:, :, :], q_cols[u][:, :, cols], work_ps[w % 2][:, None, :].to_broadcast([P, KT, CHUNK]),
                                  ALU.mult).then_inc(hat_step, 1)
                dve.wait_ge(hat_step, first + 1)
                dve.sem_inc(work_used[w % 2], 1)
                dve.tensor_copy(hat_high[:, :, cols], hat[:, :, :]).then_inc(hat_step, 1)
                dve.wait_ge(hat_step, first + 2)
                dve.tensor_tensor(hat_low[:, :, cols], hat[:, :, :], hat_high[:, :, cols].bitcast(F32), ALU.subtract).then_inc(hat_step, 1)

            def split_tokens(b, c):
                tiles = slice(PER * c, PER * c + PER)
                dve.tensor_copy(tok_high[:, tiles, :], q_tok[:, tiles, :]).then_inc(tok_high_ready, 1)
                dve.wait_ge(tok_high_ready, b * IQ + c + 1)
                dve.tensor_tensor(tok_low[:, tiles, :], q_tok[:, tiles, :], tok_high[:, tiles, :].bitcast(F32),
                                  ALU.subtract).then_inc(tok_ready, 1)

            def take(b, iq):
                cols = slice(iq * CHUNK, (iq + 1) * CHUNK)
                dve.wait_ge(value_step, b * STEPS + (iq + 1) * JT + RING)
                for k in range(KT):
                    dve.tensor_scalar(out_cols[:, k, cols], value_ps[k][:, :], gamma_col[:, 0:1], None, ALU.mult).then_inc(value_taken, 1)

            for b, u, g in images(dve):
                dve.wait_ge(length_ready, b + 1)
                diagonals(b, length[:, :], 1)
                unit_columns(b, u, 0)
                for bank in range(2):
                    dve.wait_ge(work_used[bank], b * (WORK // 2) + TURNS // 2 + 1)
                split_tokens(b, 0)
                for i in range(STEPS):
                    if i < JT and i % PER == 0 and i // PER + 1 < IQ:
                        unit_columns(b, u, i // PER + 1)
                        split_tokens(b, i // PER + 1)
                    s = i % RING
                    dve.wait_ge(exp_ready, b * STEPS + i + BANKS + 1)
                    dve.wait_ge(value_step, b * STEPS + i + 1)
                    dve.tensor_copy(exps_high[:, s, :], exps[:, s, :]).then_inc(exp_high_ready, 1)
                    dve.wait_ge(exp_high_ready, b * STEPS + i + 1)
                    dve.tensor_tensor(exps_low[:, s, :], exps[:, s, :], exps_high[:, s, :].bitcast(F32), ALU.subtract).then_inc(exp_split, 1)
                    if i == 2:
                        dve.wait_ge(out_free, b + 1)
                    if i > JT and i % JT == 2:
                        take(b, i // JT - 1)
                dve.tensor_reduce(total[:, :], sums[:, :, :], AX.X, ALU.add).then_inc(diag_step, 1)
                dve.wait_ge(diag_step, b * DIAG + 3)
                diagonals(b, total[:, :], 4)
                take(b, IQ - 1)
                dve.wait_ge(value_taken, b * (KT * IQ) + KT * IQ + 2)
                for c in range(IQ):
                    w = TURNS + IQ + c
                    cols = slice(c * CHUNK, (c + 1) * CHUNK)
                    dve.wait_ge(work_made, b * WORK + w + 1)
                    dve.tensor_tensor(out_cols[:, :, cols], out_cols[:, :, cols], work_ps[w % 2][:, None, :].to_broadcast([P, KT, CHUNK]),
                                      ALU.mult).then_inc(scaled, 1)
                    dve.wait_ge(scaled, b * IQ + c + 1)
                    dve.sem_inc(work_used[w % 2], 1)
                    dve.tensor_tensor(out_cols[:, :, cols], out_cols[:, :, cols], q_cols[u][:, :, cols], ALU.add).then_inc(out_ready, 1)


HEADS = 4
WIN = 7
QY, QX = 8, 16
RY, RX = QY + WIN - 1, QX + WIN - 1
BY, BX = HW // QY, HW // QX
KEYS = RY * RX
KEY_ROWS = [5, 5, 4]
MASKED = -1e30
EPS = 1e-5
SCALE = float(C // HEADS) ** -0.5


def region_start(k, side, region):
    return min(max(k * side - WIN // 2, 0), HW - region)


def neighbourhood_attention(nc, x, h_out, v_dram, w_qkv, w_proj, cols, rows, bias_in, ident_in):
    RING = 4
    with ExitStack() as ctx:
        mem = Memory(nc, ctx, "l2a")
        x_tok = mem.sb("x_tok", [P, TILES, C])
        res = mem.sb("res", [P, TILES, C])
        x_ch = mem.sb("x_ch", [P, N])
        x_sum = mem.sb("x_sum", [P, HW])
        q_sum = mem.sb("q_sum", [P, HW])
        k_ch = mem.sb("k_ch", [P, N])
        bias = mem.sb("bias", [P, HEADS, 9, KEYS])
        probs = mem.sb("probs", [P, RING, HEADS, KEYS])
        turned = mem.sb("turned", [P, 2, 3, HEADS, P])
        v_tile = mem.sb("v_tile", [P, 4, 3, C])
        v_stage = mem.sb("v_stage", [P, 2, 4, C])
        q_masked = mem.sb("q_masked", [P, 2, HEADS, P])
        o_band = mem.sb("o_band", [P, QY, HW])
        qkv_w = mem.sb("qkv_w", [P, 3 * C])
        proj_w = mem.sb("proj_w", [P, C])
        col = mem.sb("col", [P, 8])
        row = mem.sb("row", [P, 2, C])
        q_bias = mem.sb("q_bias", [P, 1])
        eps = mem.sb("eps", [P, 1])
        stats = mem.sb("stats", [P, TILES, 6])
        mean_var = mem.sb("mean_var", [P, TILES, 2])
        std = mem.sb("std", [P, TILES])
        maxima = mem.sb("maxima", [P, RING, HEADS])
        neg_max = mem.sb("neg_max", [P, RING, HEADS])
        sums = mem.sb("sums", [P, RING, HEADS])
        inverse = mem.sb("inverse", [P, RING, HEADS])
        ident = mem.sb("ident", [P, P])
        score_ps = [mem.ps(f"score{i}", [P, CHUNK]) for i in range(4)]
        turn_ps = [mem.ps(f"turn{i}", [P, CHUNK]) for i in range(3)]
        out_ps = mem.ps("out", [P, CHUNK])

        const_in, x_in, h_stored = mem.sem("const_in"), mem.sem("x_in"), mem.sem("h_stored")
        v_stored, v_in = [mem.sem(f"v_stored{i}") for i in range(2)], [mem.sem(f"v_in{i}") for i in range(4)]
        small_ready, res_ready, masked = mem.sem("small_ready"), mem.sem("res_ready"), mem.sem("masked")
        waited, pool_waited = mem.sem("waited"), mem.sem("pool_waited")
        norm_ready, sum_ready = mem.sem("norm_ready"), mem.sem("sum_ready")
        stat_ready, std_ready, x_normed = mem.sem("stat_ready"), mem.sem("std_ready"), mem.sem("x_normed")
        pre_made, pre_copied, v_copied = mem.sem("pre_made"), mem.sem("pre_copied"), mem.sem("v_copied")
        q_ready = mem.sem("q_ready")
        scored, score_used = mem.sem("scored"), mem.sem("score_used")
        neg_ready, exp_ready, inverse_ready = mem.sem("neg_ready"), mem.sem("exp_ready"), mem.sem("inverse_ready")
        probs_ready = mem.sem("probs_ready")
        turn_made = [mem.sem(f"turn_made{i}") for i in range(3)]
        turn_used = [mem.sem(f"turn_used{i}") for i in range(3)]
        tile_done, band_taken, h_ready = mem.sem("tile_done"), mem.sem("band_taken"), mem.sem("h_ready")
        block = ctx.enter_context(nc.Block())

        T = BY * BX
        PER0 = T + BY
        x_v = x.rearrange("b (t p) c -> b p t c", p=P)
        h_v = h_out.rearrange("b (t p) c -> b p t c", p=P)
        v_v = v_dram.rearrange("b (t p) c -> b p t c", p=P)
        v_img = v_dram.rearrange("b (y x) c -> b y x c", x=HW)
        k_img = k_ch[:, :].rearrange("p (y x) -> p y x", x=HW)

        made0 = [t + max(0, (t - 1) // BX) + 1 for t in range(T)]
        made0_band = [min(BX * (j + 1) + 1, T) + j + 1 for j in range(BY)]
        ACT_PRE = 17

        def place(i):
            j, k = divmod(i, BX)
            edge = lambda n, last: 0 if n == 0 else 2 if n == last else 1
            return j, k, region_start(j, QY, RY), region_start(k, QX, RX), 3 * edge(j, BY - 1) + edge(k, BX - 1)

        def store(sp, b, j):
            sp.wait_ge(h_ready, b * BY + j + 1)
            sp.dma_start(h_v[bass.ds(b, 1), :, 4 * j:4 * j + 4].rearrange("b p t c -> p (b t) c"), res[:, 4 * j:4 * j + 4, :]).then_inc(h_stored, 16)

        @block.sync
        def _(sp):
            for dst, src in ((qkv_w[:, :], w_qkv), (proj_w[:, :], w_proj), (col[:, :], cols), (row[:, :, :], rows),
                             (ident[:, :], ident_in), (bias[:, :, :, :], bias_in)):
                sp.dma_start(dst, src).then_inc(const_in, 16)
            with sp.Fori(0, B) as b:
                sp.wait_ge(pre_copied, b * ACT_PRE + 1)
                for a in range(0, TILES, 8):
                    sp.dma_start(x_tok[:, a:a + 8, :], x_v[bass.ds(b, 1), :, a:a + 8].rearrange("b p t c -> p (b t) c")).then_inc(x_in, 16)
                for g in range(8):
                    sp.wait_ge(v_copied, b * 8 + g + 1)
                    sp.dma_start(v_v[bass.ds(b, 1), :, 4 * g:4 * g + 4].rearrange("b p t c -> p (b t) c"),
                                 v_stage[:, g % 2, :, :]).then_inc(v_stored[g % 2], 16)
                for slot in range(2):
                    sp.wait_ge(v_stored[slot], b * 64 + 80)
                for i in range(T):
                    _, _, y0, x0, _ = place(i)
                    sp.wait_ge(tile_done, b * T + i + 1)
                    r0 = 0
                    for c, rows_c in enumerate(KEY_ROWS):
                        sp.dma_start(v_tile[0:rows_c * RX, i % 4, c, :],
                                     v_img[bass.ds(b, 1), y0 + r0:y0 + r0 + rows_c, x0:x0 + RX, :].rearrange("b r x c -> (b r) x c")).then_inc(v_in[i % 4], 16)
                        r0 += rows_c
                    if i % BX == BX - 1 and i >= 2 * BX:
                        store(sp, b, i // BX - 2)
                store(sp, b, BY - 2)
                store(sp, b, BY - 1)
            sp.wait_ge(h_stored, 16 * BY * B + 16)

        def weight(pool, b, i):
            s = i % RING
            pool.wait_ge(inverse_ready, b * T + i + 1)
            pool.tensor_tensor(probs[:, s, :, :], probs[:, s, :, :], inverse[:, s, :, None].to_broadcast([P, HEADS, KEYS]),
                               ALU.mult).then_inc(probs_ready, 1)

        @block.gpsimd
        def _(pool):
            pool.memset(eps[:, :], EPS).then_inc(small_ready, 1)
            pool.wait_ge(const_in, 96)
            pool.tensor_scalar(q_bias[:, :], col[:, 2:3], SCALE * HW, None, ALU.mult).then_inc(small_ready, 1)
            with pool.Fori(0, B) as b:
                pool.wait_ge(x_in, b * 64 + 64)
                pool.wait_ge(h_stored, b * (16 * BY) + 16)
                pool.tensor_tensor(res[:, :, :], x_tok[:, :, :], row[:, 1:2, :].to_broadcast([P, TILES, C]), ALU.add).then_inc(res_ready, 1)
                for i in range(T):
                    if i % BX == 0:
                        j = i // BX
                        pool.wait_ge(q_ready, b + 1)
                        pool.wait_ge(scored, b * (4 * T) + 16 * j + 8)
                        pool.sem_inc(pool_waited, 1)
                        for h in range(HEADS):
                            pool.tensor_scalar(q_masked[:, j % 2, h, :].rearrange("p (y x) -> p y x", x=QX),
                                               q_sum[:, QY * j:QY * j + QY, None].to_broadcast([P, QY, QX]), col[:, 4 + h:5 + h],
                                               None, ALU.mult).then_inc(masked, 1)
                    if i >= 1:
                        weight(pool, b, i - 1)
                weight(pool, b, T - 1)

        @block.tensor
        def _(pe):
            pe.wait_ge(const_in, 96)

            with pe.Fori(0, B) as b:
                pe.wait_ge(score_used, b * (4 * T) + 4)
                pe.wait_ge(x_normed, b * TILES + TILES)
                for g in range(8):
                    if g >= 4:
                        pe.wait_ge(pre_copied, b * ACT_PRE + g - 3 + 1)
                    for m in range(4):
                        mm = pe.transpose(score_ps[g % 4][:, m * P:(m + 1) * P], x_tok[:, 4 * g + m, :], ident[:, :])
                    mm.then_inc(pre_made, 1)
                for g in range(8):
                    w = 8 + g
                    pe.wait_ge(pre_copied, b * ACT_PRE + max(w - 3, g + 1) + 1)
                    pe.matmul(score_ps[w % 4][:, :], qkv_w[:, C:2 * C], x_ch[:, g * CHUNK:(g + 1) * CHUNK],
                              start=True, stop=True).then_inc(pre_made, 1)
                pe.wait_ge(sum_ready, b + 1)
                pe.wait_ge(pre_copied, b * ACT_PRE + 16 - 3 + 1)
                pe.matmul(score_ps[0][:, 0:HW], qkv_w[:, 0:C], x_sum[:, :], start=True, stop=True).then_inc(pre_made, 1)
                for g in range(8):
                    w = ACT_PRE + g
                    pe.wait_ge(pre_copied, b * ACT_PRE + min(w - 3, ACT_PRE) + 1)
                    if g >= 4:
                        pe.wait_ge(v_copied, b * 8 + g - 3)
                    for m in range(4):
                        t = 4 * g + m
                        mm = pe.matmul(score_ps[w % 4][:, m * P:(m + 1) * P], x_ch[:, t * P:(t + 1) * P], qkv_w[:, 2 * C:3 * C],
                                       start=True, stop=True)
                    mm.then_inc(pre_made, 1)
                pe.wait_ge(v_copied, b * 8 + 8)

                def scores(i):
                    j, _, y0, x0, _ = place(i)
                    pe.wait_ge(masked, b * (4 * BY) + 4 * j + 4)
                    for h in range(HEADS):
                        pe.wait_ge(score_used, b * (4 * T) + 4 * i + h + 1)
                        pe.matmul(score_ps[h][:, 0:KEYS], q_masked[:, j % 2, h, :], k_img[:, y0:y0 + RY, x0:x0 + RX],
                                  start=True, stop=True).then_inc(scored, 1)

                def turn(i):
                    j = i // BX
                    pe.wait_ge(probs_ready, b * T + i + 1)
                    k0 = 0
                    for c, rows_c in enumerate(KEY_ROWS):
                        n = rows_c * RX
                        use = b * PER0 + made0[i] - 1 if c == 0 else b * T + i
                        pe.wait_ge(turn_used[c], use + 1)
                        for h in range(HEADS):
                            mm = pe.transpose(turn_ps[c][0:n, h * P:(h + 1) * P], probs[:, i % RING, h, k0:k0 + n], ident[:, :])
                        mm.then_inc(turn_made[c], 1)
                        k0 += n

                def values(i):
                    j, k = divmod(i, BX)
                    pe.wait_ge(v_in[i % 4], (b * (T // 4) + i // 4 + 1) * (16 * 3))
                    if k == 0:
                        pe.wait_ge(band_taken, b * BY + j + 1)
                    for c, rows_c in enumerate(KEY_ROWS):
                        n = rows_c * RX
                        use = b * PER0 + made0[i] - 1 if c == 0 else b * T + i
                        pe.wait_ge(turn_used[c], use + 2)
                        for h in range(HEADS):
                            mm = pe.matmul(out_ps[32 * h:32 * h + 32, k * P:(k + 1) * P], v_tile[0:n, i % 4, c, 32 * h:32 * h + 32],
                                           turned[0:n, i % 2, c, h, :], start=(c == 0), stop=(c == 2))
                    mm.then_inc(tile_done, 1)

                def project(j):
                    pe.wait_ge(band_taken, b * BY + j + 2)
                    pe.wait_ge(turn_used[0], b * PER0 + made0_band[j])
                    flat = o_band[:, :, :].rearrange("p y x -> p (y x)")
                    for m in range(4):
                        mm = pe.matmul(turn_ps[0][:, m * P:(m + 1) * P], flat[:, m * P:(m + 1) * P], proj_w[:, :], start=True, stop=True)
                    mm.then_inc(turn_made[0], 1)

                for i in range(T + 4):
                    if i < T:
                        scores(i)
                    if i >= 4 and (i - 4) % BX == BX - 1:
                        project((i - 4) // BX)
                    if 2 <= i <= T + 1:
                        turn(i - 2)
                    if 3 <= i <= T + 2:
                        values(i - 3)

        @block.scalar
        def _(act):
            act.sem_inc(pre_copied, 1)
            act.sem_inc(turn_used[1], 1)
            act.sem_inc(turn_used[2], 1)
            act.wait_ge(small_ready, 2)
            act.wait_ge(const_in, 96)
            with act.Fori(0, B) as b:
                act.wait_ge(stat_ready, b * TILES + TILES)
                act.activation(std[:, :], mean_var[:, :, 1], ACT.Sqrt, bias=eps[:, 0:1]).then_inc(std_ready, 1)
                for g in range(8):
                    act.wait_ge(pre_made, b * 25 + g + 1)
                    act.activation(x_ch[:, g * CHUNK:(g + 1) * CHUNK], score_ps[g % 4][:, :], ACT.Identity,
                                   scale=col[:, 0:1], bias=col[:, 1:2]).then_inc(pre_copied, 1)
                for g in range(8):
                    act.wait_ge(pre_made, b * 25 + 8 + g + 1)
                    act.activation(k_ch[:, g * CHUNK:(g + 1) * CHUNK], score_ps[g % 4][:, :], ACT.Identity,
                                   bias=col[:, 3:4]).then_inc(pre_copied, 1)
                act.wait_ge(pre_made, b * 25 + 17)
                act.activation(q_sum[:, :], score_ps[0][:, 0:HW], ACT.Identity, scale=SCALE, bias=q_bias[:, 0:1]).then_inc(pre_copied, 1)
                act.wait_ge(pre_copied, b * ACT_PRE + ACT_PRE + 1)
                act.sem_inc(q_ready, 1)
                for i in range(T + 3):
                    if i >= 3:
                        t = i - 3
                        for c in (1, 2):
                            n = KEY_ROWS[c] * RX
                            act.wait_ge(turn_made[c], b * T + t + 1)
                            act.wait_ge(tile_done, b * T + t + 3)
                            act.activation(turned[0:n, t % 2, c, :, :].rearrange("p h q -> p (h q)"), turn_ps[c][0:n, :],
                                           ACT.Copy).then_inc(turn_used[c], 1)
                    if i < T:
                        act.wait_ge(neg_ready, b * T + i + 1)
                        s = i % RING
                        for h in range(HEADS):
                            act.activation(probs[:, s, h, :], probs[:, s, h, :], ACT.Exp, bias=neg_max[:, s, h:h + 1],
                                           accum_out=sums[:, s, h:h + 1]).then_inc(exp_ready, 1)

        @block.vector
        def _(dve):
            dve.sem_inc(score_used, 4)
            dve.sem_inc(scored, 24)
            dve.sem_inc(turn_used[0], 1)
            dve.sem_inc(tile_done, 4)
            dve.sem_inc(band_taken, 1)
            dve.sem_inc(h_stored, 16)
            for slot in range(2):
                dve.sem_inc(v_stored[slot], 16)
            dve.wait_ge(const_in, 96)
            with dve.Fori(0, B) as b:
                dve.wait_ge(x_in, b * 64 + 64)
                for t in range(TILES):
                    dve.bn_stats(stats[:, t, :], x_tok[:, t, :]).then_inc(norm_ready, 1)
                dve.wait_ge(norm_ready, b * (TILES + 1) + TILES)
                dve.sem_inc(waited, 1)
                for t in range(TILES):
                    dve.bn_aggr(mean_var[:, t, :], stats[:, t, :]).then_inc(stat_ready, 1)
                dve.wait_ge(std_ready, b + 1)
                dve.reciprocal(std[:, :], std[:, :]).then_inc(norm_ready, 1)
                dve.wait_ge(norm_ready, b * (TILES + 1) + TILES + 1)
                dve.wait_ge(res_ready, b + 1)
                for t in range(TILES):
                    dve.tensor_scalar(x_tok[:, t, :], x_tok[:, t, :], mean_var[:, t, 0:1], std[:, t:t + 1],
                                      ALU.subtract, ALU.mult).then_inc(x_normed, 1)
                dve.wait_ge(pre_copied, b * ACT_PRE + 8 + 1)
                dve.tensor_reduce(x_sum[:, :], x_ch[:, :].rearrange("p (y x) -> p y x", x=HW), AX.X, ALU.add).then_inc(sum_ready, 1)
                for g in range(8):
                    w = ACT_PRE + g
                    dve.wait_ge(pre_made, b * 25 + w + 1)
                    dve.wait_ge(v_stored[g % 2], b * 64 + 16 * (g // 2) + 16)
                    dve.tensor_tensor(v_stage[:, g % 2, :, :], score_ps[w % 4][:, :].rearrange("p (t c) -> p t c", c=C),
                                      row[:, 0:1, :].to_broadcast([P, 4, C]), ALU.add).then_inc(v_copied, 1)
                for i in range(T + 4):
                    if 3 <= i <= T + 2:
                        t = i - 3
                        n = KEY_ROWS[0] * RX
                        dve.wait_ge(turn_made[0], b * PER0 + made0[t])
                        dve.wait_ge(tile_done, b * T + t + 3)
                        dve.tensor_copy(turned[0:n, t % 2, 0, :, :].rearrange("p h q -> p (h q)"), turn_ps[0][0:n, :]).then_inc(turn_used[0], 1)
                    if i >= 4 and (i - 4) % BX == BX - 1:
                        j = (i - 4) // BX
                        dve.wait_ge(tile_done, b * T + BX * (j + 1) + 4)
                        for k in range(BX):
                            ins = dve.tensor_copy(o_band[:, :, k * QX:(k + 1) * QX],
                                                  out_ps[:, k * P:(k + 1) * P].rearrange("p (y x) -> p y x", x=QX))
                        ins.then_inc(band_taken, 1)
                    if i < T:
                        s = i % RING
                        cls = place(i)[4]
                        for h in range(HEADS):
                            dve.wait_ge(scored, b * (4 * T) + 4 * i + h + 25)
                            if h == 0 and i >= RING:
                                dve.wait_ge(turn_made[2], b * T + i - RING + 1)
                            dve.sem_inc(waited, 1)
                            dve.tensor_tensor_reduce(probs[:, s, h, :], score_ps[h][:, 0:KEYS], bias[:, h, cls, :], 1.0, -3e38,
                                                     ALU.add, ALU.max, maxima[:, s, h:h + 1]).then_inc(score_used, 1)
                        dve.wait_ge(score_used, b * (4 * T) + 4 * i + 8)
                        dve.tensor_scalar(neg_max[:, s, :], maxima[:, s, :], -1.0, None, ALU.mult).then_inc(neg_ready, 1)
                    if 1 <= i <= T:
                        s = (i - 1) % RING
                        dve.wait_ge(exp_ready, b * (4 * T) + 4 * (i - 1) + 4)
                        dve.reciprocal(inverse[:, s, :], sums[:, s, :]).then_inc(inverse_ready, 1)
                    if i >= 4 and (i - 4) % BX == BX - 1:
                        dve.wait_ge(turn_made[0], b * PER0 + made0_band[j])
                        r = res[:, 4 * j:4 * j + 4, :].rearrange("p t c -> p (t c)")
                        dve.tensor_tensor(r, r, turn_ps[0][:, :], ALU.add).then_inc(turn_used[0], 1)
                        dve.wait_ge(turn_used[0], b * PER0 + made0_band[j] + 1)
                        dve.sem_inc(h_ready, 1)


HID = 4 * C


def mlp(nc, h_in, y, w_fc1, w_fc2, cols, row_in, ident_in):
    F = HID // P
    with ExitStack() as ctx:
        mem = Memory(nc, ctx, "l2b")
        h_tok = mem.sb("h_tok", [P, TILES, C])
        n_tok = mem.sb("n_tok", [P, TILES, C])
        res = mem.sb("res", [P, TILES, C])
        n_ch = mem.sb("n_ch", [P, N])
        hidden = mem.sb("hidden", [P, 2, F, CHUNK])
        fc1_w = mem.sb("fc1_w", [P, HID])
        fc2_w = mem.sb("fc2_w", [P, F, C])
        col = mem.sb("col", [P, 6])
        row = mem.sb("row", [P, 1, C])
        eps = mem.sb("eps", [P, 1])
        stats = mem.sb("stats", [P, TILES, 6])
        mean_var = mem.sb("mean_var", [P, TILES, 2])
        std = mem.sb("std", [P, TILES])
        ident = mem.sb("ident", [P, P])
        turn_ps = [mem.ps(f"turn{i}", [P, CHUNK]) for i in range(2)]
        hid_ps = [mem.ps(f"hid{i}", [P, CHUNK]) for i in range(3)]
        out_ps = [mem.ps(f"out{i}", [P, CHUNK]) for i in range(2)]

        const_in, h_in_sem, y_stored = mem.sem("const_in"), mem.sem("h_in"), mem.sem("y_stored")
        eps_ready, res_ready, stats_ready = mem.sem("eps_ready"), mem.sem("res_ready"), mem.sem("stats_ready")
        aggr_ready, std_ready, inv_ready, normed = mem.sem("aggr_ready"), mem.sem("std_ready"), mem.sem("inv_ready"), mem.sem("normed")
        turned, n_ready = mem.sem("turned"), mem.sem("n_ready")
        hid_made, hid_ready, out_made, out_ready = mem.sem("hid_made"), mem.sem("hid_ready"), mem.sem("out_made"), mem.sem("out_ready")
        waited, sp_waited = mem.sem("waited"), mem.sem("sp_waited")
        block = ctx.enter_context(nc.Block())

        h_v = h_in.rearrange("b (t p) c -> b p t c", p=P)
        y_v = y.rearrange("b (t p) c -> b p t c", p=P)

        @block.sync
        def _(sp):
            for dst, src in ((fc1_w[:, :], w_fc1), (fc2_w[:, :, :], w_fc2.rearrange("(f p) c -> p f c", p=P)), (col[:, :], cols),
                             (row[:, :, :], row_in), (ident[:, :], ident_in)):
                sp.dma_start(dst, src).then_inc(const_in, 16)
            with sp.Fori(0, B) as b:
                sp.wait_ge(normed, b * TILES + 1)
                sp.sem_inc(sp_waited, 1)
                sp.wait_ge(res_ready, b + 1)
                for a in range(0, TILES, 8):
                    sp.dma_start(h_tok[:, a:a + 8, :], h_v[bass.ds(b, 1), :, a:a + 8].rearrange("b p t c -> p (b t) c")).then_inc(h_in_sem, 16)
                for g in range(CHUNKS):
                    sp.wait_ge(out_ready, b * CHUNKS + g + 3)
                    sp.dma_start(y_v[bass.ds(b, 1), :, 4 * g:4 * g + 4].rearrange("b p t c -> p (b t) c"), res[:, 4 * g:4 * g + 4, :]).then_inc(y_stored, 16)
            sp.wait_ge(y_stored, 16 * CHUNKS * B + 16)

        @block.gpsimd
        def _(pool):
            pool.memset(eps[:, :], EPS).then_inc(eps_ready, 1)
            pool.sem_inc(res_ready, 1)
            pool.sem_inc(y_stored, 16)
            pool.wait_ge(const_in, 80)
            with pool.Fori(0, B) as b:
                pool.wait_ge(h_in_sem, b * 64 + 64)
                pool.wait_ge(y_stored, b * (16 * CHUNKS) + 16)
                pool.tensor_tensor(res[:, :, :], h_tok[:, :, :], row[:, :, :].to_broadcast([P, TILES, C]), ALU.add).then_inc(res_ready, 1)

        @block.tensor
        def _(pe):
            pe.wait_ge(const_in, 80)
            with pe.Fori(0, B) as b:
                pe.wait_ge(normed, b * TILES + TILES + 1)

                def turn(g):
                    pe.wait_ge(n_ready, b * CHUNKS + g + 1)
                    for m in range(4):
                        mm = pe.transpose(turn_ps[g % 2][:, m * P:(m + 1) * P], n_tok[:, 4 * g + m, :], ident[:, :])
                    mm.then_inc(turned, 1)

                def up(g):
                    pe.wait_ge(n_ready, b * CHUNKS + g + 3)
                    for f in range(F):
                        i = g * F + f
                        pe.wait_ge(hid_ready, b * (CHUNKS * F) + i + 1)
                        pe.matmul(hid_ps[i % 3][:, :], fc1_w[:, f * P:(f + 1) * P], n_ch[:, g * CHUNK:(g + 1) * CHUNK],
                                  start=True, stop=True).then_inc(hid_made, 1)

                def down(g):
                    pe.wait_ge(hid_ready, b * (CHUNKS * F) + (g + 1) * F + 3)
                    pe.wait_ge(out_ready, b * CHUNKS + g + 1)
                    for m in range(4):
                        for f in range(F):
                            mm = pe.matmul(out_ps[g % 2][:, m * P:(m + 1) * P], hidden[:, g % 2, f, m * P:(m + 1) * P], fc2_w[:, f, :],
                                           start=(f == 0), stop=(f == F - 1))
                    mm.then_inc(out_made, 1)

                for g in range(CHUNKS):
                    turn(g)
                up(0)
                for g in range(CHUNKS):
                    if g + 1 < CHUNKS:
                        up(g + 1)
                    down(g)

        @block.scalar
        def _(act):
            act.sem_inc(n_ready, 2)
            act.sem_inc(hid_ready, 3)
            act.wait_ge(eps_ready, 1)
            act.wait_ge(const_in, 80)
            with act.Fori(0, B) as b:
                act.wait_ge(aggr_ready, b * TILES + TILES)
                act.activation(std[:, :], mean_var[:, :, 1], ACT.Sqrt, bias=eps[:, 0:1]).then_inc(std_ready, 1)
                for g in range(CHUNKS):
                    act.wait_ge(turned, b * CHUNKS + g + 1)
                    act.activation(n_ch[:, g * CHUNK:(g + 1) * CHUNK], turn_ps[g % 2][:, :], ACT.Identity,
                                   scale=col[:, 0:1], bias=col[:, 1:2]).then_inc(n_ready, 1)
                for i in range(CHUNKS * F):
                    g, f = divmod(i, F)
                    act.wait_ge(hid_made, b * (CHUNKS * F) + i + 1)
                    if f == 0 and g >= 2:
                        act.wait_ge(out_made, b * CHUNKS + g - 1)
                    act.activation(hidden[:, g % 2, f, :], hid_ps[i % 3][:, :], ACT.Gelu, bias=col[:, 2 + f:3 + f]).then_inc(hid_ready, 1)

        @block.vector
        def _(dve):
            dve.sem_inc(normed, 1)
            dve.sem_inc(out_ready, 2)
            with dve.Fori(0, B) as b:
                dve.wait_ge(h_in_sem, b * 64 + 64)
                for t in range(TILES):
                    dve.bn_stats(stats[:, t, :], h_tok[:, t, :]).then_inc(stats_ready, 1)
                dve.wait_ge(stats_ready, b * TILES + TILES)
                dve.sem_inc(waited, 1)
                for t in range(TILES):
                    dve.bn_aggr(mean_var[:, t, :], stats[:, t, :]).then_inc(aggr_ready, 1)
                dve.wait_ge(std_ready, b + 1)
                dve.reciprocal(std[:, :], std[:, :]).then_inc(inv_ready, 1)
                dve.wait_ge(inv_ready, b + 1)
                for t in range(TILES):
                    dve.tensor_scalar(n_tok[:, t, :], h_tok[:, t, :], mean_var[:, t, 0:1], std[:, t:t + 1],
                                      ALU.subtract, ALU.mult).then_inc(normed, 1)
                dve.wait_ge(res_ready, b + 2)
                for g in range(CHUNKS):
                    dve.wait_ge(out_made, b * CHUNKS + g + 1)
                    r = res[:, 4 * g:4 * g + 4, :].rearrange("p t c -> p (t c)")
                    dve.tensor_tensor(r, r, out_ps[g % 2][:, :], ALU.add).then_inc(out_ready, 1)


def gated_conv_attention(nc, x, y, w_in, ident_in):
    PW = HW + 2
    ROWS = CHUNK // HW
    PER = CHUNK // P
    DV = 16
    VE = DV + 1
    SCALE4 = 0.25
    MX = CHUNKS + 1
    FLOOR = -1e10 / SCALE4
    RING = 6
    LEAD = 6
    GROUPS = [(0, 24), (24, TILES)]
    HEAD_TAPS, SLOTS = 6, 15
    TAPS = 9
    CONSTS = 13
    with ExitStack() as ctx:
        mem = Memory(nc, ctx, "l3")
        x_tok = mem.sb("x_tok", [P, 4, PER, C])
        elu_high = mem.sb("elu_high", [P, PW, PW], F32R)
        elu_low = mem.sb("elu_low", [P, PW, PW], F32R)
        conv_high = mem.sb("conv_high", [P, PW, PW], F32R)
        conv_low = mem.sb("conv_low", [P, PW, PW], F32R)
        conv_out = mem.sb("conv_out", [P, 2, CHUNK])
        c3 = mem.sb("c3", [P, N])
        qk = mem.sb("qk", [P, 2, CHUNK])
        part = mem.sb("part", [P, 2, CHUNK], BF16)
        q_stack = mem.sb("q_stack", [P, N], BF16)
        k_stack = mem.sb("k_stack", [P, N], BF16)
        v_sum = mem.sb("v_sum", [P, TILES, DV])
        v_ext = mem.sb("v_ext", [P, TILES, 2 * VE], F32R)
        exps = mem.sb("exps", [P, RING, CHUNK])
        exps_high = mem.sb("exps_high", [P, RING, CHUNK], F32R)
        exps_low = mem.sb("exps_low", [P, RING, CHUNK], F32R)
        low = exps[:, 0:3, :]
        gate = exps[:, 3:5, :]
        sum_sb = mem.sb("sum_sb", [P, 2, CHUNK])
        out_tok = mem.sb("out_tok", [P, 2, PER, C])
        maxima = mem.sb("maxima", [P, TILES, MX])
        neg_max = mem.sb("neg_max", [P, TILES])
        max_row = mem.sb("max_row", [TILES, 2, P])
        max_parts = mem.sb("max_parts", [TILES, 2, 3, P], BF16)
        inverse = mem.sb("inverse", [P, 2, PER])
        w_high = mem.sb("w_high", [P, 3 * TAPS * C], F32R)
        w_low = mem.sb("w_low", [P, 3 * TAPS * C], F32R)
        w_q = mem.sb("w_q", [P, P])
        w_k = mem.sb("w_k", [P, P])
        w_v = mem.sb("w_v", [P, DV])
        w3 = mem.sb("w3", [P, C])
        w3_sum = mem.sb("w3_sum", [P, C])
        pick = mem.sb("pick", [P, P])
        sum_col = mem.sb("sum_col", [P, 1])
        col = mem.sb("col", [P, 9])
        v_bias = mem.sb("v_bias", [P, 1, DV])
        b3_row = mem.sb("b3_row", [P, 1, C])
        ident = mem.sb("ident", [P, P])
        tri = mem.sb("tri", [P, 2, P])
        ident_bf = mem.sb("ident_bf", [P, P], BF16)
        tri_bf = mem.sb("tri_bf", [P, 2, P], BF16)
        w_stage = c3[:, 0:3 * TAPS * C]
        work_ps = [mem.ps(f"work{i}", [P, CHUNK]) for i in range(3)]
        score_ps = [mem.ps(f"score{i}", [P, CHUNK]) for i in range(3)]
        sum_ps = [mem.ps(f"sum{i}", [P, CHUNK]) for i in range(2)]

        const_in, const_ready, pads_ready = mem.sem("const_in"), mem.sem("const_ready"), mem.sem("pads_ready")
        x_in = [mem.sem(f"x_in{i}") for i in range(4)]
        res_in, y_stored = [mem.sem(f"res_in{i}") for i in range(2)], [mem.sem(f"y_stored{i}") for i in range(2)]
        work_made, act_copied, dve_copied = mem.sem("work_made"), mem.sem("act_copied"), mem.sem("dve_copied")
        low_ready, low_exp, low_less = mem.sem("low_ready"), mem.sem("low_exp"), mem.sem("low_less")
        elu_high_ready, elu_ready = mem.sem("elu_high_ready"), mem.sem("elu_ready")
        conv_high_ready, conv_ready = mem.sem("conv_high_ready"), mem.sem("conv_ready")
        part_ready, rest_ready, stacked = mem.sem("part_ready"), mem.sem("rest_ready"), mem.sem("stacked")
        v_made, v_step, v_ready = mem.sem("v_made"), mem.sem("v_step"), mem.sem("v_ready")
        first_made, first_used = mem.sem("first_made"), mem.sem("first_used")
        maxima_cleared, max_step = mem.sem("maxima_cleared"), mem.sem("max_step")
        max_stacked = [mem.sem(f"max_stacked{i}") for i in range(2)]
        score_made, exp_ready = mem.sem("score_made"), mem.sem("exp_ready")
        high_ready = {e: mem.sem(f"{e}_high_ready") for e in ("dve", "act")}
        low_halves = {e: mem.sem(f"{e}_low_ready") for e in ("dve", "pool")}
        summed, sum_copied = mem.sem("summed"), mem.sem("sum_copied")
        w3_made, w3_ready = mem.sem("w3_made"), mem.sem("w3_ready")
        res_ready, inverse_step, out_step, out_ready = mem.sem("res_ready"), mem.sem("inverse_step"), mem.sem("out_step"), mem.sem("out_ready")
        waited, pool_waited = mem.sem("waited"), mem.sem("pool_waited")
        block = ctx.enter_context(nc.Block())

        x_v = x.rearrange("b (t p) c -> b p t c", p=P)
        y_v = y.rearrange("b (t p) c -> b p t c", p=P)

        SECOND = [(c, m) for c in range(CHUNKS) for m in range(PER * c + PER)]
        starts = [SECOND.index((c, 0)) for c in range(1, CHUNKS)]
        TAKE_AT, MIX_AT, OUTPUT_AT = ([s + d for s in starts] for d in (5, 6, 12))
        FIRST, first_of = [], []
        for c in range(CHUNKS):
            entries = [(t, k) for t in range(PER * c, PER * c + PER) for k in range(c + 1)]
            if c >= CHUNKS - 2:
                entries.append(("maxima", c - (CHUNKS - 2)))
            first_of.append([len(FIRST) + e for e in range(len(entries))])
            FIRST += entries

        def head(c):
            return first_of[c][:len(first_of[c]) * HEAD_TAPS // SLOTS]

        def tail(c):
            return first_of[c][len(first_of[c]) * HEAD_TAPS // SLOTS:]

        def share(entries, k, n):
            return entries[len(entries) * k // n:len(entries) * (k + 1) // n]

        begun = [("x", 0), ("x", 1), ("x", 2)]
        for g in range(CHUNKS):
            begun += [("conv1", g)] + ([("x", g + 3)] if g + 3 < CHUNKS else [])
        finished = list(begun)
        for g in range(CHUNKS):
            projected = [("q", g - 1), ("k", g - 1)] if g > 0 else []
            begun += [("gate", g)] + projected + [("a", g)]
            finished += projected + [("gate", g), ("a", g)]
        rest = [("q", CHUNKS - 1), ("k", CHUNKS - 1)]
        for c in range(CHUNKS):
            rest += [("values", c), ("sums", c), ("skip", c)]
        begun += rest
        finished += rest
        owner = lambda use: "act" if use[0] in ("conv1", "gate", "q", "k") else "dve"
        copies = {e: [use for use in finished if owner(use) == e] for e in ("act", "dve")}

        def bank_of(use):
            return work_ps[begun.index(use) % 3]

        def made(eng, b, use):
            eng.wait_ge(work_made, b * len(finished) + finished.index(use) + 1)

        def copied(eng, b, use):
            e = owner(use)
            eng.wait_ge(act_copied if e == "act" else dve_copied, b * len(copies[e]) + copies[e].index(use) + 2)

        high_maker = ["dve", "dve", "act"]
        low_maker = ["dve", "pool", "dve"]

        def wait_half(eng, b, sems, maker, i):
            mine = [k for k in range(len(SECOND)) if maker[k % 3] == maker[i % 3]]
            eng.wait_ge(sems[maker[i % 3]], b * len(mine) + mine.index(i) + 1)

        def high_made(eng, b, i):
            wait_half(eng, b, high_ready, high_maker, i)

        def low_made(eng, b, i):
            wait_half(eng, b, low_halves, low_maker, i)

        def halves(i):
            c, m = SECOND[i]
            return [t[:, i % RING, max(0, m - PER * c) * P:CHUNK] for t in (exps, exps_high, exps_low)]

        def high_half(eng, name, b, i):
            if high_maker[i % 3] != name:
                return
            full, high, _ = halves(i)
            eng.wait_ge(exp_ready, b * len(SECOND) + i + 4)
            if i >= RING:
                eng.wait_ge(summed, b * len(SECOND) + i - RING + 1)
            copy = eng.tensor_copy(high, full) if name == "dve" else eng.activation(high, full, ACT.Copy)
            copy.then_inc(high_ready[name], 1)

        def low_half(eng, name, b, i):
            if low_maker[i % 3] != name:
                return
            full, high, low_out = halves(i)
            high_made(eng, b, i)
            eng.tensor_tensor(low_out, full, high.bitcast(F32), ALU.subtract).then_inc(low_halves[name], 1)

        @block.sync
        def _(sp):
            for dst, src in ((w_stage[:, 0:TAPS * C].rearrange("p (t c) -> p t c", c=C), w_in["w1"].rearrange("t p c -> p t c")),
                             (w_stage[:, TAPS * C:].rearrange("p (t c) -> p t c", c=2 * C), w_in["w2"].rearrange("t p c -> p t c")),
                             (w_q[:, :], w_in["w_q"]), (w_k[:, :], w_in["w_k"]), (w_v[:, :], w_in["w_v"]), (w3[:, :], w_in["w3"]),
                             (pick[:, :], w_in["pick"]), (sum_col[:, :], w_in["sum_col"]), (col[:, :], w_in["cols"]),
                             (v_bias[:, :, :], w_in["v_bias"]), (b3_row[:, :, :], w_in["b3_row"]), (ident[:, :], ident_in),
                             (tri[:, :, :], w_in["tri"])):
                sp.dma_start(dst, src).then_inc(const_in, 16)
            with sp.Fori(0, B) as b:
                def load_residual(c):
                    sp.wait_ge(y_stored[c % 2], b * 64 + 16 * (c // 2) + 16)
                    sp.sem_inc(waited, 1)
                    sp.dma_start(out_tok[:, c % 2, :, :], x_v[bass.ds(b, 1), :, PER * c:PER * c + PER].rearrange("b p t c -> p (b t) c")).then_inc(res_in[c % 2], 16)

                load_residual(0)
                load_residual(1)
                for k, (first, end) in enumerate(GROUPS):
                    sp.wait_ge(max_step, b * 12 + 6 * k + 6)
                    sp.sem_inc(waited, 1)
                    for r in range(3):
                        sp.dma_start(q_stack[32 + r:33 + r, first * P:end * P], max_parts[0:end - first, k, r, :]).then_inc(max_stacked[k], 16)
                for c in range(CHUNKS):
                    sp.wait_ge(out_ready, b * CHUNKS + c + 1)
                    sp.sem_inc(waited, 1)
                    sp.dma_start(y_v[bass.ds(b, 1), :, PER * c:PER * c + PER].rearrange("b p t c -> p (b t) c"), out_tok[:, c % 2, :, :]).then_inc(y_stored[c % 2], 16)
                    if c + 2 < CHUNKS:
                        load_residual(c + 2)
            for k in range(2):
                sp.wait_ge(y_stored[k], 64 * B + 16)

        @block.gpsimd
        def _(pool):
            for k in range(2):
                pool.sem_inc(y_stored[k], 16)
            pads = (elu_high[:, :, :], elu_low[:, :, :], conv_high[:, :, :], conv_low[:, :, :], v_ext[:, :, :], sum_sb[:, :, :])
            for t in pads:
                pool.memset(t.bitcast(F32), 0.0).then_inc(pads_ready, 1)
            pool.wait_ge(pads_ready, len(pads))
            pool.memset(v_ext[:, :, DV:VE].bitcast(F32), 1.0).then_inc(pads_ready, 1)
            with pool.Fori(0, B) as b:
                for g in range(CHUNKS):
                    pool.wait_ge(low_exp, b * CHUNKS + g + 1)
                    pool.sem_inc(pool_waited, 1)
                    pool.tensor_scalar(low[:, g % 3, :], low[:, g % 3, :], -1.0, None, ALU.add).then_inc(low_less, 1)
                def residual(c):
                    pool.wait_ge(res_in[c % 2], b * 64 + 16 * (c // 2) + 16)
                    pool.tensor_tensor(out_tok[:, c % 2, :, :], out_tok[:, c % 2, :, :], b3_row[:, :, :].to_broadcast([P, PER, C]),
                                       ALU.add).then_inc(res_ready, 1)

                residual(0)
                residual(1)
                for i, (c, m) in enumerate(SECOND):
                    low_half(pool, "pool", b, i)
                    if c > 2 and m == 4:
                        residual(c - 1)
                residual(CHUNKS - 1)

        @block.tensor
        def _(pe):
            pe.wait_ge(const_in, 16 * CONSTS)
            pe.wait_ge(pads_ready, 7)
            pe.wait_ge(const_ready, 4)
            pe.matmul(sum_ps[0][:, 0:C], pick[:, :], w3[:, :], start=True, stop=True).then_inc(w3_made, 1)
            pe.wait_ge(w3_ready, 1)
            with pe.Fori(0, B) as b:
                def begin(use):
                    u = begun.index(use)
                    if u >= 3:
                        copied(pe, b, begun[u - 3])
                    return work_ps[u % 3]

                def turn(g):
                    ps = begin(("x", g))
                    pe.wait_ge(x_in[g % 4], b * 32 + 16 * (g // 4) + 16)
                    for m in range(PER):
                        mm = pe.transpose(ps[:, m * P:(m + 1) * P], x_tok[:, g % 4, m, :], ident[:, :])
                    mm.then_inc(work_made, 1)

                def convolve(ps, high, low, weight, g):
                    for t in range(TAPS):
                        dy, dx = divmod(t, 3)
                        w = slice(weight(t), weight(t) + C)
                        rows, cols = slice(ROWS * g + dy, ROWS * g + dy + ROWS), slice(dx, dx + HW)
                        mm = split_product(pe, ps[:, :], (w_high[:, w], w_low[:, w]), (high[:, rows, cols], low[:, rows, cols]),
                                           t == 0, t == TAPS - 1)
                        if t == TAPS - 1:
                            mm.then_inc(work_made, 1)
                        yield t

                def project(g):
                    for name, w in (("q", w_q), ("k", w_k)):
                        ps = begin((name, g))
                        copied(pe, b, ("a", g))
                        pe.matmul(ps[:, :], w[:, :], c3[:, g * CHUNK:(g + 1) * CHUNK], start=True, stop=True).then_inc(work_made, 1)

                def first(i):
                    t, c = FIRST[i]
                    pe.wait_ge(first_used, b * len(FIRST) + i + 1)
                    ps = score_ps[i % 3]
                    if t == "maxima":
                        start, end = GROUPS[c]
                        pe.wait_ge(max_step, b * 12 + 6 * c + 1)
                        pe.transpose(ps[0:end - start, 0:P], neg_max[:, start:end], ident[:, :]).then_inc(first_made, 1)
                        return
                    pe.wait_ge(stacked, b * CHUNKS + t // PER + 1)
                    wide = min(CHUNK, (t + 1) * P - c * CHUNK)
                    last = c == t // PER
                    mm = pe.matmul(ps[:, 0:wide], q_stack[:, t * P:(t + 1) * P], k_stack[:, c * CHUNK:c * CHUNK + wide],
                                   start=True, stop=not last)
                    if last:
                        mm = pe.matmul(ps[:, wide - P:wide], ident_bf[:, :], tri_bf[:, 0, :], start=False, stop=True)
                    mm.then_inc(first_made, 1)

                pe.wait_ge(dve_copied, b * len(copies["dve"]) + 1)
                for g in range(3):
                    turn(g)
                for g in range(CHUNKS):
                    ps = begin(("conv1", g))
                    pe.wait_ge(elu_ready, b * CHUNKS + min(g + 2, CHUNKS))
                    for t in convolve(ps, elu_high, elu_low, lambda t: t * C, g):
                        pass
                    if g + 3 < CHUNKS:
                        turn(g + 3)
                for g in range(CHUNKS):
                    ps = begin(("gate", g))
                    pe.wait_ge(conv_ready, b * CHUNKS + min(g + 2, CHUNKS) + 2)
                    for t in convolve(ps, conv_high, conv_low, lambda t: TAPS * C + 2 * C * t + C, g):
                        if t == 0 and g > 0:
                            project(g - 1)
                        if g > 1:
                            for i in share(tail(g - 2), t, TAPS):
                                first(i)
                    ps = begin(("a", g))
                    for t in convolve(ps, conv_high, conv_low, lambda t: TAPS * C + 2 * C * t, g):
                        if g > 0 and t >= TAPS - HEAD_TAPS:
                            for i in share(head(g - 1), t - (TAPS - HEAD_TAPS), HEAD_TAPS):
                                first(i)
                project(CHUNKS - 1)
                pe.wait_ge(sum_copied, b * CHUNKS + 2)
                for t in range(TILES):
                    mm = pe.matmul(sum_ps[1][:, DV * t:DV * t + DV], c3[:, t * P:(t + 1) * P], w_v[:, :], start=True, stop=True)
                mm.then_inc(v_made, 1)
                for i in tail(CHUNKS - 2):
                    first(i)
                for i in first_of[CHUNKS - 1]:
                    first(i)
                pe.wait_ge(first_used, (b + 1) * len(FIRST) + 3)
                pe.wait_ge(v_ready, b + 1)

                def scores(i):
                    c, m = SECOND[i]
                    if m == 0 and PER * c in (GROUPS[0][0], GROUPS[1][0]):
                        k = 0 if c == 0 else 1
                        pe.wait_ge(max_stacked[k], b * 48 + 48)
                    pe.wait_ge(exp_ready, b * len(SECOND) + i + 1)
                    ps = score_ps[i % 3]
                    skip = max(0, m - PER * c) * P
                    diagonal = m >= PER * c
                    mm = pe.matmul(ps[:, skip:CHUNK], k_stack[:, m * P:(m + 1) * P], q_stack[:, c * CHUNK + skip:(c + 1) * CHUNK],
                                   start=True, stop=not diagonal)
                    if diagonal:
                        mm = pe.matmul(ps[:, skip:skip + P], ident_bf[:, :], tri_bf[:, 1, :], start=False, stop=True)
                    mm.then_inc(score_made, 1)

                def values(i):
                    c, m = SECOND[i]
                    low_made(pe, b, i)
                    if m == 0:
                        pe.wait_ge(sum_copied, b * CHUNKS + c + 1)
                    skip = max(0, m - PER * c) * P
                    out = sum_ps[c % 2][0:2 * VE, skip:CHUNK]
                    pe.matmul(out, v_ext[:, m, :], exps_low[:, i % RING, skip:CHUNK], start=(m == 0), stop=False, skip_group_check=True)
                    pe.matmul(out, v_ext[:, m, :], exps_high[:, i % RING, skip:CHUNK], start=False, stop=(m == PER * c + 3),
                              skip_group_check=True).then_inc(summed, 1)

                def mix(c):
                    pe.wait_ge(sum_copied, b * CHUNKS + c + 3)
                    tiles = [slice(m * P, (m + 1) * P) for m in range(PER)]
                    ps = begin(("values", c))
                    for m in range(PER):
                        mm = pe.matmul(ps[:, tiles[m]], sum_sb[:, c % 2, tiles[m]], w3_sum[:, :], start=True, stop=True)
                    mm.then_inc(work_made, 1)
                    ps = begin(("sums", c))
                    for m in range(PER):
                        mm = pe.matmul(ps[:, m:m + 1], sum_sb[:, c % 2, tiles[m]], sum_col[:, :], start=True, stop=True)
                    mm.then_inc(work_made, 1)
                    ps = begin(("skip", c))
                    for m in range(PER):
                        t = PER * c + m
                        mm = pe.transpose(ps[:, tiles[m]], c3[:, t * P:(t + 1) * P], ident[:, :])
                    mm.then_inc(work_made, 1)

                for i in range(LEAD):
                    scores(i)
                for i, (c, m) in enumerate(SECOND):
                    values(i)
                    if i + LEAD < len(SECOND):
                        scores(i + LEAD)
                    if i in MIX_AT:
                        mix(MIX_AT.index(i))
                mix(CHUNKS - 1)

        @block.scalar
        def _(act):
            act.sem_inc(act_copied, 1)
            act.sem_inc(exp_ready, 3)
            act.wait_ge(const_in, 16 * CONSTS)
            act.wait_ge(pads_ready, 7)
            with act.Fori(0, B) as b:
                def load(g):
                    act.dma_start(x_tok[:, g % 4, :, :], x_v[bass.ds(b, 1), :, PER * g:PER * g + PER].rearrange("b p t c -> p (b t) c")).then_inc(x_in[g % 4], 16)

                def exp_low(g):
                    act.wait_ge(low_ready, b * CHUNKS + g + 1)
                    act.activation(low[:, g % 3, :], low[:, g % 3, :], ACT.Exp).then_inc(low_exp, 1)
                    if g + 4 < CHUNKS:
                        load(g + 4)

                def stack(g):
                    for n, name in enumerate("qk"):
                        made(act, b, (name, g))
                        act.activation(qk[:, n, :], bank_of((name, g))[:, :], ACT.Identity, bias=col[:, 3 + n:4 + n]).then_inc(act_copied, 1)
                    for step in range(2):
                        for n in range(2):
                            if step == 0:
                                copied(act, b, ("qk"[n], g))
                            else:
                                act.wait_ge(rest_ready, b * (4 * CHUNKS) + 4 * g + n + 1)
                            act.activation(part[:, n, :], qk[:, n, :], ACT.Copy).then_inc(part_ready, 1)
                    cols = slice(g * CHUNK, (g + 1) * CHUNK)
                    act.wait_ge(rest_ready, b * (4 * CHUNKS) + 4 * g + 4)
                    act.activation(q_stack[:, cols], qk[:, 0, :], ACT.Copy)
                    act.activation(k_stack[:, cols], qk[:, 1, :], ACT.Copy).then_inc(stacked, 1)

                for g in range(4):
                    load(g)
                for g in range(3):
                    exp_low(g)
                for g in range(CHUNKS):
                    made(act, b, ("conv1", g))
                    act.wait_ge(conv_ready, b * CHUNKS + g + 1)
                    act.activation(conv_out[:, g % 2, :], bank_of(("conv1", g))[:, :], ACT.Identity, bias=col[:, 0:1]).then_inc(act_copied, 1)
                    copied(act, b, ("conv1", g))
                    act.activation(conv_high[:, 1 + ROWS * g:1 + ROWS * g + ROWS, 1:1 + HW],
                                   conv_out[:, g % 2, :].rearrange("p (y x) -> p y x", x=HW), ACT.Copy).then_inc(conv_high_ready, 1)
                    if g + 3 < CHUNKS:
                        exp_low(g + 3)
                for g in range(CHUNKS):
                    if g > 0:
                        stack(g - 1)
                    made(act, b, ("gate", g))
                    if g >= 2:
                        copied(act, b, ("a", g - 2))
                    act.activation(gate[:, g % 2, :], bank_of(("gate", g))[:, :], ACT.Sigmoid, bias=col[:, 2:3]).then_inc(act_copied, 1)
                stack(CHUNKS - 1)
                for i, (c, m) in enumerate(SECOND):
                    skip = max(0, m - PER * c) * P
                    act.wait_ge(score_made, b * len(SECOND) + i + 1)
                    if i >= RING:
                        low_made(act, b, i - RING)
                    act.activation(halves(i)[0], score_ps[i % 3][:, skip:CHUNK], ACT.Exp, scale=SCALE4).then_inc(exp_ready, 1)
                    if i > 0:
                        high_half(act, "act", b, i - 1)
                high_half(act, "act", b, len(SECOND) - 1)

        @block.vector
        def _(dve):
            dve.sem_inc(dve_copied, 1)
            dve.sem_inc(conv_ready, 2)
            dve.sem_inc(first_used, 3)
            dve.sem_inc(sum_copied, 2)
            dve.wait_ge(const_in, 16 * CONSTS)
            dve.tensor_copy(ident_bf[:, :], ident[:, :]).then_inc(const_ready, 1)
            dve.tensor_copy(tri_bf[:, :, :], tri[:, :, :]).then_inc(const_ready, 1)
            dve.tensor_copy(w_high[:, :], w_stage).then_inc(const_ready, 1)
            dve.wait_ge(const_ready, 3)
            dve.tensor_tensor(w_low[:, :], w_stage, w_high[:, :].bitcast(F32), ALU.subtract).then_inc(const_ready, 1)
            dve.wait_ge(w3_made, 1)
            dve.tensor_copy(w3_sum[:, :], sum_ps[0][:, 0:C]).then_inc(w3_ready, 1)
            dve.wait_ge(pads_ready, 7)
            with dve.Fori(0, B) as b:
                def low_part(g):
                    made(dve, b, ("x", g))
                    dve.tensor_scalar(low[:, g % 3, :], bank_of(("x", g))[:, :], 0.0, None, ALU.min).then_inc(low_ready, 1)

                def elu(g):
                    rows = slice(1 + ROWS * g, 1 + ROWS * g + ROWS)
                    image = low[:, g % 3, :].rearrange("p (y x) -> p y x", x=HW)
                    dve.wait_ge(low_less, b * CHUNKS + g + 1)
                    dve.sem_inc(waited, 1)
                    dve.scalar_tensor_tensor(low[:, g % 3, :], bank_of(("x", g))[:, :], 0.0, low[:, g % 3, :],
                                             ALU.max, ALU.add).then_inc(dve_copied, 1)
                    copied(dve, b, ("x", g))
                    dve.tensor_copy(elu_high[:, rows, 1:1 + HW], image).then_inc(elu_high_ready, 1)
                    dve.wait_ge(elu_high_ready, b * CHUNKS + g + 1)
                    dve.tensor_tensor(elu_low[:, rows, 1:1 + HW], image, elu_high[:, rows, 1:1 + HW].bitcast(F32),
                                      ALU.subtract).then_inc(elu_ready, 1)

                def maximum(i):
                    t, c = FIRST[i]
                    ps = score_ps[i % 3]
                    dve.wait_ge(first_made, b * len(FIRST) + i + 1)
                    if t != "maxima":
                        wide = min(CHUNK, (t + 1) * P - c * CHUNK)
                        dve.tensor_reduce(maxima[:, t, c:c + 1], ps[:, 0:wide], AX.X, ALU.max).then_inc(first_used, 1)
                        for k, (start, end) in enumerate(GROUPS):
                            if t == end - 1 and c == t // PER:
                                dve.wait_ge(first_used, b * len(FIRST) + i + 4)
                                dve.tensor_reduce(neg_max[:, start:end], maxima[:, start:end, :], AX.X, ALU.max,
                                                  negate=True).then_inc(max_step, 1)
                        return
                    rows = slice(0, GROUPS[c][1] - GROUPS[c][0])
                    dve.tensor_copy(max_row[rows, c, :], ps[rows, 0:P]).then_inc(first_used, 1)
                    dve.wait_ge(first_used, b * len(FIRST) + i + 4)
                    for k in range(3):
                        if k > 0:
                            dve.tensor_tensor(max_row[rows, c, :], max_row[rows, c, :], max_parts[rows, c, k - 1, :],
                                              ALU.subtract).then_inc(max_step, 1)
                            dve.wait_ge(max_step, b * 12 + 6 * c + 2 * k + 1)
                        dve.tensor_copy(max_parts[rows, c, k, :], max_row[rows, c, :]).then_inc(max_step, 1)
                        dve.wait_ge(max_step, b * 12 + 6 * c + 2 * k + 2)

                def subtract_parts(g, step):
                    for n in range(2):
                        dve.wait_ge(part_ready, b * (4 * CHUNKS) + 4 * g + 2 * step + n + 1)
                        dve.sem_inc(waited, 1)
                        dve.scalar_tensor_tensor(qk[:, n, :], part[:, n, :], col[:, 5 + 2 * n + step:6 + 2 * n + step], qk[:, n, :],
                                                 ALU.mult, ALU.add).then_inc(rest_ready, 1)

                def values_split():
                    dve.wait_ge(v_made, b + 1)
                    dve.tensor_tensor(v_sum[:, :, :], sum_ps[1][:, :].rearrange("p (t d) -> p t d", d=DV),
                                      v_bias[:, :, :].to_broadcast([P, TILES, DV]), ALU.add).then_inc(v_step, 1)
                    dve.wait_ge(v_step, b * 2 + 1)
                    dve.tensor_copy(v_ext[:, :, 0:DV], v_sum[:, :, :]).then_inc(v_step, 1)
                    dve.wait_ge(v_step, b * 2 + 2)
                    dve.tensor_tensor(v_ext[:, :, VE:VE + DV], v_sum[:, :, :], v_ext[:, :, 0:DV].bitcast(F32), ALU.subtract).then_inc(v_ready, 1)

                def first_tail(c, g):
                    for k in range(3):
                        if c >= 0:
                            for i in share(tail(c), k, 3):
                                maximum(i)
                        if k < 2:
                            subtract_parts(g, k)
                        if k == 1 and g == CHUNKS - 1:
                            values_split()

                low_part(0)
                low_part(1)
                elu(0)
                low_part(2)
                elu(1)
                dve.memset(maxima[:, :, :], FLOOR).then_inc(maxima_cleared, 1)
                dve.wait_ge(maxima_cleared, b + 1)
                for g in range(CHUNKS):
                    if g + 2 < CHUNKS:
                        elu(g + 2)
                    if g + 3 < CHUNKS:
                        low_part(g + 3)
                    rows = slice(1 + ROWS * g, 1 + ROWS * g + ROWS)
                    dve.wait_ge(conv_high_ready, b * CHUNKS + g + 1)
                    dve.tensor_tensor(conv_low[:, rows, 1:1 + HW], conv_out[:, g % 2, :].rearrange("p (y x) -> p y x", x=HW),
                                      conv_high[:, rows, 1:1 + HW].bitcast(F32), ALU.subtract).then_inc(conv_ready, 1)
                for g in range(CHUNKS):
                    if g > 0:
                        first_tail(g - 2, g - 1)
                        for i in head(g - 1):
                            maximum(i)
                    made(dve, b, ("a", g))
                    copied(dve, b, ("gate", g))
                    dve.sem_inc(waited, 1)
                    dve.scalar_tensor_tensor(c3[:, g * CHUNK:(g + 1) * CHUNK], bank_of(("a", g))[:, :], col[:, 1:2], gate[:, g % 2, :],
                                             ALU.add, ALU.mult).then_inc(dve_copied, 1)
                first_tail(CHUNKS - 2, CHUNKS - 1)
                for i in first_of[CHUNKS - 1]:
                    maximum(i)

                def take(c):
                    dve.wait_ge(summed, b * len(SECOND) + 2 * (c + 1) * (c + 2))
                    dve.tensor_copy(sum_sb[0:2 * VE, c % 2, :], sum_ps[c % 2][0:2 * VE, :]).then_inc(sum_copied, 1)

                def output(c):
                    s = c % 2
                    made(dve, b, ("sums", c))
                    dve.tensor_scalar(inverse[:, s, :], bank_of(("sums", c))[:, 0:PER], 1e-10, None, ALU.add).then_inc(inverse_step, 1)
                    dve.wait_ge(inverse_step, b * (2 * CHUNKS) + 2 * c + 1)
                    dve.reciprocal(inverse[:, s, :], inverse[:, s, :]).then_inc(inverse_step, 1)
                    dve.wait_ge(inverse_step, b * (2 * CHUNKS) + 2 * c + 2)
                    dve.wait_ge(res_ready, b * CHUNKS + c + 1)
                    dve.sem_inc(waited, 1)
                    for m in range(PER):
                        dve.scalar_tensor_tensor(out_tok[:, s, m, :], bank_of(("values", c))[:, m * P:(m + 1) * P], inverse[:, s, m:m + 1],
                                                 out_tok[:, s, m, :], ALU.mult, ALU.add).then_inc(out_step, 1)
                    dve.wait_ge(out_step, b * (PER * CHUNKS) + PER * c + PER)
                    dve.sem_inc(dve_copied, 2)
                    made(dve, b, ("skip", c))
                    out = out_tok[:, s, :, :].rearrange("p t c -> p (t c)")
                    dve.tensor_tensor(out, out, bank_of(("skip", c))[:, :], ALU.add).then_inc(dve_copied, 1)
                    copied(dve, b, ("skip", c))
                    dve.sem_inc(out_ready, 1)

                for i, (c, m) in enumerate(SECOND):
                    high_half(dve, "dve", b, i)
                    if i > 0:
                        low_half(dve, "dve", b, i - 1)
                    if i in TAKE_AT:
                        take(TAKE_AT.index(i))
                    if i in OUTPUT_AT:
                        output(OUTPUT_AT.index(i))
                low_half(dve, "dve", b, len(SECOND) - 1)
                take(CHUNKS - 1)
                output(CHUNKS - 1)


def program(nc, a, out):
    def scratch(name, shape):
        return nc.dram_tensor(name, shape, F32, kind="Internal").ap()

    y0, y1, h2, y2, v = (scratch(n, (B, N, C)) for n in ("l0_y", "l1_y", "l2_h", "l2_y", "l2_v"))
    flat = out.rearrange("b y x c -> b (y x) c")
    column_softmax_attention(nc, a["x"].rearrange("b y x c -> b (y x) c"), y0, a["l0_w_fg"], a["l0_w_h"], a["l0_gamma"], a["ident"])
    cosine_attention(nc, y0.rearrange("b (i j) c -> b i j c", j=HW), y1.rearrange("b (i j) c -> b i j c", j=HW), a["l1_gamma"], a["ident"])
    neighbourhood_attention(nc, y1, h2, v, a["l2a_w_qkv"], a["l2a_w_proj"], a["l2a_cols"], a["l2a_rows"], a["l2a_bias"], a["ident"])
    mlp(nc, h2, y2, a["l2b_w_fc1"], a["l2b_w_fc2"], a["l2b_cols"], a["l2b_row"], a["ident"])
    gated_conv_attention(nc, y2, flat, {n[3:]: a[n] for n in a if n.startswith("l3_")}, a["ident"])



def bias_layout(rpb):
    def axis(side, region):
        out = []
        last = HW // side - 1
        for k in (0, 1, last):
            q = k * side + np.arange(side)[:, None]
            key = region_start(k, side, region) + np.arange(region)[None, :]
            start = np.clip(q - WIN // 2, 0, HW - WIN)
            inside = (key >= start) & (key < start + WIN)
            out.append((np.where(inside, key - q + WIN - 1, 0), inside))
        return out
    ys, xs = axis(QY, RY), axis(QX, RX)
    out = np.full((QY * QX, 4, 9, RY * RX), MASKED, np.float32)
    for a, (ry, iny) in enumerate(ys):
        for c, (rx, inx) in enumerate(xs):
            inside = (iny[:, None, :, None] & inx[None, :, None, :]).reshape(QY * QX, RY * RX)
            iy = np.broadcast_to(ry[:, None, :, None], (QY, QX, RY, RX)).reshape(QY * QX, RY * RX)
            ix = np.broadcast_to(rx[None, :, None, :], (QY, QX, RY, RX)).reshape(QY * QX, RY * RX)
            for h in range(4):
                view = out[:, h, 3 * a + c, :]
                view[inside] = rpb[h][iy[inside], ix[inside]]
    return out

def l2a(I):
    k = lambda n: I['L2_conv_' + n]
    heads = np.zeros((128, 4), np.float32)
    for h in range(4): heads[32 * h:32 * h + 32, h] = 1
    cols = np.concatenate([k('ln1_g')[:, None], k('ln1_b')[:, None], k('qkv_b')[0:128, None], k('qkv_b')[128:256, None], heads], 1)
    rows = np.tile(np.stack([k('qkv_b')[256:384], k('proj_b')])[None], (128, 1, 1))
    return dict(w_qkv=k('qkv_w'), w_proj=k('proj_w'), cols=cols.astype(np.float32), rows=rows, bias=bias_layout(k('rpb')))

def l2b(I):
    k = lambda n: I['L2_conv_' + n]
    cols = np.concatenate([k('ln2_g')[:, None], k('ln2_b')[:, None], k('fc1_b').reshape(4, 128).T], 1)
    return dict(w_fc1=k('fc1_w'), w_fc2=k('fc2_w'), cols=np.ascontiguousarray(cols), row=np.tile(k('fc2_b')[None, None], (128, 1, 1)))

def l3(I):
    k = lambda n: I['L3_conv_' + n]
    C = 128
    rows = np.arange(C)
    groups = len(LEFT_PARTS)

    def spread(v):
        return np.concatenate([np.tile(v, (1, groups)), np.zeros((v.shape[0], C - groups * v.shape[1]), np.float32)], 1)

    def masks(parts):
        of_row = np.concatenate([np.repeat(parts, C // 8 // 4), np.zeros(C - len(parts) * (C // 8 // 4), int)])
        return [-(of_row >= 1).astype(np.float32), -(of_row >= 2).astype(np.float32)]

    q_bias, k_bias = spread(k('bq')[None])[0], spread(k('bk')[None])[0]
    k_bias[32:35] = 1
    pick = np.zeros((C, C), np.float32)
    for d in range(16):
        pick[d::16, d] = 1
        pick[d::16, 17 + d] = 1
    sum_col = np.zeros((C, 1), np.float32)
    sum_col[16] = 1
    tri = np.zeros((C, 2, C), np.float32)
    tri[:, 0][rows[None, :] >= rows[:, None]] = -1e30
    tri[:, 1][rows[:, None] >= rows[None, :]] = -1e30
    cols = np.stack([k('b1'), k('b2')[0:C], k('b2')[C:2 * C], q_bias, k_bias] + masks(LEFT_PARTS) + masks(RIGHT_PARTS), 1)
    return dict(w1=k('W1').reshape(9, C, C), w2=k('W2').reshape(9, C, 2 * C), w_q=spread(k('Wq')), w_k=spread(k('Wk')), w_v=k('Wv'), w3=k('W3'),
                pick=pick, sum_col=sum_col, cols=np.ascontiguousarray(cols), v_bias=np.tile(k('bv')[None, None], (C, 1, 1)),
                b3_row=np.tile(k('b3')[None, None], (C, 1, 1)), tri=tri)


def l0(I):
    k = lambda n: I["L0_conv_kernel_" + n][0, 0]
    return dict(w_fg=np.tile(np.concatenate([k("f"), k("g")], 1), (1, 4)), w_h=k("h"), gamma=np.tile(I["L0_conv_gamma"], (P, 1)))


def arrays_of(I):
    a = {"x": I["x"], "ident": np.eye(P, dtype=np.float32), "l1_gamma": np.tile(I["L1_conv_gamma"], (P, 1))}
    for stage, made in (("l0", l0(I)), ("l2a", l2a(I)), ("l2b", l2b(I)), ("l3", l3(I))):
        a.update({f"{stage}_{n}": v for n, v in made.items()})
    return {n: np.ascontiguousarray(v) for n, v in a.items()}


def kernel(**inputs):
    import concourse.bacc as _bacc
    from concourse.bass_utils import run_bass_kernel_spmd as _run

    nc = _bacc.Bacc("TRN2", target_bir_lowering=False, num_devices=1)
    arrays = arrays_of({n: np.asarray(v) for n, v in inputs.items()})
    aps = {n: nc.dram_tensor(f"in_{n}", v.shape, mybir.dt.from_np(v.dtype), kind="ExternalInput").ap() for n, v in arrays.items()}
    out = nc.dram_tensor("out_0", (B, HW, HW, C), F32, kind="ExternalOutput").ap()
    program(nc, aps, out)
    r = _run(nc, [{f"in_{n}": v for n, v in arrays.items()}], core_ids=[0])
    return r.results[0]["out_0"]
```

```python
from contextlib import ExitStack

import numpy as np
import concourse.bass as bass
from concourse import mybir

F32 = mybir.dt.float32
F32R = mybir.dt.float32r
BF16 = mybir.dt.bfloat16
ACT = mybir.ActivationFunctionType
ALU = mybir.AluOpType
AX = mybir.AxisListType

P = 128
B = 4
HW = 64
C = 128
N = HW * HW
TILES = N // P
CHUNK = 512
CHUNKS = N // CHUNK


class Memory:

    def __init__(self, nc, ctx, stage):
        self.nc, self.ctx, self.stage = nc, ctx, stage

    def sb(self, name, shape, dt=F32):
        return self.ctx.enter_context(self.nc.sbuf_tensor(f"{self.stage}_{name}", shape, dt))

    def ps(self, name, shape, dt=F32):
        return self.ctx.enter_context(self.nc.psum_tensor(f"{self.stage}_{name}", shape, dt))

    kept = []

    def waited(self):
        if not self.kept or self.kept[0] is not self.nc:
            self.kept[:] = [self.nc, self.nc.alloc_semaphore(name="waited")]
        return self.kept[1]

    def sem(self, name):
        return self.ctx.enter_context(self.nc.semaphore(f"{self.stage}_{name}"))


def split_product(pe, out, left, right, start, stop):
    pe.matmul(out, left[1], right[0], start=start, stop=False)
    pe.matmul(out, left[0], right[1], start=False, stop=False)
    return pe.matmul(out, left[0], right[0], start=False, stop=stop)


LEFT_PARTS = [0, 0, 1, 1, 0, 2, 1, 2]
RIGHT_PARTS = [0, 1, 0, 1, 2, 0, 2, 1]


def column_softmax_attention(nc, x, y, w_fg, w_h, masks, gamma, ident_in):
    RING = 6
    GROUP = 2
    LEAD = 2
    QUARTER = 1024
    QUARTERS = N // QUARTER
    PAIRS = TILES // GROUP
    with ExitStack() as ctx:
        mem = Memory(nc, ctx, "l0")
        x_tok = mem.sb("x_tok", [P, TILES, C])
        x_ch = mem.sb("x_ch", [P, N])
        h_tok = mem.sb("h_tok", [P, TILES, C])
        out_tok = mem.sb("out_tok", [P, TILES, C])
        value = x_ch
        f_stack = mem.sb("f_stack", [P, N], BF16)
        g_stack = mem.sb("g_stack", [P, N], BF16)
        exps = mem.sb("exps", [P, RING, N])
        fg = exps[:, RING - 1, 0:4 * CHUNK].rearrange("p (s n c) -> p s n c", s=2, n=2)
        part = exps[:, RING - 2, 0:2 * CHUNK].bitcast(BF16).rearrange("p (s n c) -> p s n c", s=2, n=2)
        h_scaled = mem.sb("h_scaled", [P, RING, C])
        quarter_max = mem.sb("quarter_max", [P, RING, QUARTERS])
        neg_max = mem.sb("neg_max", [P, RING])
        total = mem.sb("total", [P, RING])
        inverse = mem.sb("inverse", [P, RING])
        fg_w = mem.sb("fg_w", [P, 2, P])
        mask = mem.sb("mask", [P, 2, 2])
        h_w = mem.sb("h_w", [P, C])
        gamma_col = mem.sb("gamma_col", [P, 1])
        ident = mem.sb("ident", [P, P])
        score_ps = [mem.ps(f"score{i}", [P, QUARTER]) for i in range(2)]
        value_ps = [mem.ps(f"value{i}", [P, CHUNK]) for i in range(2)]
        work_ps = [mem.ps(f"work{i}", [P, CHUNK]) for i in range(2)]
        value_ps += work_ps

        const_in = mem.sem("const_in")
        x_in = [mem.sem(f"x_in{g}") for g in range(2)]
        x_stored = mem.sem("x_stored")
        x_turned, x_copied = mem.sem("x_turned"), mem.sem("x_copied")
        fg_made, fg_copied = mem.sem("fg_made"), mem.sem("fg_copied")
        h_made, h_copied = mem.sem("h_made"), mem.sem("h_copied")
        part_ready = [mem.sem(f"part_ready{k}") for k in range(2)]
        rest_ready = [mem.sem(f"rest_ready{k}") for k in range(2)]
        stacked = mem.sem("stacked")
        out_turned, out_step = mem.sem("out_turned"), mem.sem("out_step")
        waited = mem.waited()
        scored = mem.sem("scored")
        score_copied = mem.sem("score_copied")
        neg_ready = mem.sem("neg_ready")
        exp_ready = mem.sem("exp_ready")
        inverse_ready = mem.sem("inverse_ready")
        h_scaled_ready = mem.sem("h_scaled_ready")
        value_made = mem.sem("value_made")
        value_added = mem.sem("value_added")
        out_ready = mem.sem("out_ready")
        block = ctx.enter_context(nc.Block())

        x_v = x.rearrange("b (t p) c -> b p t c", p=P)
        y_v = y.rearrange("b (t p) c -> b p t c", p=P)

        @block.sync
        def _(sp):
            for dst, src in ((fg_w[:, :, :], w_fg), (h_w[:, :], w_h), (mask[:, :, :], masks), (gamma_col[:, :], gamma), (ident[:, :], ident_in)):
                sp.dma_start(dst, src).then_inc(const_in, 16)
            with sp.Fori(0, B) as b:
                for g in range(CHUNKS):
                    sp.wait_ge(out_ready, b * CHUNKS + CHUNKS + g + 1)
                    sp.sem_inc(waited, 1)
                    sp.dma_start(y_v[bass.ds(b, 1), :, 4 * g:4 * g + 4].rearrange("b p t c -> p (b t) c"), out_tok[:, 4 * g:4 * g + 4, :]).then_inc(x_stored, 16)
            sp.wait_ge(x_stored, 16 * CHUNKS * B + 16)

        @block.tensor
        def _(pe):
            pe.wait_ge(const_in, 80)

            def scores(b, t):
                for q in range(QUARTERS):
                    i = t * QUARTERS + q
                    pe.wait_ge(score_copied, b * (TILES * QUARTERS) + i + 1)
                    for half in range(QUARTER // CHUNK):
                        a = q * QUARTER + half * CHUNK
                        mm = pe.matmul(score_ps[i % 2][:, half * CHUNK:(half + 1) * CHUNK],
                                       f_stack[:, t * P:(t + 1) * P], g_stack[:, a:a + CHUNK], start=True, stop=True)
                    mm.then_inc(scored, 1)
                    yield

            def values(b, pair):
                pe.wait_ge(exp_ready, b * TILES + GROUP * (pair + 1))
                pe.wait_ge(h_scaled_ready, b * TILES + GROUP * (pair + 1))
                for c in range(CHUNKS):
                    i = pair * CHUNKS + c
                    pe.wait_ge(value_added, b * (PAIRS * CHUNKS) + i + 1)
                    for k in range(GROUP):
                        slot = (GROUP * pair + k) % RING
                        mm = pe.matmul(value_ps[i % 4][:, :], h_scaled[:, slot, :],
                                       exps[:, slot, c * CHUNK:(c + 1) * CHUNK], start=(k == 0), stop=(k == GROUP - 1))
                    mm.then_inc(value_made, 1)
                    yield

            with pe.Fori(0, B) as b:
                def turn(g):
                    pe.wait_ge(x_in[g // 4], b * 64 + 64)
                    if g > 0:
                        pe.wait_ge(x_copied, b * CHUNKS + g)
                    for k in range(4):
                        mm = pe.transpose(work_ps[0][:, k * P:(k + 1) * P], x_tok[:, 4 * g + k, :], ident[:, :])
                    mm.then_inc(x_turned, 1)

                pe.wait_ge(out_step, b * CHUNKS + 2)
                turn(0)
                for g in range(CHUNKS):
                    pe.wait_ge(x_copied, b * CHUNKS + g + 1)
                    if g >= 2:
                        pe.wait_ge(fg_copied, b * CHUNKS + g - 1)
                    for n in range(2):
                        mm = pe.matmul(score_ps[g % 2][:, n * CHUNK:(n + 1) * CHUNK], fg_w[:, n, :], x_ch[:, g * CHUNK:(g + 1) * CHUNK],
                                       start=True, stop=True)
                    mm.then_inc(fg_made, 1)
                    if g + 1 < CHUNKS:
                        turn(g + 1)
                    if g > 0:
                        pe.wait_ge(h_copied, b * CHUNKS + g)
                    for k in range(4):
                        t = 4 * g + k
                        mm = pe.matmul(work_ps[1][:, k * P:(k + 1) * P], x_ch[:, t * P:(t + 1) * P], h_w[:, :], start=True, stop=True)
                    mm.then_inc(h_made, 1)
                pe.wait_ge(stacked, b * CHUNKS + CHUNKS)
                for t in range(LEAD * GROUP):
                    for _ in scores(b, t):
                        pass
                for pair in range(PAIRS):
                    ahead = range(GROUP * (pair + LEAD), min(GROUP * (pair + LEAD + 1), TILES))
                    steps = (step for t in ahead for step in scores(b, t))
                    for _ in values(b, pair):
                        next(steps, None)
                    for _ in steps:
                        pass
                for g in range(CHUNKS):
                    if g == 0:
                        pe.wait_ge(value_added, b * (PAIRS * CHUNKS) + PAIRS * CHUNKS + 4)
                    pe.wait_ge(out_step, b * CHUNKS + g + 1)
                    for k in range(4):
                        t = 4 * g + k
                        mm = pe.transpose(work_ps[g % 2][:, k * P:(k + 1) * P], value[:, t * P:(t + 1) * P], ident[:, :])
                    mm.then_inc(out_turned, 1)

        @block.scalar
        def _(act):
            act.sem_inc(x_stored, 16)
            with act.Fori(0, B) as b:
                def copy_x(g):
                    act.wait_ge(x_turned, b * CHUNKS + g + 1)
                    act.activation(x_ch[:, g * CHUNK:(g + 1) * CHUNK], work_ps[0][:, :], ACT.Copy).then_inc(x_copied, 1)

                def second_part(g):
                    act.wait_ge(rest_ready[0], b * (2 * CHUNKS) + 2 * g + 2)
                    act.activation(part[:, g % 2, :, :], fg[:, g % 2, :, :], ACT.Copy).then_inc(part_ready[1], 1)

                for g in range(CHUNKS):
                    act.wait_ge(out_ready, b * CHUNKS + g + 1)
                    act.dma_start(x_tok[:, 4 * g:4 * g + 4, :], x_v[bass.ds(b, 1), :, 4 * g:4 * g + 4].rearrange("b p t c -> p (b t) c")).then_inc(x_in[g // 4], 16)
                copy_x(0)
                for g in range(CHUNKS):
                    if g + 1 < CHUNKS:
                        copy_x(g + 1)
                    act.wait_ge(fg_made, b * CHUNKS + g + 1)
                    if g >= 2:
                        act.wait_ge(stacked, b * CHUNKS + g - 1)
                    act.activation(fg[:, g % 2, :, :].rearrange("p n c -> p (n c)"), score_ps[g % 2][:, :], ACT.Copy).then_inc(fg_copied, 1)
                    act.wait_ge(fg_copied, b * CHUNKS + g + 1)
                    act.activation(part[:, g % 2, :, :], fg[:, g % 2, :, :], ACT.Copy).then_inc(part_ready[0], 1)
                    if g > 0:
                        second_part(g - 1)
                second_part(CHUNKS - 1)
                for t in range(TILES):
                    slot = t % RING
                    act.wait_ge(neg_ready, b * TILES + t + 1)
                    act.activation(exps[:, slot, :], exps[:, slot, :], ACT.Exp, bias=neg_max[:, slot:slot + 1],
                                   accum_out=total[:, slot:slot + 1]).then_inc(exp_ready, 1)

        @block.vector
        def _(dve):
            dve.sem_inc(out_ready, CHUNKS)
            dve.sem_inc(out_step, 2)
            dve.sem_inc(score_copied, 2)
            dve.sem_inc(value_added, 4)
            dve.wait_ge(const_in, 80)

            def take_quarter(b, t, q):
                i, slot = t * QUARTERS + q, t % RING
                dve.wait_ge(scored, b * (TILES * QUARTERS) + i + 1)
                dve.tensor_scalar(exps[:, slot, q * QUARTER:(q + 1) * QUARTER], score_ps[i % 2][:, :], 1.0, None,
                                  ALU.mult, ALU.max, accum_out=quarter_max[:, slot, q:q + 1]).then_inc(score_copied, 1)
                if q == QUARTERS - 1:
                    dve.wait_ge(score_copied, b * (TILES * QUARTERS) + i + 3)
                    dve.tensor_reduce(neg_max[:, slot:slot + 1], quarter_max[:, slot, :], AX.X, ALU.max,
                                      negate=True).then_inc(neg_ready, 1)

            def scale_h(b, t):
                slot = t % RING
                dve.wait_ge(exp_ready, b * TILES + t + 1)
                dve.reciprocal(inverse[:, slot:slot + 1], total[:, slot:slot + 1]).then_inc(inverse_ready, 1)
                dve.wait_ge(inverse_ready, b * TILES + t + 1)
                dve.tensor_scalar(h_scaled[:, slot, :], h_tok[:, t, :], inverse[:, slot:slot + 1], None,
                                  ALU.mult).then_inc(h_scaled_ready, 1)

            def add_chunk(b, pair, c):
                i = pair * CHUNKS + c
                out = value[:, c * CHUNK:(c + 1) * CHUNK]
                dve.wait_ge(value_made, b * (PAIRS * CHUNKS) + i + 1)
                if pair == 0:
                    dve.tensor_copy(out, value_ps[i % 4][:, :]).then_inc(value_added, 1)
                else:
                    dve.wait_ge(value_added, b * (PAIRS * CHUNKS) + i - CHUNKS + 5)
                    dve.tensor_tensor(out, out, value_ps[i % 4][:, :], ALU.add).then_inc(value_added, 1)

            with dve.Fori(0, B) as b:
                def subtract_part(g, k):
                    dve.wait_ge(part_ready[k], b * CHUNKS + g + 1)
                    dve.sem_inc(waited, 1)
                    for n in range(2):
                        dve.scalar_tensor_tensor(fg[:, g % 2, n, :], part[:, g % 2, n, :], mask[:, n, k:k + 1], fg[:, g % 2, n, :],
                                                 ALU.mult, ALU.add).then_inc(rest_ready[k], 1)

                def stack(g):
                    subtract_part(g, 1)
                    dve.wait_ge(rest_ready[1], b * (2 * CHUNKS) + 2 * g + 2)
                    dve.tensor_copy(f_stack[:, g * CHUNK:(g + 1) * CHUNK], fg[:, g % 2, 0, :])
                    dve.tensor_copy(g_stack[:, g * CHUNK:(g + 1) * CHUNK], fg[:, g % 2, 1, :]).then_inc(stacked, 1)

                for g in range(CHUNKS):
                    dve.wait_ge(h_made, b * CHUNKS + g + 1)
                    dve.tensor_copy(h_tok[:, 4 * g:4 * g + 4, :].rearrange("p t c -> p (t c)"), work_ps[1][:, :]).then_inc(h_copied, 1)
                    subtract_part(g, 0)
                    if g > 0:
                        stack(g - 1)
                stack(CHUNKS - 1)
                dve.wait_ge(h_copied, b * CHUNKS + CHUNKS)
                for t in range(LEAD * GROUP):
                    for q in range(QUARTERS):
                        take_quarter(b, t, q)
                for k in range(GROUP):
                    scale_h(b, k)
                for pair in range(PAIRS):
                    for c in range(CHUNKS):
                        if c in (4, 5) and pair + 1 < PAIRS:
                            scale_h(b, GROUP * (pair + 1) + c - 4)
                        t = GROUP * (pair + LEAD) + c // QUARTERS
                        if t < TILES:
                            take_quarter(b, t, c % QUARTERS)
                        add_chunk(b, pair, c)
                dve.wait_ge(x_stored, b * (16 * CHUNKS) + 16)
                for g in range(CHUNKS):
                    dve.wait_ge(out_turned, b * CHUNKS + g + 1)
                    dve.scalar_tensor_tensor(out_tok[:, 4 * g:4 * g + 4, :].rearrange("p t c -> p (t c)"),
                                             work_ps[g % 2][:, :], gamma_col[:, 0:1],
                                             x_tok[:, 4 * g:4 * g + 4, :].rearrange("p t c -> p (t c)"),
                                             ALU.mult, ALU.add).then_inc(out_step, 1)
                    dve.wait_ge(out_step, b * CHUNKS + g + 3)
                    dve.sem_inc(out_ready, 1)


def cosine_attention(nc, x, y, gamma, ident_in):
    TOK = 2048
    JT = TOK // P
    IQ = TOK // CHUNK
    PER = CHUNK // P
    H = 32
    KT = 2
    RING = 6
    LEAD = 4
    STEPS = IQ * JT
    BANKS = 4
    UNROLL = 2
    with ExitStack() as ctx:
        mem = Memory(nc, ctx, "l1")
        q_img = mem.sb("q_img", [P, UNROLL, H, C])
        hat = mem.sb("hat", [P, KT, CHUNK])
        hat_high = mem.sb("hat_high", [P, KT, TOK], F32R)
        hat_low = mem.sb("hat_low", [P, KT, TOK], F32R)
        q_tok = mem.sb("q_tok", [P, JT, KT * P])
        tok_high = mem.sb("tok_high", [P, JT, KT * P], F32R)
        tok_low = mem.sb("tok_low", [P, JT, KT * P], F32R)
        exps = mem.sb("exps", [P, RING, CHUNK])
        exps_high = mem.sb("exps_high", [P, RING, CHUNK], F32R)
        exps_low = mem.sb("exps_low", [P, RING, CHUNK], F32R)
        out_img = mem.sb("out_img", [P, H, C])
        square = mem.sb("square", [P, 2, KT * P])
        diag = mem.sb("diag", [P, JT, P])
        length = mem.sb("length", [P, JT])
        sums = mem.sb("sums", [P, JT, IQ])
        total = mem.sb("total", [P, JT])
        inverse = mem.sb("inverse", [P, JT])
        ones = mem.sb("ones", [P, P])
        ident = mem.sb("ident", [P, P])
        gamma_col = mem.sb("gamma_col", [P, 1])
        energy_ps = [mem.ps(f"energy{i}", [P, CHUNK]) for i in range(BANKS)]
        value_ps = [mem.ps(f"value{i}", [P, CHUNK]) for i in range(KT)]
        work_ps = [mem.ps(f"work{i}", [P, CHUNK]) for i in range(2)]

        const_in, ones_ready = mem.sem("const_in"), mem.sem("ones_ready")
        q_in = [mem.sem(f"q_in{u}") for u in range(UNROLL)]
        work_made = mem.sem("work_made")
        work_used = [mem.sem(f"work_used{i}") for i in range(2)]
        squared, length_ready, diag_step = mem.sem("squared"), mem.sem("length_ready"), mem.sem("diag_step")
        hat_step, tok_high_ready, tok_ready = mem.sem("hat_step"), mem.sem("tok_high_ready"), mem.sem("tok_ready")
        energy_made, exp_ready = mem.sem("energy_made"), mem.sem("exp_ready")
        exp_high_ready, exp_split = mem.sem("exp_high_ready"), mem.sem("exp_split")
        value_step, value_taken = mem.sem("value_step"), mem.sem("value_taken")
        scaled, out_ready, out_stored, out_free = mem.sem("scaled"), mem.sem("out_ready"), mem.sem("out_stored"), mem.sem("out_free")
        block = ctx.enter_context(nc.Block())

        x_v = x.rearrange("(g u) i (h r) c -> g u r i h c", r=2, u=UNROLL)
        y_v = y.rearrange("(g u) i (h r) c -> g u r i h c", r=2, u=UNROLL)
        q_cols = [q_img[:, u, :, :].rearrange("p h (w r) -> p r (h w)", r=2) for u in range(UNROLL)]
        out_cols = out_img[:, :, :].rearrange("p h (w r) -> p r (h w)", r=2)
        TURNS = JT // 2
        WORK = TURNS + 2 * IQ
        DIAG = 5

        def images(eng):
            with eng.Fori(0, B // UNROLL) as g:
                for u in range(UNROLL):
                    yield g * UNROLL + u, u, g

        @block.sync
        def _(sp):
            sp.dma_start(ident[:, :], ident_in).then_inc(const_in, 16)
            sp.dma_start(gamma_col[:, :], gamma).then_inc(const_in, 16)
            for b, u, g in images(sp):
                sp.wait_ge(out_ready, b * IQ + IQ)
                for r in range(2):
                    for a in range(0, H, 8):
                        sp.dma_start(q_img[64 * r:64 * r + 64, u, a:a + 8, :],
                                     x_v[bass.ds(g, 1), u, r, :, a:a + 8, :].rearrange("g i h c -> (g i) h c")).then_inc(q_in[u], 16)

        @block.gpsimd
        def _(pool):
            pool.sem_inc(out_ready, UNROLL * IQ)
            pool.memset(ones[:, :], 1.0).then_inc(ones_ready, 1)
            for b, u, g in images(pool):
                for k in range(IQ):
                    pool.wait_ge(out_ready, b * IQ + UNROLL * IQ + k + 1)
                    for r in range(2):
                        a = H // IQ * k
                        pool.dma_start(y_v[bass.ds(g, 1), u, r, :, a:a + 8, :].rearrange("g i h c -> (g i) h c"),
                                       out_img[64 * r:64 * r + 64, a:a + 8, :]).then_inc(out_stored, 16)
                pool.wait_ge(out_stored, b * 128 + 128)
                pool.sem_inc(out_free, 1)

        @block.tensor
        def _(pe):
            pe.wait_ge(const_in, 32)
            pe.wait_ge(ones_ready, 1)

            def energy(b, i):
                iq, jt = divmod(i, JT)
                if iq == 0 and jt % PER == 0:
                    pe.wait_ge(hat_step, b * (3 * IQ) + 3 * (jt // PER) + 3)
                pe.wait_ge(exp_ready, b * STEPS + i + 1)
                rows, cols = slice(jt * P, (jt + 1) * P), slice(iq * CHUNK, (iq + 1) * CHUNK)
                for k in range(KT):
                    mm = split_product(pe, energy_ps[i % BANKS][:, :], (hat_high[:, k, rows], hat_low[:, k, rows]),
                                       (hat_high[:, k, cols], hat_low[:, k, cols]), k == 0, k == KT - 1)
                mm.then_inc(energy_made, 1)

            def value(b, i):
                iq, jt = divmod(i, JT)
                if iq == 0 and jt % PER == 0:
                    pe.wait_ge(tok_ready, b * IQ + jt // PER + 1)
                pe.wait_ge(exp_split, b * STEPS + i + RING + 1)
                s = i % RING
                for k in range(KT):
                    if jt == 0:
                        pe.wait_ge(value_taken, b * (KT * IQ) + KT * iq + k + 1)
                    rows = slice(k * P, (k + 1) * P)
                    mm = split_product(pe, value_ps[k][:, :], (tok_high[:, jt, rows], tok_low[:, jt, rows]),
                                       (exps_high[:, s, :], exps_low[:, s, :]), jt == 0, jt == JT - 1)
                mm.then_inc(value_step, 1)

            def broadcast(b, w):
                c = w % IQ
                pe.wait_ge(work_used[w % 2], b * (WORK // 2) + w // 2 + 1)
                pe.matmul(work_ps[w % 2][:, :], ones[:, :], diag[:, PER * c:PER * c + PER, :].rearrange("p t c -> p (t c)"),
                          start=True, stop=True).then_inc(work_made, 1)

            for b, u, g in images(pe):
                pe.wait_ge(q_in[u], b * (128 // UNROLL) + (128 - u * (128 // UNROLL)))
                for w in range(TURNS):
                    pe.wait_ge(work_used[w % 2], b * (WORK // 2) + w // 2 + 1)
                    for m in range(4):
                        jt, k = 2 * w + m // 2, m % 2
                        mm = pe.transpose(work_ps[w % 2][:, m * P:(m + 1) * P], q_cols[u][:, k, jt * P:(jt + 1) * P], ident[:, :])
                    mm.then_inc(work_made, 1)
                pe.wait_ge(diag_step, b * DIAG + 2)
                for c in range(IQ):
                    broadcast(b, TURNS + c)
                for i in range(LEAD):
                    energy(b, i)
                for i in range(STEPS):
                    if i + LEAD < STEPS:
                        energy(b, i + LEAD)
                    value(b, i)
                pe.wait_ge(diag_step, b * DIAG + DIAG)
                for c in range(IQ):
                    broadcast(b, TURNS + IQ + c)

        @block.scalar
        def _(act):
            act.sem_inc(exp_ready, BANKS)
            act.sem_inc(exp_split, RING)
            for b, u, g in images(act):
                for w in range(TURNS):
                    act.wait_ge(work_made, b * WORK + w + 1)
                    if w > 0:
                        act.wait_ge(squared, b * JT + 2 * w)
                    for m in range(2):
                        jt = 2 * w + m
                        act.activation(square[:, m, :], work_ps[w % 2][:, m * KT * P:(m + 1) * KT * P], ACT.Square,
                                       accum_out=length[:, jt:jt + 1]).then_inc(squared, 1)
                    act.activation(q_tok[:, 2 * w:2 * w + 2, :].rearrange("p t c -> p (t c)"), work_ps[w % 2][:, :],
                                   ACT.Copy).then_inc(work_used[w % 2], 1)
                act.wait_ge(squared, b * JT + JT)
                act.activation(length[:, :], length[:, :], ACT.Sqrt).then_inc(length_ready, 1)
                for i in range(STEPS):
                    iq, jt = divmod(i, JT)
                    act.wait_ge(energy_made, b * STEPS + i + 1)
                    act.wait_ge(exp_split, b * STEPS + i + 1)
                    act.activation(exps[:, i % RING, :], energy_ps[i % BANKS][:, :], ACT.Exp,
                                   accum_out=sums[:, jt, iq:iq + 1]).then_inc(exp_ready, 1)

        @block.vector
        def _(dve):
            for bank in range(2):
                dve.sem_inc(work_used[bank], 1)
            dve.sem_inc(out_free, 1)
            dve.sem_inc(value_taken, 2)
            dve.sem_inc(value_step, RING)
            dve.wait_ge(const_in, 32)

            def diagonals(b, numbers, step):
                dve.reciprocal(inverse[:, :], numbers).then_inc(diag_step, 1)
                dve.wait_ge(diag_step, b * DIAG + step)
                dve.tensor_tensor(diag[:, :, :], ident[:, None, :].to_broadcast([P, JT, P]),
                                  inverse[:, :, None].to_broadcast([P, JT, P]), ALU.mult).then_inc(diag_step, 1)

            def unit_columns(b, u, c):
                w, cols = TURNS + c, slice(c * CHUNK, (c + 1) * CHUNK)
                first = b * (3 * IQ) + 3 * c
                dve.wait_ge(work_made, b * WORK + w + 1)
                dve.tensor_tensor(hat[:, :, :], q_cols[u][:, :, cols], work_ps[w % 2][:, None, :].to_broadcast([P, KT, CHUNK]),
                                  ALU.mult).then_inc(hat_step, 1)
                dve.wait_ge(hat_step, first + 1)
                dve.sem_inc(work_used[w % 2], 1)
                dve.tensor_copy(hat_high[:, :, cols], hat[:, :, :]).then_inc(hat_step, 1)
                dve.wait_ge(hat_step, first + 2)
                dve.tensor_tensor(hat_low[:, :, cols], hat[:, :, :], hat_high[:, :, cols].bitcast(F32), ALU.subtract).then_inc(hat_step, 1)

            def split_tokens(b, c):
                tiles = slice(PER * c, PER * c + PER)
                dve.tensor_copy(tok_high[:, tiles, :], q_tok[:, tiles, :]).then_inc(tok_high_ready, 1)
                dve.wait_ge(tok_high_ready, b * IQ + c + 1)
                dve.tensor_tensor(tok_low[:, tiles, :], q_tok[:, tiles, :], tok_high[:, tiles, :].bitcast(F32),
                                  ALU.subtract).then_inc(tok_ready, 1)

            def take(b, iq):
                cols = slice(iq * CHUNK, (iq + 1) * CHUNK)
                dve.wait_ge(value_step, b * STEPS + (iq + 1) * JT + RING)
                for k in range(KT):
                    dve.tensor_scalar(out_cols[:, k, cols], value_ps[k][:, :], gamma_col[:, 0:1], None, ALU.mult).then_inc(value_taken, 1)

            for b, u, g in images(dve):
                dve.wait_ge(length_ready, b + 1)
                diagonals(b, length[:, :], 1)
                unit_columns(b, u, 0)
                for bank in range(2):
                    dve.wait_ge(work_used[bank], b * (WORK // 2) + TURNS // 2 + 1)
                split_tokens(b, 0)
                for i in range(STEPS):
                    if i < JT and i % PER == 0 and i // PER + 1 < IQ:
                        unit_columns(b, u, i // PER + 1)
                        split_tokens(b, i // PER + 1)
                    s = i % RING
                    dve.wait_ge(exp_ready, b * STEPS + i + BANKS + 1)
                    dve.wait_ge(value_step, b * STEPS + i + 1)
                    dve.tensor_copy(exps_high[:, s, :], exps[:, s, :]).then_inc(exp_high_ready, 1)
                    dve.wait_ge(exp_high_ready, b * STEPS + i + 1)
                    dve.tensor_tensor(exps_low[:, s, :], exps[:, s, :], exps_high[:, s, :].bitcast(F32), ALU.subtract).then_inc(exp_split, 1)
                    if i == 2:
                        dve.wait_ge(out_free, b + 1)
                    if i > JT and i % JT == 2:
                        take(b, i // JT - 1)
                dve.tensor_reduce(total[:, :], sums[:, :, :], AX.X, ALU.add).then_inc(diag_step, 1)
                dve.wait_ge(diag_step, b * DIAG + 3)
                diagonals(b, total[:, :], 4)
                take(b, IQ - 1)
                dve.wait_ge(value_taken, b * (KT * IQ) + KT * IQ + 2)
                for c in range(IQ):
                    w = TURNS + IQ + c
                    cols = slice(c * CHUNK, (c + 1) * CHUNK)
                    dve.wait_ge(work_made, b * WORK + w + 1)
                    dve.tensor_tensor(out_cols[:, :, cols], out_cols[:, :, cols], work_ps[w % 2][:, None, :].to_broadcast([P, KT, CHUNK]),
                                      ALU.mult).then_inc(scaled, 1)
                    dve.wait_ge(scaled, b * IQ + c + 1)
                    dve.sem_inc(work_used[w % 2], 1)
                    dve.tensor_tensor(out_cols[:, :, cols], out_cols[:, :, cols], q_cols[u][:, :, cols], ALU.add).then_inc(out_ready, 1)


HEADS = 4
WIN = 7
QY, QX = 8, 16
RY, RX = QY + WIN - 1, QX + WIN - 1
BY, BX = HW // QY, HW // QX
KEYS = RY * RX
KEY_ROWS = [5, 5, 4]
MASKED = -1e30
EPS = 1e-5
SCALE = float(C // HEADS) ** -0.5


def region_start(k, side, region):
    return min(max(k * side - WIN // 2, 0), HW - region)


def neighbourhood_attention(nc, x, h_out, v_dram, w_qkv, w_proj, cols, rows, bias_in, ident_in):
    RING = 4
    with ExitStack() as ctx:
        mem = Memory(nc, ctx, "l2a")
        x_tok = mem.sb("x_tok", [P, TILES, C])
        n_tok = mem.sb("n_tok", [P, TILES, C])
        res = mem.sb("res", [P, TILES, C])
        x_ch = mem.sb("x_ch", [P, N])
        x_sum = mem.sb("x_sum", [P, HW])
        q_sum = mem.sb("q_sum", [P, HW])
        k_ch = mem.sb("k_ch", [P, N])
        bias = mem.sb("bias", [P, HEADS, 9, KEYS])
        probs = mem.sb("probs", [P, RING, HEADS, KEYS])
        turned = mem.sb("turned", [P, 2, 3, HEADS, P])
        v_tile = mem.sb("v_tile", [P, 4, 3, C])
        v_stage = mem.sb("v_stage", [P, 2, 4, C])
        q_masked = mem.sb("q_masked", [P, 2, HEADS, P])
        o_band = mem.sb("o_band", [P, QY, HW])
        qkv_w = mem.sb("qkv_w", [P, 3 * C])
        proj_w = mem.sb("proj_w", [P, C])
        col = mem.sb("col", [P, 8])
        row = mem.sb("row", [P, 2, C])
        q_bias = mem.sb("q_bias", [P, 1])
        eps = mem.sb("eps", [P, 1])
        stats = mem.sb("stats", [P, TILES, 6])
        mean_var = mem.sb("mean_var", [P, TILES, 2])
        std = mem.sb("std", [P, TILES])
        maxima = mem.sb("maxima", [P, RING, HEADS])
        neg_max = mem.sb("neg_max", [P, RING, HEADS])
        sums = mem.sb("sums", [P, RING, HEADS])
        inverse = mem.sb("inverse", [P, RING, HEADS])
        ident = mem.sb("ident", [P, P])
        score_ps = [mem.ps(f"score{i}", [P, CHUNK]) for i in range(4)]
        turn_ps = [mem.ps(f"turn{i}", [P, CHUNK]) for i in range(3)]
        out_ps = mem.ps("out", [P, CHUNK])

        const_in, h_stored = mem.sem("const_in"), mem.sem("h_stored")
        x_in = [mem.sem(f"x_in{k}") for k in range(2)]
        v_stored, v_in = [mem.sem(f"v_stored{i}") for i in range(2)], [mem.sem(f"v_in{i}") for i in range(4)]
        small_ready, res_ready, masked = mem.sem("small_ready"), mem.sem("res_ready"), mem.sem("masked")
        waited = mem.waited()
        norm_ready, inverse_std, sum_ready = mem.sem("norm_ready"), mem.sem("inverse_std"), mem.sem("sum_ready")
        stat_ready, std_ready, x_normed = mem.sem("stat_ready"), mem.sem("std_ready"), mem.sem("x_normed")
        pre_made, pre_copied, v_copied = mem.sem("pre_made"), mem.sem("pre_copied"), mem.sem("v_copied")
        q_ready = mem.sem("q_ready")
        scored, score_used = mem.sem("scored"), mem.sem("score_used")
        neg_ready, exp_ready, inverse_ready = mem.sem("neg_ready"), mem.sem("exp_ready"), mem.sem("inverse_ready")
        probs_ready = mem.sem("probs_ready")
        turn_made = [mem.sem(f"turn_made{i}") for i in range(3)]
        turn_used = [mem.sem(f"turn_used{i}") for i in range(3)]
        tile_done, band_taken, h_ready = mem.sem("tile_done"), mem.sem("band_taken"), mem.sem("h_ready")
        block = ctx.enter_context(nc.Block())

        T = BY * BX
        PER0 = T + BY
        x_v = x.rearrange("b (t p) c -> b p t c", p=P)
        h_v = h_out.rearrange("b (t p) c -> b p t c", p=P)
        v_v = v_dram.rearrange("b (t p) c -> b p t c", p=P)
        v_img = v_dram.rearrange("b (y x) c -> b y x c", x=HW)
        k_img = k_ch[:, :].rearrange("p (y x) -> p y x", x=HW)

        made0 = [t + max(0, (t - 1) // BX) + 1 for t in range(T)]
        made0_band = [min(BX * (j + 1) + 1, T) + j + 1 for j in range(BY)]
        ACT_PRE = 17

        pre_uses = [("turn", 0)]
        for g in range(1, 8):
            pre_uses += [("turn", g), ("keys", g - 1)]
        pre_uses.append(("keys", 7))
        GROUPS = [(0, 4), (4, 12), (12, TILES)]

        def place(i):
            j, k = divmod(i, BX)
            edge = lambda n, last: 0 if n == 0 else 2 if n == last else 1
            return j, k, region_start(j, QY, RY), region_start(k, QX, RX), 3 * edge(j, BY - 1) + edge(k, BX - 1)

        def store(sp, b, j):
            sp.wait_ge(h_ready, b * BY + j + 1)
            sp.dma_start(h_v[bass.ds(b, 1), :, 4 * j:4 * j + 4].rearrange("b p t c -> p (b t) c"), res[:, 4 * j:4 * j + 4, :]).then_inc(h_stored, 16)

        @block.sync
        def _(sp):
            for dst, src in ((qkv_w[:, :], w_qkv), (proj_w[:, :], w_proj), (col[:, :], cols), (row[:, :, :], rows),
                             (ident[:, :], ident_in), (bias[:, :, :, :], bias_in)):
                sp.dma_start(dst, src).then_inc(const_in, 16)
            with sp.Fori(0, B) as b:
                for g in range(8):
                    sp.wait_ge(v_copied, b * 8 + g + 1)
                    sp.dma_start(v_v[bass.ds(b, 1), :, 4 * g:4 * g + 4].rearrange("b p t c -> p (b t) c"),
                                 v_stage[:, g % 2, :, :]).then_inc(v_stored[g % 2], 16)
                for slot in range(2):
                    sp.wait_ge(v_stored[slot], b * 64 + 80)
                for i in range(T):
                    _, _, y0, x0, _ = place(i)
                    sp.wait_ge(tile_done, b * T + i + 1)
                    r0 = 0
                    for c, rows_c in enumerate(KEY_ROWS):
                        sp.dma_start(v_tile[0:rows_c * RX, i % 4, c, :],
                                     v_img[bass.ds(b, 1), y0 + r0:y0 + r0 + rows_c, x0:x0 + RX, :].rearrange("b r x c -> (b r) x c")).then_inc(v_in[i % 4], 16)
                        r0 += rows_c
                    if i % BX == BX - 1 and i >= 2 * BX:
                        store(sp, b, i // BX - 2)
                store(sp, b, BY - 2)
                store(sp, b, BY - 1)
            sp.wait_ge(h_stored, 16 * BY * B + 16)

        def weight(pool, b, i):
            s = i % RING
            pool.wait_ge(inverse_ready, b * T + i + 1)
            pool.tensor_tensor(probs[:, s, :, :], probs[:, s, :, :], inverse[:, s, :, None].to_broadcast([P, HEADS, KEYS]),
                               ALU.mult).then_inc(probs_ready, 1)

        @block.gpsimd
        def _(pool):
            pool.memset(eps[:, :], EPS).then_inc(small_ready, 1)
            pool.sem_inc(x_normed, 1)
            pool.sem_inc(res_ready, 4)
            pool.wait_ge(const_in, 96)
            pool.tensor_scalar(q_bias[:, :], col[:, 2:3], SCALE * HW, None, ALU.mult).then_inc(small_ready, 1)
            with pool.Fori(0, B) as b:
                pool.wait_ge(x_normed, b * TILES + 1)
                pool.wait_ge(res_ready, b * 4 + 4)
                pool.sem_inc(waited, 1)
                for k in range(4):
                    pool.dma_start(x_tok[:, 8 * k:8 * k + 8, :], x_v[bass.ds(b, 1), :, 8 * k:8 * k + 8].rearrange("b p t c -> p (b t) c")).then_inc(x_in[k // 2], 16)
                pool.wait_ge(h_stored, b * (16 * BY) + 16)
                for k in range(4):
                    pool.wait_ge(x_in[k // 2], b * 32 + 32)
                    pool.sem_inc(waited, 1)
                    pool.tensor_tensor(res[:, 8 * k:8 * k + 8, :], x_tok[:, 8 * k:8 * k + 8, :], row[:, 1:2, :].to_broadcast([P, 8, C]),
                                       ALU.add).then_inc(res_ready, 1)
                def mask_queries(j):
                    pool.wait_ge(scored, b * (4 * T) + 16 * j + 8)
                    pool.sem_inc(waited, 1)
                    for h in range(HEADS):
                        pool.tensor_scalar(q_masked[:, j % 2, h, :].rearrange("p (y x) -> p y x", x=QX),
                                           q_sum[:, QY * j:QY * j + QY, None].to_broadcast([P, QY, QX]), col[:, 4 + h:5 + h],
                                           None, ALU.mult).then_inc(masked, 1)

                pool.wait_ge(q_ready, b + 1)
                mask_queries(0)
                for i in range(T):
                    if i >= 1:
                        weight(pool, b, i - 1)
                    if i % BX == 2 and i // BX + 1 < BY:
                        mask_queries(i // BX + 1)
                weight(pool, b, T - 1)

        @block.tensor
        def _(pe):
            pe.wait_ge(const_in, 96)

            with pe.Fori(0, B) as b:
                pe.wait_ge(score_used, b * (4 * T) + 4)
                for w, (use, g) in enumerate(pre_uses):
                    ps = score_ps[w % 4]
                    if w >= 4:
                        pe.wait_ge(pre_copied, b * ACT_PRE + w - 3 + 1)
                    if use == "turn":
                        pe.wait_ge(x_normed, b * TILES + 4 * g + 5)
                        for m in range(4):
                            mm = pe.transpose(ps[:, m * P:(m + 1) * P], n_tok[:, 4 * g + m, :], ident[:, :])
                        mm.then_inc(pre_made, 1)
                    else:
                        pe.wait_ge(pre_copied, b * ACT_PRE + pre_uses.index(("turn", g)) + 2)
                        pe.matmul(ps[:, :], qkv_w[:, C:2 * C], x_ch[:, g * CHUNK:(g + 1) * CHUNK], start=True, stop=True).then_inc(pre_made, 1)
                pe.wait_ge(sum_ready, b + 1)
                pe.wait_ge(pre_copied, b * ACT_PRE + 16 - 3 + 1)
                pe.matmul(score_ps[0][:, 0:HW], qkv_w[:, 0:C], x_sum[:, :], start=True, stop=True).then_inc(pre_made, 1)
                for g in range(8):
                    w = ACT_PRE + g
                    pe.wait_ge(pre_copied, b * ACT_PRE + min(w - 3, ACT_PRE) + 1)
                    if g >= 4:
                        pe.wait_ge(v_copied, b * 8 + g - 3)
                    for m in range(4):
                        t = 4 * g + m
                        mm = pe.matmul(score_ps[w % 4][:, m * P:(m + 1) * P], x_ch[:, t * P:(t + 1) * P], qkv_w[:, 2 * C:3 * C],
                                       start=True, stop=True)
                    mm.then_inc(pre_made, 1)
                pe.wait_ge(v_copied, b * 8 + 8)

                def scores(i):
                    j, _, y0, x0, _ = place(i)
                    pe.wait_ge(masked, b * (4 * BY) + 4 * j + 4)
                    for h in range(HEADS):
                        pe.wait_ge(score_used, b * (4 * T) + 4 * i + h + 1)
                        pe.matmul(score_ps[h][:, 0:KEYS], q_masked[:, j % 2, h, :], k_img[:, y0:y0 + RY, x0:x0 + RX],
                                  start=True, stop=True).then_inc(scored, 1)

                def turn(i):
                    j = i // BX
                    pe.wait_ge(probs_ready, b * T + i + 1)
                    k0 = 0
                    for c, rows_c in enumerate(KEY_ROWS):
                        n = rows_c * RX
                        use = b * PER0 + made0[i] - 1 if c == 0 else b * T + i
                        pe.wait_ge(turn_used[c], use + 1)
                        for h in range(HEADS):
                            mm = pe.transpose(turn_ps[c][0:n, h * P:(h + 1) * P], probs[:, i % RING, h, k0:k0 + n], ident[:, :])
                        mm.then_inc(turn_made[c], 1)
                        k0 += n

                def values(i):
                    j, k = divmod(i, BX)
                    pe.wait_ge(v_in[i % 4], (b * (T // 4) + i // 4 + 1) * (16 * 3))
                    if k == 0:
                        pe.wait_ge(band_taken, b * BY + j + 1)
                    for c, rows_c in enumerate(KEY_ROWS):
                        n = rows_c * RX
                        use = b * PER0 + made0[i] - 1 if c == 0 else b * T + i
                        pe.wait_ge(turn_used[c], use + 2)
                        for h in range(HEADS):
                            mm = pe.matmul(out_ps[32 * h:32 * h + 32, k * P:(k + 1) * P], v_tile[0:n, i % 4, c, 32 * h:32 * h + 32],
                                           turned[0:n, i % 2, c, h, :], start=(c == 0), stop=(c == 2))
                    mm.then_inc(tile_done, 1)

                def project(j):
                    pe.wait_ge(band_taken, b * BY + j + 2)
                    pe.wait_ge(turn_used[0], b * PER0 + made0_band[j])
                    flat = o_band[:, :, :].rearrange("p y x -> p (y x)")
                    for m in range(4):
                        mm = pe.matmul(turn_ps[0][:, m * P:(m + 1) * P], flat[:, m * P:(m + 1) * P], proj_w[:, :], start=True, stop=True)
                    mm.then_inc(turn_made[0], 1)

                for i in range(T + 4):
                    if i < T:
                        scores(i)
                    if i >= 4 and (i - 4) % BX == BX - 1:
                        project((i - 4) // BX)
                    if 2 <= i <= T + 1:
                        turn(i - 2)
                    if 3 <= i <= T + 2:
                        values(i - 3)

        @block.scalar
        def _(act):
            act.sem_inc(pre_copied, 1)
            act.sem_inc(turn_used[1], 1)
            act.sem_inc(turn_used[2], 1)
            act.wait_ge(small_ready, 2)
            act.wait_ge(const_in, 96)
            with act.Fori(0, B) as b:
                def deviations(k):
                    start, end = GROUPS[k]
                    act.wait_ge(stat_ready, b * TILES + end)
                    act.activation(std[:, start:end], mean_var[:, start:end, 1], ACT.Sqrt, bias=eps[:, 0:1]).then_inc(std_ready, 1)

                deviations(0)
                deviations(1)
                for w, (use, g) in enumerate(pre_uses):
                    cols = slice(g * CHUNK, (g + 1) * CHUNK)
                    act.wait_ge(pre_made, b * 25 + w + 1)
                    if use == "turn":
                        act.activation(x_ch[:, cols], score_ps[w % 4][:, :], ACT.Identity, scale=col[:, 0:1], bias=col[:, 1:2]).then_inc(pre_copied, 1)
                    else:
                        act.activation(k_ch[:, cols], score_ps[w % 4][:, :], ACT.Identity, bias=col[:, 3:4]).then_inc(pre_copied, 1)
                    if w == 0:
                        deviations(2)
                act.wait_ge(pre_made, b * 25 + 17)
                act.activation(q_sum[:, :], score_ps[0][:, 0:HW], ACT.Identity, scale=SCALE, bias=q_bias[:, 0:1]).then_inc(pre_copied, 1)
                act.wait_ge(pre_copied, b * ACT_PRE + ACT_PRE + 1)
                act.sem_inc(q_ready, 1)
                for i in range(T + 3):
                    if i >= 3:
                        t = i - 3
                        for c in (1, 2):
                            n = KEY_ROWS[c] * RX
                            act.wait_ge(turn_made[c], b * T + t + 1)
                            act.wait_ge(tile_done, b * T + t + 3)
                            act.activation(turned[0:n, t % 2, c, :, :].rearrange("p h q -> p (h q)"), turn_ps[c][0:n, :],
                                           ACT.Copy).then_inc(turn_used[c], 1)
                    if i < T:
                        act.wait_ge(neg_ready, b * T + i + 1)
                        s = i % RING
                        for h in range(HEADS):
                            act.activation(probs[:, s, h, :], probs[:, s, h, :], ACT.Exp, bias=neg_max[:, s, h:h + 1],
                                           accum_out=sums[:, s, h:h + 1]).then_inc(exp_ready, 1)

        @block.vector
        def _(dve):
            dve.sem_inc(score_used, 4)
            dve.sem_inc(scored, 24)
            dve.sem_inc(turn_used[0], 1)
            dve.sem_inc(tile_done, 4)
            dve.sem_inc(band_taken, 1)
            dve.sem_inc(h_stored, 16)
            for slot in range(2):
                dve.sem_inc(v_stored[slot], 16)
            dve.wait_ge(const_in, 96)
            with dve.Fori(0, B) as b:
                for k, (start, end) in enumerate(GROUPS):
                    for t in range(start, end):
                        if t == start or t % 8 == 0:
                            dve.wait_ge(x_in[t // 16], b * 32 + 32)
                        dve.bn_stats(stats[:, t, :], x_tok[:, t, :]).then_inc(norm_ready, 1)
                    dve.wait_ge(norm_ready, b * TILES + end)
                    dve.sem_inc(waited, 1)
                    for t in range(start, end):
                        dve.bn_aggr(mean_var[:, t, :], stats[:, t, :]).then_inc(stat_ready, 1)
                    dve.wait_ge(std_ready, b * len(GROUPS) + k + 1)
                    dve.reciprocal(std[:, start:end], std[:, start:end]).then_inc(inverse_std, 1)
                    dve.wait_ge(inverse_std, b * len(GROUPS) + k + 1)
                    for t in range(start, end):
                        dve.tensor_scalar(n_tok[:, t, :], x_tok[:, t, :], mean_var[:, t, 0:1], std[:, t:t + 1],
                                          ALU.subtract, ALU.mult).then_inc(x_normed, 1)
                dve.wait_ge(pre_copied, b * ACT_PRE + pre_uses.index(("turn", 7)) + 2)
                dve.tensor_reduce(x_sum[:, :], x_ch[:, :].rearrange("p (y x) -> p y x", x=HW), AX.X, ALU.add).then_inc(sum_ready, 1)
                for g in range(8):
                    w = ACT_PRE + g
                    dve.wait_ge(pre_made, b * 25 + w + 1)
                    dve.wait_ge(v_stored[g % 2], b * 64 + 16 * (g // 2) + 16)
                    dve.tensor_tensor(v_stage[:, g % 2, :, :], score_ps[w % 4][:, :].rearrange("p (t c) -> p t c", c=C),
                                      row[:, 0:1, :].to_broadcast([P, 4, C]), ALU.add).then_inc(v_copied, 1)
                for i in range(T + 4):
                    if 3 <= i <= T + 2:
                        t = i - 3
                        n = KEY_ROWS[0] * RX
                        dve.wait_ge(turn_made[0], b * PER0 + made0[t])
                        dve.wait_ge(tile_done, b * T + t + 3)
                        dve.tensor_copy(turned[0:n, t % 2, 0, :, :].rearrange("p h q -> p (h q)"), turn_ps[0][0:n, :]).then_inc(turn_used[0], 1)
                    if i >= 4 and (i - 4) % BX == BX - 1:
                        j = (i - 4) // BX
                        dve.wait_ge(tile_done, b * T + BX * (j + 1) + 4)
                        for k in range(BX):
                            ins = dve.tensor_copy(o_band[:, :, k * QX:(k + 1) * QX],
                                                  out_ps[:, k * P:(k + 1) * P].rearrange("p (y x) -> p y x", x=QX))
                        ins.then_inc(band_taken, 1)
                    if i < T:
                        s = i % RING
                        cls = place(i)[4]
                        for h in range(HEADS):
                            dve.wait_ge(scored, b * (4 * T) + 4 * i + h + 25)
                            if h == 0 and i >= RING:
                                dve.wait_ge(turn_made[2], b * T + i - RING + 1)
                            dve.sem_inc(waited, 1)
                            dve.tensor_tensor_reduce(probs[:, s, h, :], score_ps[h][:, 0:KEYS], bias[:, h, cls, :], 1.0, -3e38,
                                                     ALU.add, ALU.max, maxima[:, s, h:h + 1]).then_inc(score_used, 1)
                        dve.wait_ge(score_used, b * (4 * T) + 4 * i + 8)
                        dve.tensor_scalar(neg_max[:, s, :], maxima[:, s, :], -1.0, None, ALU.mult).then_inc(neg_ready, 1)
                    if 1 <= i <= T:
                        s = (i - 1) % RING
                        dve.wait_ge(exp_ready, b * (4 * T) + 4 * (i - 1) + 4)
                        dve.reciprocal(inverse[:, s, :], sums[:, s, :]).then_inc(inverse_ready, 1)
                    if i >= 4 and (i - 4) % BX == BX - 1:
                        dve.wait_ge(res_ready, b * 4 + j // 2 + 5)
                        dve.wait_ge(turn_made[0], b * PER0 + made0_band[j])
                        r = res[:, 4 * j:4 * j + 4, :].rearrange("p t c -> p (t c)")
                        dve.tensor_tensor(r, r, turn_ps[0][:, :], ALU.add).then_inc(turn_used[0], 1)
                        dve.wait_ge(turn_used[0], b * PER0 + made0_band[j] + 1)
                        dve.sem_inc(h_ready, 1)


HID = 4 * C


def mlp(nc, h_in, y, w_fc1, w_fc2, cols, row_in, ident_in):
    F = HID // P
    with ExitStack() as ctx:
        mem = Memory(nc, ctx, "l2b")
        h_tok = mem.sb("h_tok", [P, TILES, C])
        n_tok = mem.sb("n_tok", [P, TILES, C])
        res = mem.sb("res", [P, TILES, C])
        n_ch = mem.sb("n_ch", [P, N])
        hidden = mem.sb("hidden", [P, 2, F, CHUNK])
        fc1_w = mem.sb("fc1_w", [P, HID])
        fc2_w = mem.sb("fc2_w", [P, F, C])
        col = mem.sb("col", [P, 6])
        row = mem.sb("row", [P, 1, C])
        stats = mem.sb("stats", [P, TILES, 6])
        mean_var = mem.sb("mean_var", [P, TILES, 2])
        std = mem.sb("std", [P, TILES])
        eps = mem.sb("eps", [P, 1])
        ident = mem.sb("ident", [P, P])
        turn_ps = [mem.ps(f"turn{i}", [P, CHUNK]) for i in range(2)]
        hid_ps = [mem.ps(f"hid{i}", [P, CHUNK]) for i in range(3)]
        out_ps = [mem.ps(f"out{i}", [P, CHUNK]) for i in range(2)]

        const_in, y_stored = mem.sem("const_in"), mem.sem("y_stored")
        h_loaded = [mem.sem(f"h_loaded{k}") for k in range(2)]
        res_ready = mem.sem("res_ready")
        stats_ready, aggr_ready, std_ready = mem.sem("stats_ready"), mem.sem("aggr_ready"), mem.sem("std_ready")
        eps_ready, inverse_ready, normed = mem.sem("eps_ready"), mem.sem("inverse_ready"), mem.sem("normed")
        turned, n_ready = mem.sem("turned"), mem.sem("n_ready")
        hid_made, hid_ready, out_made, out_ready = mem.sem("hid_made"), mem.sem("hid_ready"), mem.sem("out_made"), mem.sem("out_ready")
        waited = mem.waited()
        block = ctx.enter_context(nc.Block())

        GROUPS = [(0, 4), (4, 12), (12, TILES)]

        h_v = h_in.rearrange("b (t p) c -> b p t c", p=P)
        y_v = y.rearrange("b (t p) c -> b p t c", p=P)

        @block.sync
        def _(sp):
            for dst, src in ((fc1_w[:, :], w_fc1), (fc2_w[:, :, :], w_fc2.rearrange("(f p) c -> p f c", p=P)), (col[:, :], cols),
                             (row[:, :, :], row_in), (ident[:, :], ident_in)):
                sp.dma_start(dst, src).then_inc(const_in, 16)
            with sp.Fori(0, B) as b:
                for g in range(CHUNKS):
                    sp.wait_ge(out_ready, b * CHUNKS + g + 3)
                    sp.dma_start(y_v[bass.ds(b, 1), :, 4 * g:4 * g + 4].rearrange("b p t c -> p (b t) c"), res[:, 4 * g:4 * g + 4, :]).then_inc(y_stored, 16)
            sp.wait_ge(y_stored, 16 * CHUNKS * B + 16)

        @block.gpsimd
        def _(pool):
            pool.memset(eps[:, :], EPS).then_inc(eps_ready, 1)
            pool.sem_inc(y_stored, 16)
            pool.sem_inc(res_ready, 4)
            pool.wait_ge(const_in, 80)
            with pool.Fori(0, B) as b:
                pool.wait_ge(normed, b * TILES + 1)
                pool.wait_ge(res_ready, b * 4 + 4)
                pool.sem_inc(waited, 1)
                for k in range(4):
                    pool.dma_start(h_tok[:, 8 * k:8 * k + 8, :], h_v[bass.ds(b, 1), :, 8 * k:8 * k + 8].rearrange("b p t c -> p (b t) c")).then_inc(h_loaded[k // 2], 16)
                pool.wait_ge(y_stored, b * (16 * CHUNKS) + 16)
                for k in range(4):
                    pool.wait_ge(h_loaded[k // 2], b * 32 + 32)
                    pool.sem_inc(waited, 1)
                    pool.tensor_tensor(res[:, 8 * k:8 * k + 8, :], h_tok[:, 8 * k:8 * k + 8, :], row[:, :, :].to_broadcast([P, 8, C]),
                                       ALU.add).then_inc(res_ready, 1)

        @block.tensor
        def _(pe):
            pe.wait_ge(const_in, 80)
            with pe.Fori(0, B) as b:
                def turn(g):
                    pe.wait_ge(n_ready, b * CHUNKS + g + 1)
                    pe.wait_ge(normed, b * TILES + 4 * g + 5)
                    for m in range(4):
                        mm = pe.transpose(turn_ps[g % 2][:, m * P:(m + 1) * P], n_tok[:, 4 * g + m, :], ident[:, :])
                    mm.then_inc(turned, 1)

                def up(g):
                    pe.wait_ge(n_ready, b * CHUNKS + g + 3)
                    for f in range(F):
                        i = g * F + f
                        pe.wait_ge(hid_ready, b * (CHUNKS * F) + i + 1)
                        pe.matmul(hid_ps[i % 3][:, :], fc1_w[:, f * P:(f + 1) * P], n_ch[:, g * CHUNK:(g + 1) * CHUNK],
                                  start=True, stop=True).then_inc(hid_made, 1)

                def down(g):
                    pe.wait_ge(hid_ready, b * (CHUNKS * F) + (g + 1) * F + 3)
                    pe.wait_ge(out_ready, b * CHUNKS + g + 1)
                    for m in range(4):
                        for f in range(F):
                            mm = pe.matmul(out_ps[g % 2][:, m * P:(m + 1) * P], hidden[:, g % 2, f, m * P:(m + 1) * P], fc2_w[:, f, :],
                                           start=(f == 0), stop=(f == F - 1))
                    mm.then_inc(out_made, 1)

                turn(0)
                up(0)
                turn(1)
                for g in range(CHUNKS):
                    if g + 1 < CHUNKS:
                        up(g + 1)
                    if g + 2 < CHUNKS:
                        turn(g + 2)
                    down(g)

        @block.scalar
        def _(act):
            act.sem_inc(n_ready, 2)
            act.sem_inc(hid_ready, 3)
            act.wait_ge(const_in, 80)
            act.wait_ge(eps_ready, 1)
            with act.Fori(0, B) as b:
                def copy_turned(g):
                    act.wait_ge(turned, b * CHUNKS + g + 1)
                    act.activation(n_ch[:, g * CHUNK:(g + 1) * CHUNK], turn_ps[g % 2][:, :], ACT.Identity,
                                   scale=col[:, 0:1], bias=col[:, 1:2]).then_inc(n_ready, 1)

                def deviations(k):
                    start, end = GROUPS[k]
                    act.wait_ge(aggr_ready, b * TILES + end)
                    act.activation(std[:, start:end], mean_var[:, start:end, 1], ACT.Sqrt, bias=eps[:, 0:1]).then_inc(std_ready, 1)

                deviations(0)
                copy_turned(0)
                deviations(1)
                for g in range(CHUNKS):
                    for f in range(F):
                        i = g * F + f
                        act.wait_ge(hid_made, b * (CHUNKS * F) + i + 1)
                        if f == 0 and g >= 2:
                            act.wait_ge(out_made, b * CHUNKS + g - 1)
                        act.activation(hidden[:, g % 2, f, :], hid_ps[i % 3][:, :], ACT.Gelu, bias=col[:, 2 + f:3 + f]).then_inc(hid_ready, 1)
                    if g + 1 < CHUNKS:
                        copy_turned(g + 1)
                    if g == 0:
                        deviations(2)

        @block.vector
        def _(dve):
            dve.sem_inc(normed, 1)
            dve.sem_inc(out_ready, 2)
            with dve.Fori(0, B) as b:
                for k, (start, end) in enumerate(GROUPS):
                    for t in range(start, end):
                        if t == start or t % 8 == 0:
                            dve.wait_ge(h_loaded[t // 16], b * 32 + 32)
                        dve.bn_stats(stats[:, t, :], h_tok[:, t, :]).then_inc(stats_ready, 1)
                    dve.wait_ge(stats_ready, b * TILES + end)
                    dve.sem_inc(waited, 1)
                    for t in range(start, end):
                        dve.bn_aggr(mean_var[:, t, :], stats[:, t, :]).then_inc(aggr_ready, 1)
                    dve.wait_ge(std_ready, b * len(GROUPS) + k + 1)
                    dve.reciprocal(std[:, start:end], std[:, start:end]).then_inc(inverse_ready, 1)
                    dve.wait_ge(inverse_ready, b * len(GROUPS) + k + 1)
                    for t in range(start, end):
                        dve.tensor_scalar(n_tok[:, t, :], h_tok[:, t, :], mean_var[:, t, 0:1], std[:, t:t + 1],
                                          ALU.subtract, ALU.mult).then_inc(normed, 1)
                for g in range(CHUNKS):
                    dve.wait_ge(out_made, b * CHUNKS + g + 1)
                    dve.wait_ge(res_ready, b * 4 + g // 2 + 5)
                    dve.sem_inc(waited, 1)
                    r = res[:, 4 * g:4 * g + 4, :].rearrange("p t c -> p (t c)")
                    dve.tensor_tensor(r, r, out_ps[g % 2][:, :], ALU.add).then_inc(out_ready, 1)


def gated_conv_attention(nc, x, y, w_in, ident_in):
    PW = HW + 2
    ROWS = CHUNK // HW
    PER = CHUNK // P
    DV = 16
    VE = DV + 1
    SCALE4 = 0.25
    MX = CHUNKS + 1
    FLOOR = -1e10 / SCALE4
    RING = 6
    LEAD = 6
    GROUPS = [(0, 24), (24, TILES)]
    HEAD_TAPS, SLOTS = 6, 15
    TAPS = 9
    CONSTS = 13
    with ExitStack() as ctx:
        mem = Memory(nc, ctx, "l3")
        x_tok = mem.sb("x_tok", [P, 4, PER, C])
        elu_high = mem.sb("elu_high", [P, PW, PW], F32R)
        elu_low = mem.sb("elu_low", [P, PW, PW], F32R)
        conv_high = mem.sb("conv_high", [P, PW, PW], F32R)
        conv_low = mem.sb("conv_low", [P, PW, PW], F32R)
        conv_out = mem.sb("conv_out", [P, 2, CHUNK])
        c3 = mem.sb("c3", [P, N])
        qk = mem.sb("qk", [P, 2, CHUNK])
        part = mem.sb("part", [P, 2, CHUNK], BF16)
        q_stack = mem.sb("q_stack", [P, N], BF16)
        k_stack = mem.sb("k_stack", [P, N], BF16)
        v_sum = mem.sb("v_sum", [P, TILES, DV])
        v_ext = mem.sb("v_ext", [P, TILES, 2 * VE], F32R)
        exps = mem.sb("exps", [P, RING, CHUNK])
        exps_high = mem.sb("exps_high", [P, RING, CHUNK], F32R)
        exps_low = mem.sb("exps_low", [P, RING, CHUNK], F32R)
        low = exps[:, 0:3, :]
        gate = exps[:, 3:5, :]
        sum_sb = mem.sb("sum_sb", [P, 2, CHUNK])
        out_tok = mem.sb("out_tok", [P, 2, PER, C])
        maxima = mem.sb("maxima", [P, TILES, MX])
        neg_max = mem.sb("neg_max", [P, TILES])
        max_row = mem.sb("max_row", [TILES, 2, P])
        max_parts = mem.sb("max_parts", [TILES, 2, 3, P], BF16)
        inverse = mem.sb("inverse", [P, 2, PER])
        w_high = mem.sb("w_high", [P, 3 * TAPS * C], F32R)
        w_low = mem.sb("w_low", [P, 3 * TAPS * C], F32R)
        w_q = mem.sb("w_q", [P, P])
        w_k = mem.sb("w_k", [P, P])
        w_v = mem.sb("w_v", [P, P])
        w3 = mem.sb("w3", [P, C])
        w3_sum = mem.sb("w3_sum", [P, C])
        pick = mem.sb("pick", [P, P])
        sum_col = mem.sb("sum_col", [P, 1])
        col = mem.sb("col", [P, 9])
        v_bias = mem.sb("v_bias", [P, 1, DV])
        b3_row = mem.sb("b3_row", [P, 1, C])
        ident = mem.sb("ident", [P, P])
        tri = mem.sb("tri", [P, 2, P])
        ident_bf = mem.sb("ident_bf", [P, P], BF16)
        tri_bf = mem.sb("tri_bf", [P, 2, P], BF16)
        w_stage = c3[:, 0:3 * TAPS * C]
        work_ps = [mem.ps(f"work{i}", [P, CHUNK]) for i in range(3)]
        score_ps = [mem.ps(f"score{i}", [P, CHUNK]) for i in range(3)]
        sum_ps = [mem.ps(f"sum{i}", [P, CHUNK]) for i in range(2)]

        const_in, const_ready, pads_ready = mem.sem("const_in"), mem.sem("const_ready"), mem.sem("pads_ready")
        x_in = [mem.sem(f"x_in{i}") for i in range(4)]
        res_in, y_stored = [mem.sem(f"res_in{i}") for i in range(2)], [mem.sem(f"y_stored{i}") for i in range(2)]
        work_made, act_copied, dve_copied = mem.sem("work_made"), mem.sem("act_copied"), mem.sem("dve_copied")
        low_ready, low_exp, low_less = mem.sem("low_ready"), mem.sem("low_exp"), mem.sem("low_less")
        elu_high_ready, elu_ready = mem.sem("elu_high_ready"), mem.sem("elu_ready")
        conv_high_ready, conv_ready = mem.sem("conv_high_ready"), mem.sem("conv_ready")
        part_ready, rest_ready, stacked = mem.sem("part_ready"), mem.sem("rest_ready"), mem.sem("stacked")
        v_step, v_ready = mem.sem("v_step"), mem.sem("v_ready")
        first_made, first_used = mem.sem("first_made"), mem.sem("first_used")
        maxima_cleared, max_step = mem.sem("maxima_cleared"), mem.sem("max_step")
        max_stacked = [mem.sem(f"max_stacked{i}") for i in range(2)]
        score_made, exp_ready = mem.sem("score_made"), mem.sem("exp_ready")
        high_ready = {e: mem.sem(f"{e}_high_ready") for e in ("dve", "act")}
        low_halves = {e: mem.sem(f"{e}_low_ready") for e in ("dve", "pool")}
        summed, sum_copied = mem.sem("summed"), mem.sem("sum_copied")
        w3_made, w3_ready = mem.sem("w3_made"), mem.sem("w3_ready")
        res_ready, inverse_step, out_step, out_ready = mem.sem("res_ready"), mem.sem("inverse_step"), mem.sem("out_step"), mem.sem("out_ready")
        waited = mem.waited()
        block = ctx.enter_context(nc.Block())

        x_v = x.rearrange("b (t p) c -> b p t c", p=P)
        y_v = y.rearrange("b (t p) c -> b p t c", p=P)

        SECOND = [(c, m) for c in range(CHUNKS) for m in range(PER * c + PER)]
        starts = [SECOND.index((c, 0)) for c in range(1, CHUNKS)]
        TAKE_AT, MIX_AT, OUTPUT_AT = ([s + d for s in starts] for d in (5, 7, 13))
        FIRST, first_of = [], []
        for c in range(CHUNKS):
            entries = [(t, k) for t in range(PER * c, PER * c + PER) for k in range(c + 1)]
            if c >= CHUNKS - 2:
                entries.append(("maxima", c - (CHUNKS - 2)))
            first_of.append([len(FIRST) + e for e in range(len(entries))])
            FIRST += entries

        def head(c):
            return first_of[c][:len(first_of[c]) * HEAD_TAPS // SLOTS]

        def tail(c):
            return first_of[c][len(first_of[c]) * HEAD_TAPS // SLOTS:]

        def share(entries, k, n):
            return entries[len(entries) * k // n:len(entries) * (k + 1) // n]

        begun = [("x", 0), ("x", 1), ("x", 2)]
        for g in range(CHUNKS):
            begun += [("conv1", g)] + ([("x", g + 3)] if g + 3 < CHUNKS else [])
        finished = list(begun)
        for g in range(CHUNKS):
            projected = [("q", g - 1), ("k", g - 1)] if g > 0 else []
            values = [("v", g - 1)] if g > 0 else []
            begun += [("gate", g)] + projected + [("a", g)] + values
            finished += projected + [("gate", g)] + values + [("a", g)]
        rest = [("q", CHUNKS - 1), ("k", CHUNKS - 1), ("v", CHUNKS - 1)]
        for c in range(CHUNKS):
            rest += [("values", c), ("sums", c), ("skip", c)]
        begun += rest
        finished += rest
        owner = lambda use: "act" if use[0] in ("conv1", "gate", "q", "k") else "dve"
        copies = {e: [use for use in finished if owner(use) == e] for e in ("act", "dve")}

        def bank_of(use):
            return work_ps[begun.index(use) % 3]

        def made(eng, b, use):
            eng.wait_ge(work_made, b * len(finished) + finished.index(use) + 1)

        def copied(eng, b, use):
            e = owner(use)
            eng.wait_ge(act_copied if e == "act" else dve_copied, b * len(copies[e]) + copies[e].index(use) + 2)

        high_maker = ["dve", "dve", "act"]
        low_maker = ["dve", "pool", "dve"]

        def wait_half(eng, b, sems, maker, i):
            mine = [k for k in range(len(SECOND)) if maker[k % 3] == maker[i % 3]]
            eng.wait_ge(sems[maker[i % 3]], b * len(mine) + mine.index(i) + 1)

        def high_made(eng, b, i):
            wait_half(eng, b, high_ready, high_maker, i)

        def low_made(eng, b, i):
            wait_half(eng, b, low_halves, low_maker, i)

        def halves(i):
            c, m = SECOND[i]
            return [t[:, i % RING, max(0, m - PER * c) * P:CHUNK] for t in (exps, exps_high, exps_low)]

        def high_half(eng, name, b, i):
            if high_maker[i % 3] != name:
                return
            full, high, _ = halves(i)
            eng.wait_ge(exp_ready, b * len(SECOND) + i + 4)
            if i >= RING:
                eng.wait_ge(summed, b * len(SECOND) + i - RING + 1)
            copy = eng.tensor_copy(high, full) if name == "dve" else eng.activation(high, full, ACT.Copy)
            copy.then_inc(high_ready[name], 1)

        def low_half(eng, name, b, i):
            if low_maker[i % 3] != name:
                return
            full, high, low_out = halves(i)
            high_made(eng, b, i)
            eng.tensor_tensor(low_out, full, high.bitcast(F32), ALU.subtract).then_inc(low_halves[name], 1)

        @block.sync
        def _(sp):
            for dst, src in ((w_stage[:, 0:TAPS * C].rearrange("p (t c) -> p t c", c=C), w_in["w1"].rearrange("t p c -> p t c")),
                             (w_stage[:, TAPS * C:].rearrange("p (t c) -> p t c", c=2 * C), w_in["w2"].rearrange("t p c -> p t c")),
                             (w_q[:, :], w_in["w_q"]), (w_k[:, :], w_in["w_k"]), (w_v[:, :], w_in["w_v"]), (w3[:, :], w_in["w3"]),
                             (pick[:, :], w_in["pick"]), (sum_col[:, :], w_in["sum_col"]), (col[:, :], w_in["cols"]),
                             (v_bias[:, :, :], w_in["v_bias"]), (b3_row[:, :, :], w_in["b3_row"]), (ident[:, :], ident_in),
                             (tri[:, :, :], w_in["tri"])):
                sp.dma_start(dst, src).then_inc(const_in, 16)
            with sp.Fori(0, B) as b:
                def load_residual(c):
                    sp.wait_ge(y_stored[c % 2], b * 64 + 16 * (c // 2) + 16)
                    sp.sem_inc(waited, 1)
                    sp.dma_start(out_tok[:, c % 2, :, :], x_v[bass.ds(b, 1), :, PER * c:PER * c + PER].rearrange("b p t c -> p (b t) c")).then_inc(res_in[c % 2], 16)

                load_residual(0)
                load_residual(1)
                for k, (first, end) in enumerate(GROUPS):
                    sp.wait_ge(max_step, b * 12 + 6 * k + 6)
                    sp.sem_inc(waited, 1)
                    for r in range(3):
                        sp.dma_start(q_stack[32 + r:33 + r, first * P:end * P], max_parts[0:end - first, k, r, :]).then_inc(max_stacked[k], 16)
                for c in range(CHUNKS):
                    sp.wait_ge(out_ready, b * CHUNKS + c + 1)
                    sp.sem_inc(waited, 1)
                    sp.dma_start(y_v[bass.ds(b, 1), :, PER * c:PER * c + PER].rearrange("b p t c -> p (b t) c"), out_tok[:, c % 2, :, :]).then_inc(y_stored[c % 2], 16)
                    if c + 2 < CHUNKS:
                        load_residual(c + 2)
            for k in range(2):
                sp.wait_ge(y_stored[k], 64 * B + 16)

        @block.gpsimd
        def _(pool):
            for k in range(2):
                pool.sem_inc(y_stored[k], 16)
            pads = (elu_high[:, :, :], elu_low[:, :, :], conv_high[:, :, :], conv_low[:, :, :], v_ext[:, :, :], sum_sb[:, :, :])
            for t in pads:
                pool.memset(t.bitcast(F32), 0.0).then_inc(pads_ready, 1)
            pool.wait_ge(pads_ready, len(pads))
            pool.memset(v_ext[:, :, DV:VE].bitcast(F32), 1.0).then_inc(pads_ready, 1)
            with pool.Fori(0, B) as b:
                for g in range(CHUNKS):
                    pool.wait_ge(low_exp, b * CHUNKS + g + 1)
                    pool.sem_inc(waited, 1)
                    pool.tensor_scalar(low[:, g % 3, :], low[:, g % 3, :], -1.0, None, ALU.add).then_inc(low_less, 1)
                def residual(c):
                    pool.wait_ge(res_in[c % 2], b * 64 + 16 * (c // 2) + 16)
                    pool.tensor_tensor(out_tok[:, c % 2, :, :], out_tok[:, c % 2, :, :], b3_row[:, :, :].to_broadcast([P, PER, C]),
                                       ALU.add).then_inc(res_ready, 1)

                residual(0)
                residual(1)
                for i, (c, m) in enumerate(SECOND):
                    low_half(pool, "pool", b, i)
                    if c > 2 and m == 4:
                        residual(c - 1)
                residual(CHUNKS - 1)

        @block.tensor
        def _(pe):
            pe.wait_ge(const_in, 16 * CONSTS)
            pe.wait_ge(pads_ready, 7)
            pe.wait_ge(const_ready, 4)
            pe.matmul(sum_ps[0][:, 0:C], pick[:, :], w3[:, :], start=True, stop=True).then_inc(w3_made, 1)
            pe.wait_ge(w3_ready, 1)
            with pe.Fori(0, B) as b:
                def begin(use):
                    u = begun.index(use)
                    if u >= 3:
                        copied(pe, b, begun[u - 3])
                    return work_ps[u % 3]

                def turn(g):
                    ps = begin(("x", g))
                    pe.wait_ge(x_in[g % 4], b * 32 + 16 * (g // 4) + 16)
                    for m in range(PER):
                        mm = pe.transpose(ps[:, m * P:(m + 1) * P], x_tok[:, g % 4, m, :], ident[:, :])
                    mm.then_inc(work_made, 1)

                def convolve(ps, high, low, weight, g):
                    for t in range(TAPS):
                        dy, dx = divmod(t, 3)
                        w = slice(weight(t), weight(t) + C)
                        rows, cols = slice(ROWS * g + dy, ROWS * g + dy + ROWS), slice(dx, dx + HW)
                        mm = split_product(pe, ps[:, :], (w_high[:, w], w_low[:, w]), (high[:, rows, cols], low[:, rows, cols]),
                                           t == 0, t == TAPS - 1)
                        if t == TAPS - 1:
                            mm.then_inc(work_made, 1)
                        yield t

                def project(g):
                    for name, w in (("q", w_q), ("k", w_k)):
                        ps = begin((name, g))
                        copied(pe, b, ("a", g))
                        pe.matmul(ps[:, :], w[:, :], c3[:, g * CHUNK:(g + 1) * CHUNK], start=True, stop=True).then_inc(work_made, 1)

                def project_values(g):
                    ps = begin(("v", g))
                    copied(pe, b, ("a", g))
                    for m in range(PER):
                        t = PER * g + m
                        mm = pe.matmul(ps[:, m * P:(m + 1) * P], c3[:, t * P:(t + 1) * P], w_v[:, :], start=True, stop=True)
                    mm.then_inc(work_made, 1)

                def first(i):
                    t, c = FIRST[i]
                    pe.wait_ge(first_used, b * len(FIRST) + i + 1)
                    ps = score_ps[i % 3]
                    if t == "maxima":
                        start, end = GROUPS[c]
                        pe.wait_ge(max_step, b * 12 + 6 * c + 1)
                        pe.transpose(ps[0:end - start, 0:P], neg_max[:, start:end], ident[:, :]).then_inc(first_made, 1)
                        return
                    pe.wait_ge(stacked, b * CHUNKS + t // PER + 1)
                    wide = min(CHUNK, (t + 1) * P - c * CHUNK)
                    last = c == t // PER
                    mm = pe.matmul(ps[:, 0:wide], q_stack[:, t * P:(t + 1) * P], k_stack[:, c * CHUNK:c * CHUNK + wide],
                                   start=True, stop=not last)
                    if last:
                        mm = pe.matmul(ps[:, wide - P:wide], ident_bf[:, :], tri_bf[:, 0, :], start=False, stop=True)
                    mm.then_inc(first_made, 1)

                pe.wait_ge(dve_copied, b * len(copies["dve"]) + 1)
                for g in range(3):
                    turn(g)
                for g in range(CHUNKS):
                    ps = begin(("conv1", g))
                    pe.wait_ge(elu_ready, b * CHUNKS + min(g + 2, CHUNKS))
                    for t in convolve(ps, elu_high, elu_low, lambda t: t * C, g):
                        pass
                    if g + 3 < CHUNKS:
                        turn(g + 3)
                for g in range(CHUNKS):
                    ps = begin(("gate", g))
                    pe.wait_ge(conv_ready, b * CHUNKS + min(g + 2, CHUNKS) + 2)
                    for t in convolve(ps, conv_high, conv_low, lambda t: TAPS * C + 2 * C * t + C, g):
                        if t == 1 and g > 0:
                            project(g - 1)
                        if g > 1:
                            for i in share(tail(g - 2), t, TAPS):
                                first(i)
                    ps = begin(("a", g))
                    for t in convolve(ps, conv_high, conv_low, lambda t: TAPS * C + 2 * C * t, g):
                        if t == 1 and g > 0:
                            project_values(g - 1)
                        if g > 0 and t >= TAPS - HEAD_TAPS:
                            for i in share(head(g - 1), t - (TAPS - HEAD_TAPS), HEAD_TAPS):
                                first(i)
                project(CHUNKS - 1)
                project_values(CHUNKS - 1)
                for i in tail(CHUNKS - 2):
                    first(i)
                for i in first_of[CHUNKS - 1]:
                    first(i)
                pe.wait_ge(first_used, (b + 1) * len(FIRST) + 3)
                pe.wait_ge(v_ready, b * CHUNKS + CHUNKS)

                def scores(i):
                    c, m = SECOND[i]
                    if m == 0 and PER * c in (GROUPS[0][0], GROUPS[1][0]):
                        k = 0 if c == 0 else 1
                        pe.wait_ge(max_stacked[k], b * 48 + 48)
                    pe.wait_ge(exp_ready, b * len(SECOND) + i + 1)
                    ps = score_ps[i % 3]
                    skip = max(0, m - PER * c) * P
                    diagonal = m >= PER * c
                    mm = pe.matmul(ps[:, skip:CHUNK], k_stack[:, m * P:(m + 1) * P], q_stack[:, c * CHUNK + skip:(c + 1) * CHUNK],
                                   start=True, stop=not diagonal)
                    if diagonal:
                        mm = pe.matmul(ps[:, skip:skip + P], ident_bf[:, :], tri_bf[:, 1, :], start=False, stop=True)
                    mm.then_inc(score_made, 1)

                def values(i):
                    c, m = SECOND[i]
                    low_made(pe, b, i)
                    if m == 0:
                        pe.wait_ge(sum_copied, b * CHUNKS + c + 1)
                    skip = max(0, m - PER * c) * P
                    out = sum_ps[c % 2][0:2 * VE, skip:CHUNK]
                    pe.matmul(out, v_ext[:, m, :], exps_low[:, i % RING, skip:CHUNK], start=(m == 0), stop=False, skip_group_check=True)
                    pe.matmul(out, v_ext[:, m, :], exps_high[:, i % RING, skip:CHUNK], start=False, stop=(m == PER * c + 3),
                              skip_group_check=True).then_inc(summed, 1)

                def mix(c):
                    pe.wait_ge(sum_copied, b * CHUNKS + c + 3)
                    tiles = [slice(m * P, (m + 1) * P) for m in range(PER)]
                    ps = begin(("values", c))
                    for m in range(PER):
                        mm = pe.matmul(ps[:, tiles[m]], sum_sb[:, c % 2, tiles[m]], w3_sum[:, :], start=True, stop=True)
                    mm.then_inc(work_made, 1)
                    ps = begin(("sums", c))
                    for m in range(PER):
                        mm = pe.matmul(ps[:, m:m + 1], sum_sb[:, c % 2, tiles[m]], sum_col[:, :], start=True, stop=True)
                    mm.then_inc(work_made, 1)
                    ps = begin(("skip", c))
                    for m in range(PER):
                        t = PER * c + m
                        mm = pe.transpose(ps[:, tiles[m]], c3[:, t * P:(t + 1) * P], ident[:, :])
                    mm.then_inc(work_made, 1)

                for i in range(LEAD):
                    scores(i)
                for i, (c, m) in enumerate(SECOND):
                    values(i)
                    if i + LEAD < len(SECOND):
                        scores(i + LEAD)
                    if i in MIX_AT:
                        mix(MIX_AT.index(i))
                mix(CHUNKS - 1)

        @block.scalar
        def _(act):
            act.sem_inc(act_copied, 1)
            act.sem_inc(exp_ready, 3)
            act.wait_ge(const_in, 16 * CONSTS)
            act.wait_ge(pads_ready, 7)
            with act.Fori(0, B) as b:
                def load(g):
                    act.dma_start(x_tok[:, g % 4, :, :], x_v[bass.ds(b, 1), :, PER * g:PER * g + PER].rearrange("b p t c -> p (b t) c")).then_inc(x_in[g % 4], 16)

                def exp_low(g):
                    act.wait_ge(low_ready, b * CHUNKS + g + 1)
                    act.activation(low[:, g % 3, :], low[:, g % 3, :], ACT.Exp).then_inc(low_exp, 1)
                    if g + 4 < CHUNKS:
                        load(g + 4)

                def stack(g):
                    for n, name in enumerate("qk"):
                        made(act, b, (name, g))
                        act.activation(qk[:, n, :], bank_of((name, g))[:, :], ACT.Identity, bias=col[:, 3 + n:4 + n]).then_inc(act_copied, 1)
                    for step in range(2):
                        for n in range(2):
                            if step == 0:
                                copied(act, b, ("qk"[n], g))
                            else:
                                act.wait_ge(rest_ready, b * (4 * CHUNKS) + 4 * g + n + 1)
                            act.activation(part[:, n, :], qk[:, n, :], ACT.Copy).then_inc(part_ready, 1)
                    cols = slice(g * CHUNK, (g + 1) * CHUNK)
                    act.wait_ge(rest_ready, b * (4 * CHUNKS) + 4 * g + 4)
                    act.activation(q_stack[:, cols], qk[:, 0, :], ACT.Copy)
                    act.activation(k_stack[:, cols], qk[:, 1, :], ACT.Copy).then_inc(stacked, 1)

                for g in range(4):
                    load(g)
                for g in range(3):
                    exp_low(g)
                for g in range(CHUNKS):
                    made(act, b, ("conv1", g))
                    act.wait_ge(conv_ready, b * CHUNKS + g + 1)
                    act.activation(conv_out[:, g % 2, :], bank_of(("conv1", g))[:, :], ACT.Identity, bias=col[:, 0:1]).then_inc(act_copied, 1)
                    copied(act, b, ("conv1", g))
                    act.activation(conv_high[:, 1 + ROWS * g:1 + ROWS * g + ROWS, 1:1 + HW],
                                   conv_out[:, g % 2, :].rearrange("p (y x) -> p y x", x=HW), ACT.Copy).then_inc(conv_high_ready, 1)
                    if g + 3 < CHUNKS:
                        exp_low(g + 3)
                for g in range(CHUNKS):
                    if g > 0:
                        stack(g - 1)
                    made(act, b, ("gate", g))
                    if g >= 2:
                        copied(act, b, ("a", g - 2))
                    act.activation(gate[:, g % 2, :], bank_of(("gate", g))[:, :], ACT.Sigmoid, bias=col[:, 2:3]).then_inc(act_copied, 1)
                stack(CHUNKS - 1)
                for i, (c, m) in enumerate(SECOND):
                    skip = max(0, m - PER * c) * P
                    act.wait_ge(score_made, b * len(SECOND) + i + 1)
                    if i >= RING:
                        low_made(act, b, i - RING)
                    act.activation(halves(i)[0], score_ps[i % 3][:, skip:CHUNK], ACT.Exp, scale=SCALE4).then_inc(exp_ready, 1)
                    if i > 0:
                        high_half(act, "act", b, i - 1)
                high_half(act, "act", b, len(SECOND) - 1)

        @block.vector
        def _(dve):
            dve.sem_inc(dve_copied, 1)
            dve.sem_inc(conv_ready, 2)
            dve.sem_inc(first_used, 3)
            dve.sem_inc(sum_copied, 2)
            dve.wait_ge(const_in, 16 * CONSTS)
            dve.tensor_copy(ident_bf[:, :], ident[:, :]).then_inc(const_ready, 1)
            dve.tensor_copy(tri_bf[:, :, :], tri[:, :, :]).then_inc(const_ready, 1)
            dve.tensor_copy(w_high[:, :], w_stage).then_inc(const_ready, 1)
            dve.wait_ge(const_ready, 3)
            dve.tensor_tensor(w_low[:, :], w_stage, w_high[:, :].bitcast(F32), ALU.subtract).then_inc(const_ready, 1)
            dve.wait_ge(w3_made, 1)
            dve.tensor_copy(w3_sum[:, :], sum_ps[0][:, 0:C]).then_inc(w3_ready, 1)
            dve.wait_ge(pads_ready, 7)
            with dve.Fori(0, B) as b:
                def low_part(g):
                    made(dve, b, ("x", g))
                    dve.tensor_scalar(low[:, g % 3, :], bank_of(("x", g))[:, :], 0.0, None, ALU.min).then_inc(low_ready, 1)

                def elu(g):
                    rows = slice(1 + ROWS * g, 1 + ROWS * g + ROWS)
                    image = low[:, g % 3, :].rearrange("p (y x) -> p y x", x=HW)
                    dve.wait_ge(low_less, b * CHUNKS + g + 1)
                    dve.sem_inc(waited, 1)
                    dve.scalar_tensor_tensor(low[:, g % 3, :], bank_of(("x", g))[:, :], 0.0, low[:, g % 3, :],
                                             ALU.max, ALU.add).then_inc(dve_copied, 1)
                    copied(dve, b, ("x", g))
                    dve.tensor_copy(elu_high[:, rows, 1:1 + HW], image).then_inc(elu_high_ready, 1)
                    dve.wait_ge(elu_high_ready, b * CHUNKS + g + 1)
                    dve.tensor_tensor(elu_low[:, rows, 1:1 + HW], image, elu_high[:, rows, 1:1 + HW].bitcast(F32),
                                      ALU.subtract).then_inc(elu_ready, 1)

                def maximum(i):
                    t, c = FIRST[i]
                    ps = score_ps[i % 3]
                    dve.wait_ge(first_made, b * len(FIRST) + i + 1)
                    if t != "maxima":
                        wide = min(CHUNK, (t + 1) * P - c * CHUNK)
                        dve.tensor_reduce(maxima[:, t, c:c + 1], ps[:, 0:wide], AX.X, ALU.max).then_inc(first_used, 1)
                        for k, (start, end) in enumerate(GROUPS):
                            if t == end - 1 and c == t // PER:
                                dve.wait_ge(first_used, b * len(FIRST) + i + 4)
                                dve.tensor_reduce(neg_max[:, start:end], maxima[:, start:end, :], AX.X, ALU.max,
                                                  negate=True).then_inc(max_step, 1)
                        return
                    rows = slice(0, GROUPS[c][1] - GROUPS[c][0])
                    dve.tensor_copy(max_row[rows, c, :], ps[rows, 0:P]).then_inc(first_used, 1)
                    dve.wait_ge(first_used, b * len(FIRST) + i + 4)
                    for k in range(3):
                        if k > 0:
                            dve.tensor_tensor(max_row[rows, c, :], max_row[rows, c, :], max_parts[rows, c, k - 1, :],
                                              ALU.subtract).then_inc(max_step, 1)
                            dve.wait_ge(max_step, b * 12 + 6 * c + 2 * k + 1)
                        dve.tensor_copy(max_parts[rows, c, k, :], max_row[rows, c, :]).then_inc(max_step, 1)
                        dve.wait_ge(max_step, b * 12 + 6 * c + 2 * k + 2)

                def subtract_parts(g, step):
                    for n in range(2):
                        dve.wait_ge(part_ready, b * (4 * CHUNKS) + 4 * g + 2 * step + n + 1)
                        dve.sem_inc(waited, 1)
                        dve.scalar_tensor_tensor(qk[:, n, :], part[:, n, :], col[:, 5 + 2 * n + step:6 + 2 * n + step], qk[:, n, :],
                                                 ALU.mult, ALU.add).then_inc(rest_ready, 1)

                def split_values(g):
                    tiles = slice(PER * g, PER * g + PER)
                    made(dve, b, ("v", g))
                    dve.tensor_tensor(v_sum[:, tiles, :], bank_of(("v", g))[:, :].rearrange("p (t d) -> p t d", d=P)[:, :, 0:DV],
                                      v_bias[:, :, :].to_broadcast([P, PER, DV]), ALU.add).then_inc(dve_copied, 1)
                    copied(dve, b, ("v", g))
                    dve.tensor_copy(v_ext[:, tiles, 0:DV], v_sum[:, tiles, :]).then_inc(v_step, 1)
                    dve.wait_ge(v_step, b * CHUNKS + g + 1)
                    dve.tensor_tensor(v_ext[:, tiles, VE:VE + DV], v_sum[:, tiles, :], v_ext[:, tiles, 0:DV].bitcast(F32),
                                      ALU.subtract).then_inc(v_ready, 1)

                def first_tail(c, g):
                    for k in range(3):
                        if c >= 0:
                            for i in share(tail(c), k, 3):
                                maximum(i)
                        if k < 2:
                            subtract_parts(g, k)
                        if k == 1 and g == CHUNKS - 1:
                            split_values(g)

                low_part(0)
                low_part(1)
                elu(0)
                low_part(2)
                elu(1)
                dve.memset(maxima[:, :, :], FLOOR).then_inc(maxima_cleared, 1)
                dve.wait_ge(maxima_cleared, b + 1)
                for g in range(CHUNKS):
                    if g + 2 < CHUNKS:
                        elu(g + 2)
                    if g + 3 < CHUNKS:
                        low_part(g + 3)
                    rows = slice(1 + ROWS * g, 1 + ROWS * g + ROWS)
                    dve.wait_ge(conv_high_ready, b * CHUNKS + g + 1)
                    dve.tensor_tensor(conv_low[:, rows, 1:1 + HW], conv_out[:, g % 2, :].rearrange("p (y x) -> p y x", x=HW),
                                      conv_high[:, rows, 1:1 + HW].bitcast(F32), ALU.subtract).then_inc(conv_ready, 1)
                for g in range(CHUNKS):
                    if g > 0:
                        first_tail(g - 2, g - 1)
                        split_values(g - 1)
                        for i in head(g - 1):
                            maximum(i)
                    made(dve, b, ("a", g))
                    copied(dve, b, ("gate", g))
                    dve.sem_inc(waited, 1)
                    dve.scalar_tensor_tensor(c3[:, g * CHUNK:(g + 1) * CHUNK], bank_of(("a", g))[:, :], col[:, 1:2], gate[:, g % 2, :],
                                             ALU.add, ALU.mult).then_inc(dve_copied, 1)
                first_tail(CHUNKS - 2, CHUNKS - 1)
                for i in first_of[CHUNKS - 1]:
                    maximum(i)

                def take(c):
                    dve.wait_ge(summed, b * len(SECOND) + 2 * (c + 1) * (c + 2))
                    dve.tensor_copy(sum_sb[0:2 * VE, c % 2, :], sum_ps[c % 2][0:2 * VE, :]).then_inc(sum_copied, 1)

                def output(c):
                    s = c % 2
                    made(dve, b, ("sums", c))
                    dve.tensor_scalar(inverse[:, s, :], bank_of(("sums", c))[:, 0:PER], 1e-10, None, ALU.add).then_inc(inverse_step, 1)
                    dve.wait_ge(inverse_step, b * (2 * CHUNKS) + 2 * c + 1)
                    dve.reciprocal(inverse[:, s, :], inverse[:, s, :]).then_inc(inverse_step, 1)
                    dve.wait_ge(inverse_step, b * (2 * CHUNKS) + 2 * c + 2)
                    dve.wait_ge(res_ready, b * CHUNKS + c + 1)
                    dve.sem_inc(waited, 1)
                    for m in range(PER):
                        dve.scalar_tensor_tensor(out_tok[:, s, m, :], bank_of(("values", c))[:, m * P:(m + 1) * P], inverse[:, s, m:m + 1],
                                                 out_tok[:, s, m, :], ALU.mult, ALU.add).then_inc(out_step, 1)
                    dve.wait_ge(out_step, b * (PER * CHUNKS) + PER * c + PER)
                    dve.sem_inc(dve_copied, 2)
                    made(dve, b, ("skip", c))
                    out = out_tok[:, s, :, :].rearrange("p t c -> p (t c)")
                    dve.tensor_tensor(out, out, bank_of(("skip", c))[:, :], ALU.add).then_inc(dve_copied, 1)
                    copied(dve, b, ("skip", c))
                    dve.sem_inc(out_ready, 1)

                for i, (c, m) in enumerate(SECOND):
                    high_half(dve, "dve", b, i)
                    if i > 0:
                        low_half(dve, "dve", b, i - 1)
                    if i in TAKE_AT:
                        take(TAKE_AT.index(i))
                    if i in OUTPUT_AT:
                        output(OUTPUT_AT.index(i))
                low_half(dve, "dve", b, len(SECOND) - 1)
                take(CHUNKS - 1)
                output(CHUNKS - 1)


def program(nc, a, out):
    def scratch(name, shape):
        return nc.dram_tensor(name, shape, F32, kind="Internal").ap()

    y0, y1, h2, y2, v = (scratch(n, (B, N, C)) for n in ("l0_y", "l1_y", "l2_h", "l2_y", "l2_v"))
    flat = out.rearrange("b y x c -> b (y x) c")
    column_softmax_attention(nc, a["x"].rearrange("b y x c -> b (y x) c"), y0, a["l0_w_fg"], a["l0_w_h"], a["l0_masks"], a["l0_gamma"], a["ident"])
    cosine_attention(nc, y0.rearrange("b (i j) c -> b i j c", j=HW), y1.rearrange("b (i j) c -> b i j c", j=HW), a["l1_gamma"], a["ident"])
    neighbourhood_attention(nc, y1, h2, v, a["l2a_w_qkv"], a["l2a_w_proj"], a["l2a_cols"], a["l2a_rows"], a["l2a_bias"], a["ident"])
    mlp(nc, h2, y2, a["l2b_w_fc1"], a["l2b_w_fc2"], a["l2b_cols"], a["l2b_row"], a["ident"])
    gated_conv_attention(nc, y2, flat, {n[3:]: a[n] for n in a if n.startswith("l3_")}, a["ident"])



def bias_layout(rpb):
    def axis(side, region):
        out = []
        last = HW // side - 1
        for k in (0, 1, last):
            q = k * side + np.arange(side)[:, None]
            key = region_start(k, side, region) + np.arange(region)[None, :]
            start = np.clip(q - WIN // 2, 0, HW - WIN)
            inside = (key >= start) & (key < start + WIN)
            out.append((np.where(inside, key - q + WIN - 1, 0), inside))
        return out
    ys, xs = axis(QY, RY), axis(QX, RX)
    out = np.full((QY * QX, 4, 9, RY * RX), MASKED, np.float32)
    for a, (ry, iny) in enumerate(ys):
        for c, (rx, inx) in enumerate(xs):
            inside = (iny[:, None, :, None] & inx[None, :, None, :]).reshape(QY * QX, RY * RX)
            iy = np.broadcast_to(ry[:, None, :, None], (QY, QX, RY, RX)).reshape(QY * QX, RY * RX)
            ix = np.broadcast_to(rx[None, :, None, :], (QY, QX, RY, RX)).reshape(QY * QX, RY * RX)
            for h in range(4):
                view = out[:, h, 3 * a + c, :]
                view[inside] = rpb[h][iy[inside], ix[inside]]
    return out

def l2a(I):
    k = lambda n: I['L2_conv_' + n]
    heads = np.zeros((128, 4), np.float32)
    for h in range(4): heads[32 * h:32 * h + 32, h] = 1
    cols = np.concatenate([k('ln1_g')[:, None], k('ln1_b')[:, None], k('qkv_b')[0:128, None], k('qkv_b')[128:256, None], heads], 1)
    rows = np.tile(np.stack([k('qkv_b')[256:384], k('proj_b')])[None], (128, 1, 1))
    return dict(w_qkv=k('qkv_w'), w_proj=k('proj_w'), cols=cols.astype(np.float32), rows=rows, bias=bias_layout(k('rpb')))

def l2b(I):
    k = lambda n: I['L2_conv_' + n]
    cols = np.concatenate([k('ln2_g')[:, None], k('ln2_b')[:, None], k('fc1_b').reshape(4, 128).T], 1)
    return dict(w_fc1=k('fc1_w'), w_fc2=k('fc2_w'), cols=np.ascontiguousarray(cols), row=np.tile(k('fc2_b')[None, None], (128, 1, 1)))

def part_masks(parts, width):
    of_row = np.zeros(128, int)
    of_row[:len(parts) * width] = np.repeat(parts, width)
    return [-(of_row >= 1).astype(np.float32), -(of_row >= 2).astype(np.float32)]


def l0_arrays(f, g):
    w_fg = np.stack([np.tile(f, (1, 8)), np.tile(g, (1, 8))], 1)
    masks = np.stack([np.stack(part_masks(parts, 16), 1) for parts in (LEFT_PARTS, RIGHT_PARTS)], 1)
    return dict(w_fg=w_fg, masks=masks)


def l3(I):
    k = lambda n: I['L3_conv_' + n]
    C = 128
    rows = np.arange(C)
    groups = len(LEFT_PARTS)

    def spread(v):
        return np.concatenate([np.tile(v, (1, groups)), np.zeros((v.shape[0], C - groups * v.shape[1]), np.float32)], 1)

    q_bias, k_bias = spread(k('bq')[None])[0], spread(k('bk')[None])[0]
    k_bias[32:35] = 1
    pick = np.zeros((C, C), np.float32)
    for d in range(16):
        pick[d::16, d] = 1
        pick[d::16, 17 + d] = 1
    sum_col = np.zeros((C, 1), np.float32)
    sum_col[16] = 1
    tri = np.zeros((C, 2, C), np.float32)
    tri[:, 0][rows[None, :] >= rows[:, None]] = -1e30
    tri[:, 1][rows[:, None] >= rows[None, :]] = -1e30
    cols = np.stack([k('b1'), k('b2')[0:C], k('b2')[C:2 * C], q_bias, k_bias] + part_masks(LEFT_PARTS, C // 32) + part_masks(RIGHT_PARTS, C // 32), 1)
    return dict(w1=k('W1').reshape(9, C, C), w2=k('W2').reshape(9, C, 2 * C), w_q=spread(k('Wq')), w_k=spread(k('Wk')), w_v=np.concatenate([k('Wv'), np.zeros((C, C - 16), np.float32)], 1), w3=k('W3'),
                pick=pick, sum_col=sum_col, cols=np.ascontiguousarray(cols), v_bias=np.tile(k('bv')[None, None], (C, 1, 1)),
                b3_row=np.tile(k('b3')[None, None], (C, 1, 1)), tri=tri)


def l0(I):
    k = lambda n: I["L0_conv_kernel_" + n][0, 0]
    return dict(**l0_arrays(k("f"), k("g")), w_h=k("h"), gamma=np.tile(I["L0_conv_gamma"], (P, 1)))


def arrays_of(I):
    a = {"x": I["x"], "ident": np.eye(P, dtype=np.float32), "l1_gamma": np.tile(I["L1_conv_gamma"], (P, 1))}
    for stage, made in (("l0", l0(I)), ("l2a", l2a(I)), ("l2b", l2b(I)), ("l3", l3(I))):
        a.update({f"{stage}_{n}": v for n, v in made.items()})
    return {n: np.ascontiguousarray(v) for n, v in a.items()}


def kernel(**inputs):
    import concourse.bacc as _bacc
    from concourse.bass_utils import run_bass_kernel_spmd as _run

    nc = _bacc.Bacc("TRN2", target_bir_lowering=False, num_devices=1)
    arrays = arrays_of({n: np.asarray(v) for n, v in inputs.items()})
    aps = {n: nc.dram_tensor(f"in_{n}", v.shape, mybir.dt.from_np(v.dtype), kind="ExternalInput").ap() for n, v in arrays.items()}
    out = nc.dram_tensor("out_0", (B, HW, HW, C), F32, kind="ExternalOutput").ap()
    program(nc, aps, out)
    r = _run(nc, [{f"in_{n}": v for n, v in arrays.items()}], core_ids=[0])
    return r.results[0]["out_0"]
```
